# Optimizing a Trainium2 kernel written in Bass

```python
import numpy as np
import jax
import jax.numpy as jnp

def _softmax(x, axis=-1):
    return jax.nn.softmax(x, axis=axis)

def _gelu(x):
    return jax.nn.gelu(x, approximate=True)

def _silu(x):
    return jax.nn.silu(x)

def _sigmoid(x):
    return jax.nn.sigmoid(x)

def _layernorm(x, axis=-1, eps=1e-05):
    m = jnp.mean(x, axis=axis, keepdims=True)
    v = jnp.var(x, axis=axis, keepdims=True)
    return (x - m) / jnp.sqrt(v + eps)

def _scatter_add(tgt, idx, src, axis=0):
    return tgt.at[idx].add(src)

def _segment_sum(src, seg, n):
    return jax.ops.segment_sum(src, seg, n)
kernel_name = 'mk_decoder_preln_d4_seqx_r4_f682ff'

def setup_inputs(seed: int=0):
    np.random.seed(seed)
    _w = jnp.asarray

    def _rec_inputs():
        import jax
        import jax.numpy as jnp
        _rk = jax.random.key(seed)
        x = 0.002226 + 0.9996 * jax.random.normal(jax.random.fold_in(_rk, 1), (8, 256, 256), jnp.float32)
        _lenS = 256 - jax.random.randint(jax.random.fold_in(_rk, 7), (8,), 0, max(1, 256 // 4) + 1, jnp.int32)
        _lenS2 = 77 - jax.random.randint(jax.random.fold_in(_rk, 8), (8,), 0, max(1, 77 // 4) + 1, jnp.int32)
        _ctx_1024P = jax.random.normal(jax.random.fold_in(_rk, 11), (8, 16, 256), jnp.float32)
        _ctx_1024c = jax.random.dirichlet(jax.random.fold_in(_rk, 511), 0.3 * jnp.ones((16,), jnp.float32), (8, 77))
        _ctx_1024t = jnp.einsum('bsk,bkd->bsd', _ctx_1024c, _ctx_1024P)
        _ctx_1024t = _ctx_1024t * jax.lax.rsqrt(jnp.mean(jnp.square(_ctx_1024t)) + 1e-12) * 0.953939
        ctx_1024 = -0.000125008 + 0.999885 * (_ctx_1024t + 0.3 * jax.random.normal(jax.random.fold_in(_rk, 611), (8, 77, 256), jnp.float32))
        fside_Bx16xSxS2_0 = 9.80324e-06 + 0.100009 * jax.random.normal(jax.random.fold_in(_rk, 12), (8, 16, 256, 77), jnp.float32)
        fside_SxS2_0 = -2.64403e-05 + 0.100002 * jax.random.normal(jax.random.fold_in(_rk, 14), (256, 77), jnp.float32)
        _validS = jnp.arange(256)[None, :] < _lenS[:, None]
        _validS2 = jnp.arange(77)[None, :] < _lenS2[:, None]
        _causal = jnp.tril(jnp.ones((256, 256), dtype=bool))
        mask_BxS2_bf0 = jnp.logical_not(jnp.ones((8, 77), dtype=bool))
        mask_BxS2_bk0 = jnp.logical_not(jnp.broadcast_to(_validS2[:, :], (8, 77)))
        return (x, ctx_1024, fside_Bx16xSxS2_0, fside_SxS2_0, mask_BxS2_bf0, mask_BxS2_bk0)
    x, ctx_1024, fside_Bx16xSxS2_0, fside_SxS2_0, mask_BxS2_bf0, mask_BxS2_bk0 = _rec_inputs()

    def _L0_attn_setup():
        import jax, jax.numpy as jnp
        import numpy as np
        D_MODEL = 256
        D_INNER = 512
        D_CONV = 4
        D_STATE = 16
        DT_RANK = 64
        BATCH = 2
        SEQ = 256

        def _depthwise_causal_conv(u, w, b):
            out = jax.lax.conv_general_dilated(u, w, window_strides=(1,), padding=[(D_CONV - 1, 0)], dimension_numbers=('NCH', 'OIH', 'NCH'), feature_group_count=D_INNER)
            return out + b[None, :, None]

        def _s6(u, A_log, D, Wx, Wdt, bdt):
            A = -jnp.exp(A_log)
            dbc = jnp.einsum('bld,ed->ble', u, Wx)
            dt = dbc[..., :DT_RANK]
            Bm = dbc[..., DT_RANK:DT_RANK + D_STATE]
            Cm = dbc[..., DT_RANK + D_STATE:]
            delta = jax.nn.softplus(jnp.einsum('blr,dr->bld', dt, Wdt) + bdt)
            dA = jnp.exp(delta[..., None] * A)
            dBu = delta[..., None] * Bm[:, :, None, :] * u[..., None]

            def step(h, inp):
                dA_t, dBu_t, C_t = inp
                h = dA_t * h + dBu_t
                y = jnp.einsum('bdn,bn->bd', h, C_t)
                return (h, y)
            h0 = jnp.zeros((u.shape[0], u.shape[2], D_STATE), u.dtype)
            _, ys = jax.lax.scan(step, h0, (dA.transpose(1, 0, 2, 3), dBu.transpose(1, 0, 2, 3), Cm.transpose(1, 0, 2)))
            return ys.transpose(1, 0, 2) + u * D
        key = jax.random.key(seed)
        ks = jax.random.split(key, 16)
        s = 0.02
        inp = {'x': jax.random.normal(ks[0], (BATCH, SEQ, D_MODEL), jnp.float32), 'W_in': jax.random.normal(ks[1], (2 * D_INNER, D_MODEL), jnp.float32) * s, 'W_conv': jax.random.normal(ks[2], (D_INNER, 1, D_CONV), jnp.float32) * 0.2, 'b_conv': jnp.zeros((D_INNER,), jnp.float32), 'W_out': jax.random.normal(ks[3], (D_MODEL, D_INNER), jnp.float32) * s, 'fA_log': jnp.broadcast_to(jnp.log(jnp.arange(1, D_STATE + 1, dtype=jnp.float32)), (D_INNER, D_STATE)) + 0.0, 'fD': jnp.ones((D_INNER,), jnp.float32), 'fWx': jax.random.normal(ks[4], (DT_RANK + 2 * D_STATE, D_INNER), jnp.float32) * s, 'fWdt': jax.random.normal(ks[5], (D_INNER, DT_RANK), jnp.float32) * s, 'fbdt': jax.random.normal(ks[6], (D_INNER,), jnp.float32) * 0.1, 'bA_log': jnp.broadcast_to(jnp.log(jnp.arange(1, D_STATE + 1, dtype=jnp.float32)), (D_INNER, D_STATE)) + 0.0, 'bD': jnp.ones((D_INNER,), jnp.float32), 'bWx': jax.random.normal(ks[7], (DT_RANK + 2 * D_STATE, D_INNER), jnp.float32) * s, 'bWdt': jax.random.normal(ks[8], (D_INNER, DT_RANK), jnp.float32) * s, 'bbdt': jax.random.normal(ks[9], (D_INNER,), jnp.float32) * 0.1}
        return inp
    _L0_attn_all = _L0_attn_setup()
    _L0_attn_in = {k: v for k, v in _L0_attn_all.items() if k in ('W_in', 'W_conv', 'b_conv', 'W_out', 'fA_log', 'fD', 'fWx', 'fWdt', 'fbdt', 'bA_log', 'bD', 'bWx', 'bWdt', 'bbdt')}
    del _L0_attn_all

    def _L0_xattn_setup():
        import jax, jax.numpy as jnp
        import numpy as np
        EPS = 1e-05

        def layer_norm(x, g, b):
            mu = jnp.mean(x, axis=-1, keepdims=True)
            var = jnp.var(x, axis=-1, keepdims=True)
            return (x - mu) * jax.lax.rsqrt(var + EPS) * g + b
        key = jax.random.key(seed)
        ks = jax.random.split(key, 8)
        dim, heads, dim_head = (256, 16, 64)
        inner = heads * dim_head
        b, n, m = (8, 1024, 64)
        s = dim ** (-0.5)
        return {'x': jax.random.normal(ks[0], (b, n, dim), jnp.float32), 'latents': jax.random.normal(ks[1], (b, m, dim), jnp.float32), 'ln_m_g': jnp.ones((dim,), jnp.float32), 'ln_m_b': jnp.zeros((dim,), jnp.float32), 'ln_l_g': jnp.ones((dim,), jnp.float32), 'ln_l_b': jnp.zeros((dim,), jnp.float32), 'Wq': jax.random.normal(ks[2], (dim, inner), jnp.float32) * s, 'Wkv': jax.random.normal(ks[3], (dim, 2 * inner), jnp.float32) * s, 'Wout': jax.random.normal(ks[4], (inner, dim), jnp.float32) * s}
    _L0_xattn_all = _L0_xattn_setup()
    _L0_xattn_in = {k: v for k, v in _L0_xattn_all.items() if k in ('ln_m_g', 'ln_m_b', 'ln_l_g', 'ln_l_b', 'Wq', 'Wkv', 'Wout')}
    del _L0_xattn_all

    def _L0_ffn_setup():
        import jax, jax.numpy as jnp
        import numpy as np
        D = 256
        H = 512
        E = 8
        TOP_K = 2
        N_SHARED = 1
        B, S = (2, 256)
        key = jax.random.key(seed)
        ks = jax.random.split(key, 12)
        sc = 0.02
        return {'hidden': jax.random.normal(ks[0], (B, S, D), jnp.float32), 'router_w': jax.random.normal(ks[1], (D, E), jnp.float32) * sc, 'router_b': jnp.zeros((E,), jnp.float32), 'sw1': jax.random.normal(ks[2], (D, H), jnp.float32) * sc, 'sb1': jnp.zeros((H,), jnp.float32), 'sw2': jax.random.normal(ks[3], (H, D), jnp.float32) * sc, 'sb2': jnp.zeros((D,), jnp.float32), 'rw1': jax.random.normal(ks[4], (E, D, H), jnp.float32) * sc, 'rb1': jnp.zeros((E, H), jnp.float32), 'rw2': jax.random.normal(ks[5], (E, H, D), jnp.float32) * sc, 'rb2': jnp.zeros((E, D), jnp.float32)}
    _L0_ffn_all = _L0_ffn_setup()
    _L0_ffn_in = {k: v for k, v in _L0_ffn_all.items() if k in ('router_w', 'router_b', 'sw1', 'sb1', 'sw2', 'sb2', 'rw1', 'rb1', 'rw2', 'rb2')}
    del _L0_ffn_all

    def _L1_attn_setup():
        import jax, jax.numpy as jnp
        import numpy as np
        EMBED_DIM = 256
        HEADS = 16
        HEAD_DIM = EMBED_DIM // HEADS
        ROPE_THETA = 10000.0

        def apply_rope(x):
            D = x.shape[-1]
            T = x.shape[-2]
            half = D // 2
            inv_freq = 1.0 / ROPE_THETA ** (jnp.arange(half, dtype=jnp.float32) / half)
            ang = jnp.arange(T, dtype=jnp.float32)[:, None] * inv_freq[None, :]
            cos, sin = (jnp.cos(ang), jnp.sin(ang))
            x1, x2 = (x[..., :half], x[..., half:])
            return jnp.concatenate([x1 * cos - x2 * sin, x1 * sin + x2 * cos], axis=-1)
        key = jax.random.key(seed)
        ks = jax.random.split(key, 6)
        B, T, E, H = (2, 512, EMBED_DIM, HEADS)
        s = 0.02
        return {'x': jax.random.normal(ks[0], (B, T, E), dtype=jnp.float32), 'w_qkv': jax.random.normal(ks[1], (E, 3 * E), dtype=jnp.float32) * s, 'w_pre': jax.random.normal(ks[2], (H, H), dtype=jnp.float32) * s, 'w_post': jax.random.normal(ks[3], (H, H), dtype=jnp.float32) * s, 'w_out': jax.random.normal(ks[4], (E, E), dtype=jnp.float32) * s, 'b_out': jax.random.normal(ks[5], (E,), dtype=jnp.float32) * s}
    _L1_attn_all = _L1_attn_setup()
    _L1_attn_in = {k: v for k, v in _L1_attn_all.items() if k in ('w_qkv', 'w_pre', 'w_post', 'w_out', 'b_out')}
    del _L1_attn_all

    def _L1_xattn_setup():
        import jax, jax.numpy as jnp
        import numpy as np
        E = 256
        H = 16
        D = E // H
        key = jax.random.key(seed)
        ks = jax.random.split(key, 12)
        B, T, S = (2, 512, 512)
        inp = {'query': jax.random.normal(ks[0], (B, T, E), jnp.float32), 'key': jax.random.normal(ks[1], (B, S, E), jnp.float32), 'value': jax.random.normal(ks[2], (B, S, E), jnp.float32), 'spatial_bias': jax.random.normal(ks[3], (B, H, T, S), jnp.float32) * 0.1, 'directional_bias': jax.random.normal(ks[4], (B, H, T, S), jnp.float32) * 0.1, 'key_padding_mask': jnp.zeros((B, S), dtype=bool), 'attn_mask': jax.random.normal(ks[5], (T, S), jnp.float32) * 0.1, 'Wq': jax.random.normal(ks[6], (E, E), jnp.float32) / np.sqrt(E), 'bq': jnp.zeros((E,), jnp.float32), 'Wk': jax.random.normal(ks[7], (E, E), jnp.float32) / np.sqrt(E), 'bk': jnp.zeros((E,), jnp.float32), 'Wv': jax.random.normal(ks[8], (E, E), jnp.float32) / np.sqrt(E), 'bv': jnp.zeros((E,), jnp.float32), 'Wo': jax.random.normal(ks[9], (E, E), jnp.float32) / np.sqrt(E), 'bo': jnp.zeros((E,), jnp.float32)}
        return inp
    _L1_xattn_all = _L1_xattn_setup()
    _L1_xattn_in = {k: v for k, v in _L1_xattn_all.items() if k in ('Wq', 'bq', 'Wk', 'bk', 'Wv', 'bv', 'Wo', 'bo')}
    del _L1_xattn_all

    def _L1_ffn_setup():
        import jax, jax.numpy as jnp
        import numpy as np
        N_HEADS = 16
        NUM_EXPERTS = 4
        TOP_K = 2
        D_MODEL = 256
        GATE_HID = 128
        key = jax.random.key(seed)
        ks = jax.random.split(key, 12)
        B, T, C, E = (2, 256, D_MODEL, NUM_EXPERTS)
        s = 1.0 / np.sqrt(C)
        return {'hidden_states': jax.random.normal(ks[0], (B, T, C), jnp.float32), 'Wq': jax.random.normal(ks[1], (E, C, C), jnp.float32) * s, 'bq': jnp.zeros((E, C), jnp.float32), 'Wk': jax.random.normal(ks[2], (E, C, C), jnp.float32) * s, 'bk': jnp.zeros((E, C), jnp.float32), 'Wv': jax.random.normal(ks[3], (E, C, C), jnp.float32) * s, 'bv': jnp.zeros((E, C), jnp.float32), 'Wg1': jax.random.normal(ks[4], (C, GATE_HID), jnp.float32) * s, 'bg1': jnp.zeros((GATE_HID,), jnp.float32), 'Wg2': jax.random.normal(ks[5], (GATE_HID, E), jnp.float32) / np.sqrt(GATE_HID), 'bg2': jnp.zeros((E,), jnp.float32), 'Wo': jax.random.normal(ks[6], (C, C), jnp.float32) * s, 'bo': jnp.zeros((C,), jnp.float32)}
    _L1_ffn_all = _L1_ffn_setup()
    _L1_ffn_in = {k: v for k, v in _L1_ffn_all.items() if k in ('Wq', 'bq', 'Wk', 'bk', 'Wv', 'bv', 'Wg1', 'bg1', 'Wg2', 'bg2', 'Wo', 'bo')}
    del _L1_ffn_all

    def _L2_attn_setup():
        import jax, jax.numpy as jnp
        import numpy as np
        DIM = 256
        HEADS = 16
        HEAD_DIM = DIM // HEADS
        WINDOW = 64
        THETA = 10000.0

        def _rope_tables(n, hd, dtype):
            inv_freq = 1.0 / THETA ** (jnp.arange(0, hd, 2, dtype=jnp.float32) / hd)
            ang = jnp.arange(n, dtype=jnp.float32)[:, None] * inv_freq[None, :]
            cos = jnp.concatenate([jnp.cos(ang), jnp.cos(ang)], axis=-1).astype(dtype)
            sin = jnp.concatenate([jnp.sin(ang), jnp.sin(ang)], axis=-1).astype(dtype)
            return (cos, sin)

        def _rotate_half(x):
            h = x.shape[-1] // 2
            return jnp.concatenate([-x[..., h:], x[..., :h]], axis=-1)

        def _alibi_slopes(h):
            return 2.0 ** (-jnp.arange(1, h + 1, dtype=jnp.float32) * (8.0 / h))
        key = jax.random.key(seed)
        k0, k1, k2, k3, k4 = jax.random.split(key, 5)
        s = 1.0 / np.sqrt(DIM)
        x = jax.random.normal(k0, (2, 512, DIM), dtype=jnp.float32)
        Wq = jax.random.normal(k1, (DIM, DIM), dtype=jnp.float32) * s
        Wk = jax.random.normal(k2, (DIM, DIM), dtype=jnp.float32) * s
        Wv = jax.random.normal(k3, (DIM, DIM), dtype=jnp.float32) * s
        Wo = jax.random.normal(k4, (DIM, DIM), dtype=jnp.float32) * s
        return {'x': x, 'Wq': Wq, 'Wk': Wk, 'Wv': Wv, 'Wo': Wo}
    _L2_attn_all = _L2_attn_setup()
    _L2_attn_in = {k: v for k, v in _L2_attn_all.items() if k in ('Wq', 'Wk', 'Wv', 'Wo')}
    del _L2_attn_all

    def _L2_xattn_setup():
        import jax, jax.numpy as jnp
        import numpy as np
        DIM = 256
        DIM_LATENT = 256
        DIM_HEAD = 64
        INNER = max(DIM, DIM_LATENT)
        HEADS = INNER // DIM_HEAD
        SCALE = DIM_HEAD ** (-0.5)
        LN_EPS = 1e-05
        RMS_EPS = 1e-08

        def layernorm(x, g, b):
            mu = jnp.mean(x, axis=-1, keepdims=True)
            var = jnp.mean(jnp.square(x - mu), axis=-1, keepdims=True)
            return (x - mu) * jax.lax.rsqrt(var + LN_EPS) * g + b

        def rmsnorm(x, gamma):
            n = jnp.linalg.norm(x, axis=-1, keepdims=True) * x.shape[-1] ** (-0.5)
            return x / jnp.maximum(n, RMS_EPS) * gamma
        key = jax.random.key(seed)
        ks = jax.random.split(key, 8)
        b, n, nl = (8, 512, 128)
        x = jax.random.normal(ks[0], (b, n, DIM), dtype=jnp.float32)
        latents = jax.random.normal(ks[1], (b, nl, DIM_LATENT), dtype=jnp.float32)
        mask = jax.random.randint(ks[2], (b, n), 0, 2).astype(bool)
        init = lambda k, shape, fan_in: jax.random.normal(k, shape, jnp.float32) * fan_in ** (-0.5)
        return {'x': x, 'latents': latents, 'mask': mask, 'ln_x_g': jnp.ones((DIM,), jnp.float32), 'ln_x_b': jnp.zeros((DIM,), jnp.float32), 'ln_l_g': jnp.ones((DIM_LATENT,), jnp.float32), 'ln_l_b': jnp.zeros((DIM_LATENT,), jnp.float32), 'q_gamma': jnp.ones((DIM_HEAD,), jnp.float32), 'k_gamma': jnp.ones((DIM_HEAD,), jnp.float32), 'W_q': init(ks[3], (DIM_LATENT, INNER), DIM_LATENT), 'W_kv': init(ks[4], (DIM, 2 * INNER), DIM), 'W_out': init(ks[5], (INNER, DIM_LATENT), INNER), 'b_out': jnp.zeros((DIM_LATENT,), jnp.float32)}
    _L2_xattn_all = _L2_xattn_setup()
    _L2_xattn_in = {k: v for k, v in _L2_xattn_all.items() if k in ('ln_x_g', 'ln_x_b', 'ln_l_g', 'ln_l_b', 'q_gamma', 'k_gamma', 'W_q', 'W_kv', 'W_out', 'b_out')}
    del _L2_xattn_all

    def _L2_ffn_setup():
        import jax, jax.numpy as jnp
        import numpy as np
        import math
        D_IN = 256
        FEATURES = (1024, 1024, 256)
        BATCH, SEQ = (8, 512)

        def _conn_dense(kernel_bool, x):
            w = jnp.where(kernel_bool, jnp.float32(1.0), jnp.float32(-1.0))
            return x @ w
        key = jax.random.key(seed)
        kx, kk0, kk1, kk2 = jax.random.split(key, 4)
        x = jax.random.normal(kx, (BATCH, SEQ, D_IN), dtype=jnp.float32)
        k0 = jax.random.randint(kk0, (2 * D_IN, FEATURES[0]), 0, 2).astype(jnp.bool_)
        k1 = jax.random.randint(kk1, (FEATURES[0], FEATURES[1]), 0, 2).astype(jnp.bool_)
        k2 = jax.random.randint(kk2, (FEATURES[1], FEATURES[2]), 0, 2).astype(jnp.bool_)
        s0 = jnp.asarray(1.0 / math.sqrt(2 * D_IN), dtype=jnp.float32)
        s1 = jnp.asarray(1.0 / math.sqrt(FEATURES[0]), dtype=jnp.float32)
        s2 = jnp.asarray(1.0 / math.sqrt(FEATURES[1]), dtype=jnp.float32)
        return {'x': x, 'k0': k0, 'k1': k1, 'k2': k2, 's0': s0, 's1': s1, 's2': s2}
    _L2_ffn_all = _L2_ffn_setup()
    _L2_ffn_in = {k: v for k, v in _L2_ffn_all.items() if k in ('k0', 'k1', 'k2', 's0', 's1', 's2')}
    del _L2_ffn_all

    def _L3_attn_setup():
        import jax, jax.numpy as jnp
        import numpy as np
        B, T, D = (4, 1024, 256)
        C = 8.0
        LOGIT_LO = float(np.log(0.9 / 0.1))
        LOGIT_HI = float(np.log(0.999 / 0.001))

        def rms_norm(x, g):
            n = jnp.maximum(jnp.linalg.norm(x, axis=-1, keepdims=True), 1e-12)
            return x / n * x.shape[-1] ** 0.5 * g

        def rg_lru(x, Wa, ba, Wx, bx, Lam):
            rt = jax.nn.sigmoid(jnp.einsum('btd,hd->bth', x, Wa) + ba)
            it = jax.nn.sigmoid(jnp.einsum('btd,hd->bth', x, Wx) + bx)
            log_a = -jax.nn.softplus(-Lam)
            a = jnp.exp(log_a * rt / C)
            gated = jnp.sqrt(1.0 - a * a) * (it * x)

            def step(h, ag):
                at, gt = ag
                h = at * h + gt
                return (h, h)
            h0 = jnp.zeros((x.shape[0], x.shape[2]), x.dtype)
            _, hs = jax.lax.scan(step, h0, (jnp.swapaxes(a, 0, 1), jnp.swapaxes(gated, 0, 1)))
            return jnp.swapaxes(hs, 0, 1)
        key = jax.random.key(seed)
        ks = jax.random.split(key, 12)
        s = 1.0 / np.sqrt(D)
        z = lambda: jnp.zeros((D,), jnp.float32)
        return {'x': jax.random.normal(ks[0], (B, T, D), jnp.float32), 'g1': jnp.ones((D,), jnp.float32), 'g2': jnp.ones((D,), jnp.float32), 'W_lin': jax.random.normal(ks[1], (D, D), jnp.float32) * s, 'b_lin': z(), 'W_conv': jax.random.normal(ks[2], (D, D), jnp.float32) * s, 'b_conv': z(), 'W_lin2': jax.random.normal(ks[3], (D, D), jnp.float32) * s, 'b_lin2': z(), 'Wa': jax.random.normal(ks[4], (D, D), jnp.float32) * s, 'ba': z(), 'Wx': jax.random.normal(ks[5], (D, D), jnp.float32) * s, 'bx': z(), 'Lam': jax.random.uniform(ks[6], (D,), jnp.float32, LOGIT_LO, LOGIT_HI), 'W1': jax.random.normal(ks[7], (D, D), jnp.float32) * s, 'b1': z(), 'W2': jax.random.normal(ks[8], (D, D), jnp.float32) * s, 'b2': z(), 'W3': jax.random.normal(ks[9], (D, D), jnp.float32) * s, 'b3': z()}
    _L3_attn_all = _L3_attn_setup()
    _L3_attn_in = {k: v for k, v in _L3_attn_all.items() if k in ('g1', 'g2', 'W_lin', 'b_lin', 'W_conv', 'b_conv', 'W_lin2', 'b_lin2', 'Wa', 'ba', 'Wx', 'bx', 'Lam', 'W1', 'b1', 'W2', 'b2', 'W3', 'b3')}
    del _L3_attn_all

    def _L3_xattn_setup():
        import jax, jax.numpy as jnp
        import numpy as np
        B, S, F = (2, 512, 256)
        H, DH = (16, 64)
        O = 256
        key = jax.random.key(seed)
        ks = jax.random.split(key, 7)
        sc = 0.02
        return {'inputs_q': jax.random.normal(ks[0], (B, S, F), jnp.float32), 'inputs_kv': jax.random.normal(ks[1], (B, S, F), jnp.float32), 'wq': jax.random.normal(ks[2], (F, H, DH), jnp.float32) * sc, 'wk': jax.random.normal(ks[3], (F, H, DH), jnp.float32) * sc, 'wv': jax.random.normal(ks[4], (F, H, DH), jnp.float32) * sc, 'wo': jax.random.normal(ks[5], (H, DH, O), jnp.float32) * sc, 'bo': jnp.zeros((O,), jnp.float32)}
    _L3_xattn_all = _L3_xattn_setup()
    _L3_xattn_in = {k: v for k, v in _L3_xattn_all.items() if k in ('wq', 'wk', 'wv', 'wo', 'bo')}
    del _L3_xattn_all

    def _L3_ffn_setup():
        import jax, jax.numpy as jnp
        import numpy as np
        EPS = 1e-08

        def _ternary_linear(x, w):
            alpha = jnp.mean(jnp.abs(w))
            w_t = jnp.sign(w) * (jnp.abs(w) > 0.5 * alpha).astype(w.dtype)
            w_q = w + jax.lax.stop_gradient(w_t - w)
            d = x.shape[-1]
            rms = jnp.sqrt(jnp.sum(x * x, axis=-1, keepdims=True)) / jnp.sqrt(jnp.asarray(d, x.dtype))
            x_norm = x / (rms + EPS)
            return jnp.einsum('bsd,fd->bsf', x_norm, w_q)
        key = jax.random.key(seed)
        k1, k2, k3 = jax.random.split(key, 3)
        d_model, d_ff = (256, 1024)
        B, S = (4, 1024)
        x = jax.random.normal(k1, (B, S, d_model), dtype=jnp.float32)
        w_up = jax.random.normal(k2, (d_ff, d_model), dtype=jnp.float32) * 0.02
        w_down = jax.random.normal(k3, (d_model, d_ff), dtype=jnp.float32) * 0.02
        return {'x': x, 'w_up': w_up, 'w_down': w_down}
    _L3_ffn_all = _L3_ffn_setup()
    _L3_ffn_in = {k: v for k, v in _L3_ffn_all.items() if k in ('w_up', 'w_down')}
    del _L3_ffn_all
    return {'x': x, 'ctx_1024': ctx_1024, 'fside_Bx16xSxS2_0': fside_Bx16xSxS2_0, 'fside_SxS2_0': fside_SxS2_0, 'mask_BxS2_bf0': mask_BxS2_bf0, 'mask_BxS2_bk0': mask_BxS2_bk0, 'L0_attn_W_in': _L0_attn_in['W_in'], 'L0_attn_W_conv': _L0_attn_in['W_conv'], 'L0_attn_b_conv': _L0_attn_in['b_conv'], 'L0_attn_W_out': _L0_attn_in['W_out'], 'L0_attn_fA_log': _L0_attn_in['fA_log'], 'L0_attn_fD': _L0_attn_in['fD'], 'L0_attn_fWx': _L0_attn_in['fWx'], 'L0_attn_fWdt': _L0_attn_in['fWdt'], 'L0_attn_fbdt': _L0_attn_in['fbdt'], 'L0_attn_bA_log': _L0_attn_in['bA_log'], 'L0_attn_bD': _L0_attn_in['bD'], 'L0_attn_bWx': _L0_attn_in['bWx'], 'L0_attn_bWdt': _L0_attn_in['bWdt'], 'L0_attn_bbdt': _L0_attn_in['bbdt'], 'L0_xattn_ln_m_g': _L0_xattn_in['ln_m_g'], 'L0_xattn_ln_m_b': _L0_xattn_in['ln_m_b'], 'L0_xattn_ln_l_g': _L0_xattn_in['ln_l_g'], 'L0_xattn_ln_l_b': _L0_xattn_in['ln_l_b'], 'L0_xattn_Wq': _L0_xattn_in['Wq'], 'L0_xattn_Wkv': _L0_xattn_in['Wkv'], 'L0_xattn_Wout': _L0_xattn_in['Wout'], 'L0_ffn_router_w': _L0_ffn_in['router_w'], 'L0_ffn_router_b': _L0_ffn_in['router_b'], 'L0_ffn_sw1': _L0_ffn_in['sw1'], 'L0_ffn_sb1': _L0_ffn_in['sb1'], 'L0_ffn_sw2': _L0_ffn_in['sw2'], 'L0_ffn_sb2': _L0_ffn_in['sb2'], 'L0_ffn_rw1': _L0_ffn_in['rw1'], 'L0_ffn_rb1': _L0_ffn_in['rb1'], 'L0_ffn_rw2': _L0_ffn_in['rw2'], 'L0_ffn_rb2': _L0_ffn_in['rb2'], 'L1_attn_w_qkv': _L1_attn_in['w_qkv'], 'L1_attn_w_pre': _L1_attn_in['w_pre'], 'L1_attn_w_post': _L1_attn_in['w_post'], 'L1_attn_w_out': _L1_attn_in['w_out'], 'L1_attn_b_out': _L1_attn_in['b_out'], 'L1_xattn_Wq': _L1_xattn_in['Wq'], 'L1_xattn_bq': _L1_xattn_in['bq'], 'L1_xattn_Wk': _L1_xattn_in['Wk'], 'L1_xattn_bk': _L1_xattn_in['bk'], 'L1_xattn_Wv': _L1_xattn_in['Wv'], 'L1_xattn_bv': _L1_xattn_in['bv'], 'L1_xattn_Wo': _L1_xattn_in['Wo'], 'L1_xattn_bo': _L1_xattn_in['bo'], 'L1_ffn_Wq': _L1_ffn_in['Wq'], 'L1_ffn_bq': _L1_ffn_in['bq'], 'L1_ffn_Wk': _L1_ffn_in['Wk'], 'L1_ffn_bk': _L1_ffn_in['bk'], 'L1_ffn_Wv': _L1_ffn_in['Wv'], 'L1_ffn_bv': _L1_ffn_in['bv'], 'L1_ffn_Wg1': _L1_ffn_in['Wg1'], 'L1_ffn_bg1': _L1_ffn_in['bg1'], 'L1_ffn_Wg2': _L1_ffn_in['Wg2'], 'L1_ffn_bg2': _L1_ffn_in['bg2'], 'L1_ffn_Wo': _L1_ffn_in['Wo'], 'L1_ffn_bo': _L1_ffn_in['bo'], 'L2_attn_Wq': _L2_attn_in['Wq'], 'L2_attn_Wk': _L2_attn_in['Wk'], 'L2_attn_Wv': _L2_attn_in['Wv'], 'L2_attn_Wo': _L2_attn_in['Wo'], 'L2_xattn_ln_x_g': _L2_xattn_in['ln_x_g'], 'L2_xattn_ln_x_b': _L2_xattn_in['ln_x_b'], 'L2_xattn_ln_l_g': _L2_xattn_in['ln_l_g'], 'L2_xattn_ln_l_b': _L2_xattn_in['ln_l_b'], 'L2_xattn_q_gamma': _L2_xattn_in['q_gamma'], 'L2_xattn_k_gamma': _L2_xattn_in['k_gamma'], 'L2_xattn_W_q': _L2_xattn_in['W_q'], 'L2_xattn_W_kv': _L2_xattn_in['W_kv'], 'L2_xattn_W_out': _L2_xattn_in['W_out'], 'L2_xattn_b_out': _L2_xattn_in['b_out'], 'L2_ffn_k0': _L2_ffn_in['k0'], 'L2_ffn_k1': _L2_ffn_in['k1'], 'L2_ffn_k2': _L2_ffn_in['k2'], 'L2_ffn_s0': _L2_ffn_in['s0'], 'L2_ffn_s1': _L2_ffn_in['s1'], 'L2_ffn_s2': _L2_ffn_in['s2'], 'L3_attn_g1': _L3_attn_in['g1'], 'L3_attn_g2': _L3_attn_in['g2'], 'L3_attn_W_lin': _L3_attn_in['W_lin'], 'L3_attn_b_lin': _L3_attn_in['b_lin'], 'L3_attn_W_conv': _L3_attn_in['W_conv'], 'L3_attn_b_conv': _L3_attn_in['b_conv'], 'L3_attn_W_lin2': _L3_attn_in['W_lin2'], 'L3_attn_b_lin2': _L3_attn_in['b_lin2'], 'L3_attn_Wa': _L3_attn_in['Wa'], 'L3_attn_ba': _L3_attn_in['ba'], 'L3_attn_Wx': _L3_attn_in['Wx'], 'L3_attn_bx': _L3_attn_in['bx'], 'L3_attn_Lam': _L3_attn_in['Lam'], 'L3_attn_W1': _L3_attn_in['W1'], 'L3_attn_b1': _L3_attn_in['b1'], 'L3_attn_W2': _L3_attn_in['W2'], 'L3_attn_b2': _L3_attn_in['b2'], 'L3_attn_W3': _L3_attn_in['W3'], 'L3_attn_b3': _L3_attn_in['b3'], 'L3_xattn_wq': _L3_xattn_in['wq'], 'L3_xattn_wk': _L3_xattn_in['wk'], 'L3_xattn_wv': _L3_xattn_in['wv'], 'L3_xattn_wo': _L3_xattn_in['wo'], 'L3_xattn_bo': _L3_xattn_in['bo'], 'L3_ffn_w_up': _L3_ffn_in['w_up'], 'L3_ffn_w_down': _L3_ffn_in['w_down']}

def reference(x, ctx_1024, fside_Bx16xSxS2_0, fside_SxS2_0, mask_BxS2_bf0, mask_BxS2_bk0, L0_attn_W_in, L0_attn_W_conv, L0_attn_b_conv, L0_attn_W_out, L0_attn_fA_log, L0_attn_fD, L0_attn_fWx, L0_attn_fWdt, L0_attn_fbdt, L0_attn_bA_log, L0_attn_bD, L0_attn_bWx, L0_attn_bWdt, L0_attn_bbdt, L0_xattn_ln_m_g, L0_xattn_ln_m_b, L0_xattn_ln_l_g, L0_xattn_ln_l_b, L0_xattn_Wq, L0_xattn_Wkv, L0_xattn_Wout, L0_ffn_router_w, L0_ffn_router_b, L0_ffn_sw1, L0_ffn_sb1, L0_ffn_sw2, L0_ffn_sb2, L0_ffn_rw1, L0_ffn_rb1, L0_ffn_rw2, L0_ffn_rb2, L1_attn_w_qkv, L1_attn_w_pre, L1_attn_w_post, L1_attn_w_out, L1_attn_b_out, L1_xattn_Wq, L1_xattn_bq, L1_xattn_Wk, L1_xattn_bk, L1_xattn_Wv, L1_xattn_bv, L1_xattn_Wo, L1_xattn_bo, L1_ffn_Wq, L1_ffn_bq, L1_ffn_Wk, L1_ffn_bk, L1_ffn_Wv, L1_ffn_bv, L1_ffn_Wg1, L1_ffn_bg1, L1_ffn_Wg2, L1_ffn_bg2, L1_ffn_Wo, L1_ffn_bo, L2_attn_Wq, L2_attn_Wk, L2_attn_Wv, L2_attn_Wo, L2_xattn_ln_x_g, L2_xattn_ln_x_b, L2_xattn_ln_l_g, L2_xattn_ln_l_b, L2_xattn_q_gamma, L2_xattn_k_gamma, L2_xattn_W_q, L2_xattn_W_kv, L2_xattn_W_out, L2_xattn_b_out, L2_ffn_k0, L2_ffn_k1, L2_ffn_k2, L2_ffn_s0, L2_ffn_s1, L2_ffn_s2, L3_attn_g1, L3_attn_g2, L3_attn_W_lin, L3_attn_b_lin, L3_attn_W_conv, L3_attn_b_conv, L3_attn_W_lin2, L3_attn_b_lin2, L3_attn_Wa, L3_attn_ba, L3_attn_Wx, L3_attn_bx, L3_attn_Lam, L3_attn_W1, L3_attn_b1, L3_attn_W2, L3_attn_b2, L3_attn_W3, L3_attn_b3, L3_xattn_wq, L3_xattn_wk, L3_xattn_wv, L3_xattn_wo, L3_xattn_bo, L3_ffn_w_up, L3_ffn_w_down):
    import jax
    import jax.numpy as jnp

    def _L0_attn_ref(x, W_in, W_conv, b_conv, W_out, fA_log, fD, fWx, fWdt, fbdt, bA_log, bD, bWx, bWdt, bbdt):
        import jax, jax.numpy as jnp
        import numpy as np
        D_MODEL = 256
        D_INNER = 512
        D_CONV = 4
        D_STATE = 16
        DT_RANK = 64
        BATCH = 2
        SEQ = 256

        def _depthwise_causal_conv(u, w, b):
            out = jax.lax.conv_general_dilated(u, w, window_strides=(1,), padding=[(D_CONV - 1, 0)], dimension_numbers=('NCH', 'OIH', 'NCH'), feature_group_count=D_INNER)
            return out + b[None, :, None]

        def _s6(u, A_log, D, Wx, Wdt, bdt):
            A = -jnp.exp(A_log)
            dbc = jnp.einsum('bld,ed->ble', u, Wx)
            dt = dbc[..., :DT_RANK]
            Bm = dbc[..., DT_RANK:DT_RANK + D_STATE]
            Cm = dbc[..., DT_RANK + D_STATE:]
            delta = jax.nn.softplus(jnp.einsum('blr,dr->bld', dt, Wdt) + bdt)
            dA = jnp.exp(delta[..., None] * A)
            dBu = delta[..., None] * Bm[:, :, None, :] * u[..., None]

            def step(h, inp):
                dA_t, dBu_t, C_t = inp
                h = dA_t * h + dBu_t
                y = jnp.einsum('bdn,bn->bd', h, C_t)
                return (h, y)
            h0 = jnp.zeros((u.shape[0], u.shape[2], D_STATE), u.dtype)
            _, ys = jax.lax.scan(step, h0, (dA.transpose(1, 0, 2, 3), dBu.transpose(1, 0, 2, 3), Cm.transpose(1, 0, 2)))
            return ys.transpose(1, 0, 2) + u * D
        xr = jnp.einsum('blm,em->ble', x, W_in)
        u, res = jnp.split(xr, 2, axis=-1)
        u = _depthwise_causal_conv(u.transpose(0, 2, 1), W_conv, b_conv).transpose(0, 2, 1)
        u = jax.nn.silu(u)
        y_fwd = _s6(u, fA_log, fD, fWx, fWdt, fbdt)
        y_rev = jnp.flip(_s6(jnp.flip(u, axis=1), bA_log, bD, bWx, bWdt, bbdt), axis=1)
        y = (y_fwd + y_rev) * 0.5 * jax.nn.silu(res)
        return jnp.einsum('bld,md->blm', y, W_out)

    def _L0_xattn_ref(x, latents, ln_m_g, ln_m_b, ln_l_g, ln_l_b, Wq, Wkv, Wout):
        import jax, jax.numpy as jnp
        import numpy as np
        EPS = 1e-05

        def layer_norm(x, g, b):
            mu = jnp.mean(x, axis=-1, keepdims=True)
            var = jnp.var(x, axis=-1, keepdims=True)
            return (x - mu) * jax.lax.rsqrt(var + EPS) * g + b
        heads, dim_head = (16, 64)
        scale = dim_head ** (-0.5)
        x = layer_norm(x, ln_m_g, ln_m_b)
        lat = layer_norm(latents, ln_l_g, ln_l_b)
        b, m, _ = lat.shape
        q = lat @ Wq
        kv_input = jnp.concatenate([x, lat], axis=1)
        kv = kv_input @ Wkv
        k, v = jnp.split(kv, 2, axis=-1)

        def split_heads(t):
            return t.reshape(t.shape[0], t.shape[1], heads, dim_head).transpose(0, 2, 1, 3)
        q, k, v = (split_heads(q), split_heads(k), split_heads(v))
        dots = jnp.einsum('bhid,bhjd->bhij', q, k) * scale
        attn = jax.nn.softmax(dots, axis=-1)
        out = jnp.einsum('bhij,bhjd->bhid', attn, v)
        out = out.transpose(0, 2, 1, 3).reshape(b, m, heads * dim_head)
        return out @ Wout

    def _L0_ffn_ref(hidden, router_w, router_b, sw1, sb1, sw2, sb2, rw1, rb1, rw2, rb2):
        import jax, jax.numpy as jnp
        import numpy as np
        D = 256
        H = 512
        E = 8
        TOP_K = 2
        N_SHARED = 1
        B, S = (2, 256)
        b, s, d = hidden.shape
        T = b * s
        flat = hidden.reshape(T, d)
        router_logits = flat @ router_w + router_b
        router_probs = jax.nn.softmax(router_logits, axis=-1)
        topk_probs, topk_idx = jax.lax.top_k(router_probs, TOP_K)
        weights = jnp.zeros_like(router_probs).at[jnp.arange(T)[:, None], topk_idx].add(topk_probs)
        sh = jax.nn.gelu(flat @ sw1 + sb1, approximate=False)
        shared_out = (sh @ sw2 + sb2) / N_SHARED
        h1 = jax.nn.gelu(jnp.einsum('td,edh->teh', flat, rw1) + rb1[None], approximate=False)
        expert_out = jnp.einsum('teh,ehd->ted', h1, rw2) + rb2[None]
        mixed = jnp.einsum('ted,te->td', expert_out, weights)
        return (shared_out + mixed).reshape(b, s, d)

    def _L1_attn_ref(x, w_qkv, w_pre, w_post, w_out, b_out):
        import jax, jax.numpy as jnp
        import numpy as np
        EMBED_DIM = 256
        HEADS = 16
        HEAD_DIM = EMBED_DIM // HEADS
        ROPE_THETA = 10000.0

        def apply_rope(x):
            D = x.shape[-1]
            T = x.shape[-2]
            half = D // 2
            inv_freq = 1.0 / ROPE_THETA ** (jnp.arange(half, dtype=jnp.float32) / half)
            ang = jnp.arange(T, dtype=jnp.float32)[:, None] * inv_freq[None, :]
            cos, sin = (jnp.cos(ang), jnp.sin(ang))
            x1, x2 = (x[..., :half], x[..., half:])
            return jnp.concatenate([x1 * cos - x2 * sin, x1 * sin + x2 * cos], axis=-1)
        B, T, E = x.shape
        H, D = (HEADS, HEAD_DIM)
        qkv = x @ w_qkv
        q, k, v = jnp.split(qkv, 3, axis=-1)
        q = q.reshape(B, T, H, D).transpose(0, 2, 1, 3)
        k = k.reshape(B, T, H, D).transpose(0, 2, 1, 3)
        v = v.reshape(B, T, H, D).transpose(0, 2, 1, 3)
        q = apply_rope(q)
        k = apply_rope(k)
        scale = D ** (-0.5)
        dots = jnp.einsum('bhid,bhjd->bhij', q, k) * scale
        dots = jnp.einsum('bhij,gh->bgij', dots, w_pre)
        attn = jax.nn.softmax(dots, axis=-1)
        attn = jnp.einsum('bhij,gh->bgij', attn, w_post)
        out = jnp.einsum('bhij,bhjd->bhid', attn, v)
        out = out.transpose(0, 2, 1, 3).reshape(B, T, E)
        return out @ w_out.T + b_out

    def _L1_xattn_ref(query, key, value, spatial_bias, directional_bias, key_padding_mask, attn_mask, Wq, bq, Wk, bk, Wv, bv, Wo, bo):
        import jax, jax.numpy as jnp
        import numpy as np
        E = 256
        H = 16
        D = E // H
        B, T, _ = query.shape
        S = key.shape[1]
        scale = D ** (-0.5)
        q = (query @ Wq.T + bq).reshape(B, T, H, D).transpose(0, 2, 1, 3)
        k = (key @ Wk.T + bk).reshape(B, S, H, D).transpose(0, 2, 1, 3)
        v = (value @ Wv.T + bv).reshape(B, S, H, D).transpose(0, 2, 1, 3)
        scores = jnp.einsum('bhtd,bhsd->bhts', q, k) * scale
        scores = scores + attn_mask[None, None, :, :]
        pad = key_padding_mask[:, None, None, :]
        scores = jnp.where(pad, -jnp.inf, scores)
        if T == S:
            scores = scores + spatial_bias + directional_bias
        probs = jax.nn.softmax(scores, axis=-1)
        out = jnp.einsum('bhts,bhsd->bhtd', probs, v)
        out = out.transpose(0, 2, 1, 3).reshape(B, T, E)
        return out @ Wo.T + bo

    def _L1_ffn_ref(hidden_states, Wq, bq, Wk, bk, Wv, bv, Wg1, bg1, Wg2, bg2, Wo, bo):
        import jax, jax.numpy as jnp
        import numpy as np
        N_HEADS = 16
        NUM_EXPERTS = 4
        TOP_K = 2
        D_MODEL = 256
        GATE_HID = 128
        B, T, C = hidden_states.shape
        H = N_HEADS
        D = C // H
        pooled = hidden_states.mean(axis=1)
        logits = jax.nn.relu(pooled @ Wg1 + bg1) @ Wg2 + bg2
        vals, idx = jax.lax.top_k(logits, TOP_K)
        sm = jax.nn.softmax(vals, axis=-1)
        weights = jnp.zeros_like(logits).at[jnp.arange(B)[:, None], idx].set(sm)

        def moe_proj(W, b):
            Wc = jnp.einsum('be,ecd->bcd', weights, W)
            bc = weights @ b
            return jnp.einsum('btc,bcd->btd', hidden_states, Wc) + bc[:, None, :]
        q = moe_proj(Wq, bq).reshape(B, T, H, D)
        k = moe_proj(Wk, bk).reshape(B, T, H, D)
        v = moe_proj(Wv, bv).reshape(B, T, H, D)
        scores = jnp.einsum('bthd,bshd->bhts', q, k) / np.sqrt(D).astype(np.float32)
        attn = jax.nn.softmax(scores, axis=-1)
        out = jnp.einsum('bhts,bshd->bthd', attn, v).reshape(B, T, C)
        return out @ Wo + bo

    def _L2_attn_ref(x, Wq, Wk, Wv, Wo):
        import jax, jax.numpy as jnp
        import numpy as np
        DIM = 256
        HEADS = 16
        HEAD_DIM = DIM // HEADS
        WINDOW = 64
        THETA = 10000.0

        def _rope_tables(n, hd, dtype):
            inv_freq = 1.0 / THETA ** (jnp.arange(0, hd, 2, dtype=jnp.float32) / hd)
            ang = jnp.arange(n, dtype=jnp.float32)[:, None] * inv_freq[None, :]
            cos = jnp.concatenate([jnp.cos(ang), jnp.cos(ang)], axis=-1).astype(dtype)
            sin = jnp.concatenate([jnp.sin(ang), jnp.sin(ang)], axis=-1).astype(dtype)
            return (cos, sin)

        def _rotate_half(x):
            h = x.shape[-1] // 2
            return jnp.concatenate([-x[..., h:], x[..., :h]], axis=-1)

        def _alibi_slopes(h):
            return 2.0 ** (-jnp.arange(1, h + 1, dtype=jnp.float32) * (8.0 / h))
        B, N, C = x.shape
        H, hd = (HEADS, HEAD_DIM)
        scale = hd ** (-0.5)
        neg = jnp.float32(-jnp.inf)
        q = (x @ Wq).reshape(B, N, H, hd).transpose(0, 2, 1, 3)
        k = (x @ Wk).reshape(B, N, H, hd).transpose(0, 2, 1, 3)
        v = (x @ Wv).reshape(B, N, H, hd).transpose(0, 2, 1, 3)
        cos, sin = _rope_tables(N, hd, x.dtype)
        q = q * cos + _rotate_half(q) * sin
        k = k * cos + _rotate_half(k) * sin
        scores = jnp.einsum('bhid,bhjd->bhij', q, k) * scale
        idx = jnp.arange(N)
        dist = (idx[None, :] - idx[:, None]).astype(x.dtype)
        slopes = _alibi_slopes(H).astype(x.dtype)
        scores = scores + dist[None, None, :, :] * slopes[None, :, None, None]
        causal = idx[:, None] >= idx[None, :]
        band = jnp.abs(idx[:, None] - idx[None, :]) <= WINDOW
        mask_local = causal & band
        scores_local = jnp.where(mask_local[None, None], scores, neg)
        attn_local = jax.nn.softmax(scores_local, axis=-1)
        out_local = jnp.einsum('bhij,bhjd->bhid', attn_local, v)
        kg = k[:, :, ::WINDOW, :]
        vg = v[:, :, ::WINDOW, :]
        scores_g = jnp.einsum('bhid,bhjd->bhij', q, kg) * scale
        attn_g = jax.nn.softmax(scores_g, axis=-1)
        out_g = jnp.einsum('bhij,bhjd->bhid', attn_g, vg)
        out = (out_local + out_g).transpose(0, 2, 1, 3).reshape(B, N, C)
        return out @ Wo

    def _L2_xattn_ref(x, latents, mask, ln_x_g, ln_x_b, ln_l_g, ln_l_b, q_gamma, k_gamma, W_q, W_kv, W_out, b_out):
        import jax, jax.numpy as jnp
        import numpy as np
        DIM = 256
        DIM_LATENT = 256
        DIM_HEAD = 64
        INNER = max(DIM, DIM_LATENT)
        HEADS = INNER // DIM_HEAD
        SCALE = DIM_HEAD ** (-0.5)
        LN_EPS = 1e-05
        RMS_EPS = 1e-08

        def layernorm(x, g, b):
            mu = jnp.mean(x, axis=-1, keepdims=True)
            var = jnp.mean(jnp.square(x - mu), axis=-1, keepdims=True)
            return (x - mu) * jax.lax.rsqrt(var + LN_EPS) * g + b

        def rmsnorm(x, gamma):
            n = jnp.linalg.norm(x, axis=-1, keepdims=True) * x.shape[-1] ** (-0.5)
            return x / jnp.maximum(n, RMS_EPS) * gamma
        b, n, _ = x.shape
        nl = latents.shape[1]
        xn = layernorm(x, ln_x_g, ln_x_b)
        ln = layernorm(latents, ln_l_g, ln_l_b)
        q = ln @ W_q
        kv = jnp.concatenate([xn @ W_kv, ln @ W_kv], axis=1)
        k, v = (kv[..., :INNER], kv[..., INNER:])
        to_heads = lambda t: t.reshape(t.shape[0], t.shape[1], HEADS, DIM_HEAD).transpose(0, 2, 1, 3)
        q, k, v = (to_heads(q), to_heads(k), to_heads(v))
        qn = rmsnorm(q, q_gamma) * SCALE
        kn = rmsnorm(k, k_gamma)
        sim = jnp.einsum('bhid,bhjd->bhij', qn, kn)
        full_mask = jnp.pad(mask, ((0, 0), (0, nl)), constant_values=True)
        neg = -jnp.finfo(sim.dtype).max
        sim = jnp.where(full_mask[:, None, None, :], sim, neg)
        attn = jax.nn.softmax(sim.astype(jnp.float32), axis=-1).astype(sim.dtype)
        out = jnp.einsum('bhij,bhjd->bhid', attn, v)
        out = out.transpose(0, 2, 1, 3).reshape(b, nl, INNER)
        return out @ W_out + b_out

    def _L2_ffn_ref(x, k0, k1, k2, s0, s1, s2):
        import jax, jax.numpy as jnp
        import numpy as np
        import math
        D_IN = 256
        FEATURES = (1024, 1024, 256)
        BATCH, SEQ = (8, 512)

        def _conn_dense(kernel_bool, x):
            w = jnp.where(kernel_bool, jnp.float32(1.0), jnp.float32(-1.0))
            return x @ w
        h = jnp.concatenate([x, -x], axis=-1)
        h = s0 * _conn_dense(k0, h)
        h = jax.nn.relu(h) * 2
        h = s1 * _conn_dense(k1, h)
        h = jax.nn.relu(h) * 2
        h = s2 * _conn_dense(k2, h)
        return h

    def _L3_attn_ref(x, g1, g2, W_lin, b_lin, W_conv, b_conv, W_lin2, b_lin2, Wa, ba, Wx, bx, Lam, W1, b1, W2, b2, W3, b3):
        import jax, jax.numpy as jnp
        import numpy as np
        B, T, D = (4, 1024, 256)
        C = 8.0
        LOGIT_LO = float(np.log(0.9 / 0.1))
        LOGIT_HI = float(np.log(0.999 / 0.001))

        def rms_norm(x, g):
            n = jnp.maximum(jnp.linalg.norm(x, axis=-1, keepdims=True), 1e-12)
            return x / n * x.shape[-1] ** 0.5 * g

        def rg_lru(x, Wa, ba, Wx, bx, Lam):
            rt = jax.nn.sigmoid(jnp.einsum('btd,hd->bth', x, Wa) + ba)
            it = jax.nn.sigmoid(jnp.einsum('btd,hd->bth', x, Wx) + bx)
            log_a = -jax.nn.softplus(-Lam)
            a = jnp.exp(log_a * rt / C)
            gated = jnp.sqrt(1.0 - a * a) * (it * x)

            def step(h, ag):
                at, gt = ag
                h = at * h + gt
                return (h, h)
            h0 = jnp.zeros((x.shape[0], x.shape[2]), x.dtype)
            _, hs = jax.lax.scan(step, h0, (jnp.swapaxes(a, 0, 1), jnp.swapaxes(gated, 0, 1)))
            return jnp.swapaxes(hs, 0, 1)
        residual = x
        xn = rms_norm(x, g1)
        lin = xn @ W_lin.T + b_lin
        x_gel = jax.nn.gelu(lin, approximate=False)
        x_rg = lin @ W_conv.T + b_conv
        x_rg = rg_lru(x_rg, Wa, ba, Wx, bx, Lam)
        xr = x_gel * x_rg @ W_lin2.T + b_lin2
        residual = xr + residual
        xm = rms_norm(residual, g2)
        out = jax.nn.sigmoid(xm @ W1.T + b1)
        gate = jax.nn.gelu(out, approximate=False)
        combined = gate * (xm @ W2.T + b2)
        y = combined @ W3.T + b3
        return y + residual

    def _L3_xattn_ref(inputs_q, inputs_kv, wq, wk, wv, wo, bo):
        import jax, jax.numpy as jnp
        import numpy as np
        B, S, F = (2, 512, 256)
        H, DH = (16, 64)
        O = 256
        q = jnp.einsum('bsf,fhd->bshd', inputs_q, wq)
        k = jnp.einsum('bsf,fhd->bshd', inputs_kv, wk)
        v = jnp.einsum('bsf,fhd->bshd', inputs_kv, wv)
        q = q / jnp.sqrt(jnp.asarray(DH, q.dtype))
        scores = jnp.einsum('bqhd,bkhd->bhqk', q, k)
        attn = jax.nn.softmax(scores, axis=-1)
        y = jnp.einsum('bhqk,bkhd->bqhd', attn, v)
        out = jnp.einsum('bqhd,hdo->bqo', y, wo) + bo
        return out

    def _L3_ffn_ref(x, w_up, w_down):
        import jax, jax.numpy as jnp
        import numpy as np
        EPS = 1e-08

        def _ternary_linear(x, w):
            alpha = jnp.mean(jnp.abs(w))
            w_t = jnp.sign(w) * (jnp.abs(w) > 0.5 * alpha).astype(w.dtype)
            w_q = w + jax.lax.stop_gradient(w_t - w)
            d = x.shape[-1]
            rms = jnp.sqrt(jnp.sum(x * x, axis=-1, keepdims=True)) / jnp.sqrt(jnp.asarray(d, x.dtype))
            x_norm = x / (rms + EPS)
            return jnp.einsum('bsd,fd->bsf', x_norm, w_q)
        h = jax.nn.gelu(_ternary_linear(x, w_up), approximate=False)
        return _ternary_linear(h, w_down)
    x = x + _L0_attn_ref(_layernorm(x, axis=-1), L0_attn_W_in, L0_attn_W_conv, L0_attn_b_conv, L0_attn_W_out, L0_attn_fA_log, L0_attn_fD, L0_attn_fWx, L0_attn_fWdt, L0_attn_fbdt, L0_attn_bA_log, L0_attn_bD, L0_attn_bWx, L0_attn_bWdt, L0_attn_bbdt)
    x = x + _L0_xattn_ref(ctx_1024, _layernorm(x, axis=-1), L0_xattn_ln_m_g, L0_xattn_ln_m_b, L0_xattn_ln_l_g, L0_xattn_ln_l_b, L0_xattn_Wq, L0_xattn_Wkv, L0_xattn_Wout)
    x = x + _L0_ffn_ref(_layernorm(x, axis=-1), L0_ffn_router_w, L0_ffn_router_b, L0_ffn_sw1, L0_ffn_sb1, L0_ffn_sw2, L0_ffn_sb2, L0_ffn_rw1, L0_ffn_rb1, L0_ffn_rw2, L0_ffn_rb2)
    x = x + _L1_attn_ref(_layernorm(x, axis=-1), L1_attn_w_qkv, L1_attn_w_pre, L1_attn_w_post, L1_attn_w_out, L1_attn_b_out)
    x = x + _L1_xattn_ref(_layernorm(x, axis=-1), ctx_1024, ctx_1024, fside_Bx16xSxS2_0, fside_Bx16xSxS2_0, mask_BxS2_bf0, fside_SxS2_0, L1_xattn_Wq, L1_xattn_bq, L1_xattn_Wk, L1_xattn_bk, L1_xattn_Wv, L1_xattn_bv, L1_xattn_Wo, L1_xattn_bo)
    x = x + _L1_ffn_ref(_layernorm(x, axis=-1), L1_ffn_Wq, L1_ffn_bq, L1_ffn_Wk, L1_ffn_bk, L1_ffn_Wv, L1_ffn_bv, L1_ffn_Wg1, L1_ffn_bg1, L1_ffn_Wg2, L1_ffn_bg2, L1_ffn_Wo, L1_ffn_bo)
    x = x + _L2_attn_ref(_layernorm(x, axis=-1), L2_attn_Wq, L2_attn_Wk, L2_attn_Wv, L2_attn_Wo)
    x = x + _L2_xattn_ref(ctx_1024, _layernorm(x, axis=-1), mask_BxS2_bk0, L2_xattn_ln_x_g, L2_xattn_ln_x_b, L2_xattn_ln_l_g, L2_xattn_ln_l_b, L2_xattn_q_gamma, L2_xattn_k_gamma, L2_xattn_W_q, L2_xattn_W_kv, L2_xattn_W_out, L2_xattn_b_out)
    x = x + _L2_ffn_ref(_layernorm(x, axis=-1), L2_ffn_k0, L2_ffn_k1, L2_ffn_k2, L2_ffn_s0, L2_ffn_s1, L2_ffn_s2)
    x = x + _L3_attn_ref(_layernorm(x, axis=-1), L3_attn_g1, L3_attn_g2, L3_attn_W_lin, L3_attn_b_lin, L3_attn_W_conv, L3_attn_b_conv, L3_attn_W_lin2, L3_attn_b_lin2, L3_attn_Wa, L3_attn_ba, L3_attn_Wx, L3_attn_bx, L3_attn_Lam, L3_attn_W1, L3_attn_b1, L3_attn_W2, L3_attn_b2, L3_attn_W3, L3_attn_b3)
    x = x + _L3_xattn_ref(_layernorm(x, axis=-1), ctx_1024, L3_xattn_wq, L3_xattn_wk, L3_xattn_wv, L3_xattn_wo, L3_xattn_bo)
    x = x + _L3_ffn_ref(_layernorm(x, axis=-1), L3_ffn_w_up, L3_ffn_w_down)
    return x

_drawn_inputs = setup_inputs


def setup_inputs(seed=0):
    import zlib

    import numpy as np

    out = dict(_drawn_inputs(seed))
    spreads = {'L0_attn_b_conv': (0.0, 0.1),
     'L0_attn_fD': (1.0, 0.2),
     'L0_attn_bD': (1.0, 0.2),
     'L0_xattn_ln_m_g': (1.0, 0.2),
     'L0_xattn_ln_m_b': (0.0, 0.1),
     'L0_xattn_ln_l_g': (1.0, 0.2),
     'L0_xattn_ln_l_b': (0.0, 0.1),
     'L0_ffn_router_b': (0.0, 0.1),
     'L0_ffn_sb1': (0.0, 0.1),
     'L0_ffn_sb2': (0.0, 0.1),
     'L0_ffn_rb1': (0.0, 0.1),
     'L0_ffn_rb2': (0.0, 0.1),
     'L1_xattn_bq': (0.0, 0.1),
     'L1_xattn_bk': (0.0, 0.1),
     'L1_xattn_bv': (0.0, 0.1),
     'L1_xattn_bo': (0.0, 0.1),
     'L1_ffn_bq': (0.0, 0.1),
     'L1_ffn_bk': (0.0, 0.1),
     'L1_ffn_bv': (0.0, 0.1),
     'L1_ffn_bg1': (0.0, 0.1),
     'L1_ffn_bg2': (0.0, 0.1),
     'L1_ffn_bo': (0.0, 0.1),
     'L2_xattn_ln_x_g': (1.0, 0.2),
     'L2_xattn_ln_x_b': (0.0, 0.1),
     'L2_xattn_ln_l_g': (1.0, 0.2),
     'L2_xattn_ln_l_b': (0.0, 0.1),
     'L2_xattn_q_gamma': (1.0, 0.2),
     'L2_xattn_k_gamma': (1.0, 0.2),
     'L2_xattn_b_out': (0.0, 0.1),
     'L3_attn_g1': (1.0, 0.2),
     'L3_attn_g2': (1.0, 0.2),
     'L3_attn_b_lin': (0.0, 0.1),
     'L3_attn_b_conv': (0.0, 0.1),
     'L3_attn_b_lin2': (0.0, 0.1),
     'L3_attn_ba': (0.0, 0.1),
     'L3_attn_bx': (0.0, 0.1),
     'L3_attn_b1': (0.0, 0.1),
     'L3_attn_b2': (0.0, 0.1),
     'L3_attn_b3': (0.0, 0.1),
     'L3_xattn_bo': (0.0, 0.1)}
    factors = {}
    for name, (base, spread) in spreads.items():
        noise = np.random.default_rng([zlib.crc32(name.encode()), seed]).standard_normal(out[name].shape)
        drawn = base * np.exp(spread * noise) if base else spread * noise
        out[name] = jnp.asarray(drawn.astype(out[name].dtype))
    for name, factor in factors.items():
        out[name] = (out[name] * factor).astype(out[name].dtype)
    return out
```

```python
from contextlib import ExitStack

import concourse.bass as bass
import numpy as np
from concourse import mybir

LAYERS = [0, 1, 2, 3, 4, 5, 6, 7, 8, 9, 10, 11]

P = 128
NB = 8
S = 256
D = 256
NT = 16
S2 = 77
WREG = 8448
F32 = mybir.dt.float32
BF16 = mybir.dt.bfloat16
U8 = mybir.dt.uint8
ALU = mybir.AluOpType
ACT = mybir.ActivationFunctionType
AX = mybir.AxisListType

SPEC = {
    0: [("Win", 2048), ("Wdt0", 512), ("Wdt1", 512), ("Wout", 1024), ("Wxd0", 256), ("Wxd1", 256),
        ("Wxb0", 384), ("Wxb1", 384), ("conv", 16), ("bconv", 4), ("D0", 4), ("D1", 4), ("bdt0", 4), ("bdt1", 4),
        ("A0", 64), ("A1", 64)],
    1: [("Wq", 2048), ("Wkv", 4096), ("Wout", 2048), ("mg", 2), ("mb", 2), ("lg", 2), ("lb", 2)],
    2: [("rw", 16), ("rb", 8), ("b1", 36), ("b2", 256)],
    3: [("Wqk", 1024), ("Wv", 512), ("Wout", 512), ("wpre", 32), ("wpost", 256), ("bo", 256)],
    4: [("Wq", 512), ("Wk", 512), ("Wv", 512), ("Wo", 512), ("bq", 2), ("bk", 2), ("bv", 256), ("bo", 256),
        ("am", 154)],
    5: [("We", 6144), ("Wo", 512), ("Wg1", 256), ("Wg2", 4), ("bg1", 1), ("bg2", 4), ("bqk", 16), ("bv", 1024),
        ("bo", 256)],
    6: [("Wqk", 1024), ("Wv", 512), ("Wo", 512), ("dist", 384), ("gsel", 128), ("gmask", 256)],
    7: [("Wqk", 1024), ("Wv", 512), ("Wo", 512), ("xg", 2), ("xb", 2), ("lg", 2), ("lb", 2), ("gq", 1), ("gk", 1),
        ("bo", 256)],
    8: [],
    9: [("lin", 512), ("conv", 512), ("a", 512), ("x", 512), ("lin2", 512), ("w1", 512), ("w2", 512), ("w3", 512),
        ("blin", 2), ("bconv", 2), ("ba", 2), ("bx", 2), ("b1", 2), ("b2", 2), ("blin2", 256), ("b3", 256),
        ("g1", 2), ("g2", 2), ("lam", 2)],
    10: [("wq", 2048), ("wk", 2048), ("wv", 2048), ("wo", 2048), ("bo", 256)],
    11: [("up", 2048), ("down", 2048)],
}
CONST = [("ident", 128), ("sel", 32), ("hm", 8), ("cos", 32), ("sin", 32), ("jgt", 64), ("one", 128)]


def offsets(spec):
    at, out = 0, {}
    for name, n in spec:
        out[name] = (at, n)
        at += n
    return out, at


class Line:

    def __init__(self, sem):
        self.sem, self.n, self.items, self.seen = sem, 0, [], {}

    def wait(self, toks):
        for t in toks:
            if t is None or t == ():
                continue
            if isinstance(t, list):
                self.wait(t)
                continue
            sem, value = t
            if self.seen.get(id(sem), 0) < value:
                self.seen[id(sem)] = value
                self.items.append((sem, value))

    def __call__(self, f, *args, w=(), sig=True, **kw):
        self.wait(list(w))
        self.n += 1 if sig else 0
        self.items.append((f, args, kw, self.sem if sig else None, 1))
        return (self.sem, self.n)

    def now(self):
        return (self.sem, self.n)

    def play(self, eng):
        for it in self.items:
            if len(it) == 2:
                eng.wait_ge(it[0], it[1])
                continue
            f, args, kw, sem, by = it
            ins = f(*args, **kw)
            if sem is not None:
                ins.then_inc(sem, by)


class Buf:
    def __init__(self, ap):
        self.ap, self.w = ap, []


class Ring:

    def __init__(self, aps):
        self.free = [Buf(a) for a in aps]

    def take(self):
        return self.free.pop(0)

    def give(self, b, *toks):
        b.w = list(toks)
        self.free.append(b)


def build(nc, A, out):
    ctx = ExitStack()
    with ctx:
        def sb(name, n, dt=F32):
            return ctx.enter_context(nc.sbuf_tensor(name, [P, n], dt))

        pe, act, dve, pool, sp = [Line(ctx.enter_context(nc.semaphore("s_" + n)))
                                  for n in ("pe", "act", "dve", "pool", "sp")]
        T, V, C, G = nc.tensor, nc.vector, nc.scalar, nc.gpsimd

        dsem = [ctx.enter_context(nc.semaphore(f"dma{i}")) for i in range(32)]
        dcount = [0]

        def dma(dst, src, w=()):
            i = dcount[0]
            dcount[0] += 1
            sem, k = dsem[i % 32], i // 32
            sp.wait([(sem, 16 * k)] if k else [])
            sp.wait(list(w))
            sp.items.append((nc.sync.dma_start, (dst, src), {}, sem, 16))
            return (sem, 16 * (k + 1))

        X = sb("X", NT * D)[:, :].rearrange("p (t d) -> p t d", t=NT)
        xnT = sb("xnT", 2 * 2048)[:, :].rearrange("p (k n) -> p k n", k=2)
        XNr = sb("XNr", 2 * 1024)
        stat = sb("stat", 2 * 64)
        Wr = [sb("W0", WREG), sb("W1", WREG)]
        coff, cw = offsets(CONST)
        cst = sb("cst", cw)
        ctxT = sb("ctxT", 2 * 616)[:, :].rearrange("p (k n) -> p k n", k=2)
        cnT = sb("cnT", 2 * 616)[:, :].rearrange("p (k n) -> p k n", k=2)
        NSCR = 23040
        scr = sb("scr", NSCR)
        PS = ctx.enter_context(nc.psum_tensor("PS", [P, 8, 512], F32))
        ps = Ring([PS[:, i, :] for i in range(8)])
        xn_ring = Ring([XNr[:, i * 1024:(i + 1) * 1024].rearrange("p (t d) -> p t d", t=4) for i in range(2)])
        st_ring = Ring([stat[:, i * 64:(i + 1) * 64] for i in range(2)])

        def K(name, rows=P):
            o, n = coff[name]
            return cst[0:rows, o:o + n]

        ident = K("ident")
        ones = K("one")

        class Arena:
            def __init__(self, segs):
                self.segs = list(segs)

            def get(self, n):
                for i, (t, lo, hi) in enumerate(self.segs):
                    if hi - lo >= n:
                        self.segs[i] = (t, lo + n, hi)
                        return t[:, lo:lo + n]
                raise ValueError(f"arena: {n} of {[(b - a) for _, a, b in self.segs]}")

            def ring(self, n, count):
                return Ring([self.get(n) for _ in range(count)])

        c_tok = dma(cst[:, :], A["const"])
        xv = A["x"].rearrange("b (h p) d -> p (b h) d", p=P)
        xtok = [None] * NT
        for c in range(4):
            t = dma(X[:, 4 * c:4 * c + 4, :], xv[:, 4 * c:4 * c + 4, :])
            for j in range(4):
                xtok[4 * c + j] = t

        bars = []

        def barrier():
            toks = [e.now() for e in (pe, act, dve, pool) if e.n]
            for e in (pe, act, dve, pool):
                e.wait(toks)
            bars.append(toks)
            return toks

        wtok = {}

        def load_weights(n, w):
            off, width = offsets(SPEC[n])
            if width:
                wtok[n] = dma(Wr[order[n] % 2][:, 0:width], A[f"w{n}"], w)

        order = {n: i for i, n in enumerate(LAYERS)}

        def W(n, name, rows=P):
            off, _ = offsets(SPEC[n])
            o, k = off[name]
            return Wr[order[n] % 2][0:rows, o:o + k]

        def Wk(n, name, kt):
            return W(n, name).rearrange("p (k f) -> p k f", k=kt)

        def mm(o, pairs, w=(), first=True, last=True, sig=True):
            for i, (l, r) in enumerate(pairs):
                t = pe(T.matmul, o, l, r, start=(first and i == 0), stop=(last and i == len(pairs) - 1),
                       w=w if i == 0 else (), sig=sig and i == len(pairs) - 1)
            return t

        flip = [0]

        def copy(o, i, w=(), on=None):
            if on is None:
                flip[0] ^= 1
                on = act if flip[0] else dve
            if on is act:
                return act(C.activation, o, i, ACT.Copy, w=w)
            return on(V.tensor_copy, o, i, w=w)

        cz = sb("cz", 8)
        z_tok = dve(V.memset, cz[:, 0:1], 1e-5)
        z_tok = dve(V.memset, cz[:, 1:2], 1.0)
        eps_ap = cz[:, 0:1]
        one_ap = cz[:, 1:2]

        def normalise_steps(dst, src, n, rows, kind, w, st, tile_w=None):
            mv = st.ap[0:rows, 0:2 * n].rearrange("p (t s) -> p t s", s=2)
            bs = st.ap[0:rows, 8:8 + 6 * n].rearrange("p (t s) -> p t s", s=6)
            sd = st.ap[0:rows, 40:40 + n]
            rs = st.ap[0:rows, 48:48 + n]
            ms = st.ap[0:rows, 56:56 + n]
            for j in range(n):
                wj = w if tile_w is None else [w, tile_w[j]]
                t = dve(V.bn_stats, bs[:, j, :], src[:, j, :], w=[st.w, wj])
            for j in range(n):
                t = dve(V.bn_aggr, mv[:, j, :], bs[:, j, :], w=[t])
            yield None
            if kind == "ln":
                t = act(C.activation, sd, mv[:, :, 1], ACT.Sqrt, bias=eps_ap[0:rows], w=[t, z_tok])
                yield None
                t = dve(V.reciprocal, rs, sd, w=[t])
                for j in range(n):
                    t = dve(V.tensor_scalar, dst[:, j, :], src[:, j, :], mv[:, j, 0:1], rs[:, j:j + 1],
                            ALU.subtract, ALU.mult, w=[t])
            else:
                t = dve(V.tensor_tensor, ms, mv[:, :, 0], mv[:, :, 0], ALU.mult, w=[t])
                t = dve(V.tensor_tensor, ms, ms, mv[:, :, 1], ALU.add, w=[t])
                yield None
                if kind == "rms16":
                    t = act(C.activation, sd, ms, ACT.Sqrt, scale=256.0, w=[t])
                    yield None
                    t = dve(V.tensor_scalar, sd, sd, 1e-12, 0.0625, ALU.max, ALU.mult, w=[t])
                else:
                    t = act(C.activation, sd, ms, ACT.Sqrt, w=[t])
                    yield None
                    t = dve(V.tensor_scalar, sd, sd, 1e-8, None, ALU.add, w=[t])
                t = dve(V.reciprocal, rs, sd, w=[t])
                for j in range(n):
                    t = dve(V.tensor_scalar, dst[:, j, :], src[:, j, :], rs[:, j:j + 1], None, ALU.mult, w=[t])
            yield t

        def normalise(*args):
            for t in normalise_steps(*args):
                pass
            return t

        def norm_steps(c, toks, kinds, g=None, b=None, w=(), source=None):
            xb, st = xn_ring.take(), st_ring.take()
            src, t = X[:, 4 * c:4 * c + 4, :], [xb.w, w]
            tw = xtok[4 * c:4 * c + 4]
            if source is not None:
                src, tw = source
            for kind in kinds:
                for r in normalise_steps(xb.ap, src, 4, P, kind, [t], st, tw):
                    yield
                t = r
                src, tw = xb.ap, None
            st_ring.give(st, t)
            for k in range(2):
                bank = ps.take()
                for j in range(4):
                    tt = pe(T.transpose, bank.ap[:, j * P:(j + 1) * P], xb.ap[:, j, k * P:(k + 1) * P], ident,
                            w=[t, bank.w, c_tok], sig=j == 3)
                o = xnT[:, k, c * 512:(c + 1) * 512]
                if g is not None:
                    e = act(C.activation, o, bank.ap, ACT.Identity, scale=g[:, k:k + 1],
                            bias=b[:, k:k + 1] if b is not None else 0.0, w=[tt, w])
                else:
                    e = copy(o, bank.ap, w=[tt])
                ps.give(bank, e)
                toks.append(e)
            xn_ring.give(xb, tt)

        def norm_chunk(c, kinds, **kw):
            toks = []
            for _ in norm_steps(c, toks, kinds, **kw):
                pass
            return toks

        NORM = {1: (["ln", "ln"], "lg", "lb"), 7: (["ln", "ln"], "lg", "lb"), 11: (["ln", "rms"],)}
        ahead = {}
        running = []

        def start_norm(n, c):
            kinds, *gb = NORM.get(n, (["ln"],))
            toks = []
            kw = dict(g=W(n, gb[0]), b=W(n, gb[1]), w=[wtok[n]]) if gb else {}
            running.append(norm_steps(c, toks, kinds, **kw))
            ahead[(n, c)] = toks

        def poll():
            for g in list(running):
                if next(g, "end") == "end":
                    running.remove(g)

        def finished(n, c):
            i = order[n] + 1
            if i < len(LAYERS) and LAYERS[i] != 9:
                while len(running) >= 2:
                    poll()
                start_norm(LAYERS[i], c)

        def inputs_of(n):
            for c in range(4):
                if (n, c) not in ahead:
                    while len(running) >= 2:
                        poll()
                    start_norm(n, c)
                    if c % 2:
                        while running:
                            poll()
            while running:
                poll()
            return [ahead[(n, c)] for c in range(4)]

        def to_x(t, yT, kt, Wo, w, bias=None, scale=None, onto=None):
            bank = ps.take()
            pairs = [(yT(k), Wo[:, k, :]) for k in range(kt)]
            if bias is not None:
                pairs.append((ones[0:1, :], bias))
            m = mm(bank.ap[:, 0:D], pairs, w=[w, bank.w])
            if onto is not None:
                e = dve(V.tensor_tensor, onto[0], onto[0], bank.ap[:, 0:D], ALU.add, w=[m, onto[1]])
                ps.give(bank, e)
                return e
            if scale is None:
                xtok[t] = dve(V.tensor_tensor, X[:, t, :], X[:, t, :], bank.ap[:, 0:D], ALU.add, w=[m, xtok[t]])
            else:
                xtok[t] = dve(V.scalar_tensor_tensor, X[:, t, :], bank.ap[:, 0:D], scale, X[:, t, :], ALU.mult,
                              ALU.add, w=[m, xtok[t]])
            ps.give(bank, xtok[t])
            return m

        env = dict(nc=nc, T=T, V=V, C=C, G=G, pe=pe, act=act, dve=dve, pool=pool, dma=dma, X=X, xnT=xnT, ps=ps, A=A,
                   K=K, ident=ident, ones=ones, Arena=Arena, W=W, Wk=Wk, mm=mm, copy=copy, one_ap=one_ap,
                   eps_ap=eps_ap, z_tok=z_tok, normalise=normalise, norm_chunk=norm_chunk, to_x=to_x, xtok=xtok,
                   wtok=wtok, scr=scr, NSCR=NSCR, Wr=Wr, order=order, c_tok=c_tok, ctxT=ctxT, cnT=cnT,
                   barrier=barrier, XNr=XNr, poll=poll, finished=finished, inputs_of=inputs_of, st_ring=st_ring, xn_ring=xn_ring, PS=PS, bars=bars)
        env["ctx_tok"] = None
        if any(n in LAYERS for n in (1, 4, 7, 10)):
            env["ctx_tok"] = load_context(env)
        load_weights(LAYERS[0], [])
        for i, n in enumerate(LAYERS):
            b = barrier()
            if i + 1 < len(LAYERS):
                load_weights(LAYERS[i + 1], b)
            SUB[n](env, n)
        dones = []
        for c in range(4):
            ov = out.rearrange("b (h p) d -> p (b h) d", p=P)
            dones.append(dma(ov[:, 4 * c:4 * c + 4, :], X[:, 4 * c:4 * c + 4, :], xtok[4 * c:4 * c + 4]))
        sp.wait(dones)
        for i, s in enumerate(dsem):
            n = (dcount[0] - i + 31) // 32
            if n > 0:
                sp.wait([(s, 16 * n)])
        block = ctx.enter_context(nc.Block())
        block.sync(lambda e: sp.play(e))
        block.tensor(lambda e: pe.play(e))
        block.scalar(lambda e: act.play(e))
        block.vector(lambda e: dve.play(e))
        block.gpsimd(lambda e: pool.play(e))


def load_context(E):
    pe, T, V, dve, ps, dma = E["pe"], E["T"], E["V"], E["dve"], E["ps"], E["dma"]
    ar = E["Arena"]([(E["scr"], 0, E["NSCR"])])
    raw = ar.get(8 * D).rearrange("p (t d) -> p t d", t=8)
    nrm = ar.get(8 * D).rearrange("p (t d) -> p t d", t=8)
    ld = dma(raw[0:S2, :, :], E["A"]["ctx"].rearrange("b s d -> s b d"))
    st = E["st_ring"].take()
    toks = []
    t = []
    for h in range(2):
        t = E["normalise"](nrm[0:S2, 4 * h:4 * h + 4, :], raw[0:S2, 4 * h:4 * h + 4, :], 4, S2, "ln", [ld, t], st)
    E["st_ring"].give(st, t)
    for src, dst, w in ((raw, E["ctxT"], ld), (nrm, E["cnT"], t)):
        for k in range(2):
            for h in range(2):
                bank = ps.take()
                for j in range(4):
                    m = pe(T.transpose, bank.ap[:, j * S2:(j + 1) * S2], src[0:S2, 4 * h + j, k * P:(k + 1) * P],
                           E["ident"][0:S2, 0:S2], w=[w, bank.w, E["c_tok"]], sig=j == 3)
                e = E["copy"](dst[:, k, 4 * h * S2:4 * (h + 1) * S2], bank.ap[:, 0:4 * S2], w=[m])
                ps.give(bank, e)
                toks.append(e)
    return toks


def ternary(E, n):
    pe, act, dve, pool, T, V, C, ps = E["pe"], E["act"], E["dve"], E["pool"], E["T"], E["V"], E["C"], E["ps"]
    mm, X, xnT, wt = E["mm"], E["X"], E["xnT"], E["wtok"][n]
    ar = E["Arena"]([(E["scr"], 0, E["NSCR"])])
    small = ar.get(16)
    tmp = [ar.get(2048) for _ in range(3)]
    ready = []
    t = None
    for m, name in enumerate(("up", "down")):
        w = E["W"](n, name)
        q = dve(V.tensor_reduce, tmp[0][:, 0:64], w.rearrange("p (a b) -> p a b", a=64), AX.X, ALU.add,
                apply_absolute_value=True, w=[wt, t])
        q = dve(V.tensor_reduce, small[:, m:m + 1], tmp[0][:, 0:64], AX.X, ALU.add, w=[q])
        bank = ps.take()
        q = mm(bank.ap[:, 0:1], [(E["ones"], small[:, m:m + 1])], w=[q, bank.w])
        th = small[:, 4 + m:5 + m]
        q = dve(V.tensor_scalar, th, bank.ap[:, 0:1], 0.5 / (1024 * 256), None, ALU.mult, w=[q])
        ps.give(bank, q)
        a, s, g = tmp
        q1 = act(C.activation, a, w, ACT.Abs, w=[wt, t, q])
        q2 = act(C.activation, s, w, ACT.Sign, w=[wt, t])
        q = dve(V.scalar_tensor_tensor, g, a, th, s, ALU.is_gt, ALU.mult, w=[q, q1, q2, t])
        q = dve(V.tensor_tensor, g, g, w, ALU.subtract, w=[q])
        t = dve(V.tensor_tensor, w, w, g, ALU.add, w=[q])
        ready.append(t)
    up = E["Wk"](n, "up", 2)
    down = E["Wk"](n, "down", 8)
    hs = ar.ring(4096, 2)
    sq = ar.ring(4096, 1)
    prev = None

    def second(c, hb, ht):
        h = hb.ap.rearrange("p (f n) -> p f n", f=8)
        qb = sq.take()
        q = qb.ap.rearrange("p (f n) -> p f n", f=8)
        qt = pool(E["G"].tensor_tensor, qb.ap, hb.ap, hb.ap, ALU.mult, w=[ht, qb.w])
        for j in range(4):
            tl = 4 * c + j
            bank = ps.take()
            s1 = mm(bank.ap[:, 0:D], [(h[:, k, j * P:(j + 1) * P], down[:, k, :]) for k in range(8)],
                    w=[bank.w, ht, ready[1]])
            s2 = mm(bank.ap[:, 256:257], [(q[:, k, j * P:(j + 1) * P], E["ones"][:, 0:1]) for k in range(8)], w=[qt])
            r = small[:, 8 + 2 * (tl % 2):9 + 2 * (tl % 2)]
            r2 = small[:, 9 + 2 * (tl % 2):10 + 2 * (tl % 2)]
            u = act(C.activation, r, bank.ap[:, 256:257], ACT.Sqrt, scale=1.0 / 1024, w=[s2, E["xtok"][tl - 2]])
            u = dve(V.tensor_scalar, r, r, 1e-8, None, ALU.add, w=[u])
            u = dve(V.reciprocal, r2, r, w=[u])
            E["xtok"][tl] = dve(V.scalar_tensor_tensor, X[:, tl, :], bank.ap[:, 0:D], r2, X[:, tl, :], ALU.mult,
                                ALU.add, w=[u, s1, E["xtok"][tl]])
            ps.give(bank, E["xtok"][tl])
        sq.give(qb, s2)
        hs.give(hb, s1, qt)

    xts = E["inputs_of"](n)
    for c in range(4):
        xt = xts[c]
        hb = hs.take()
        h = hb.ap.rearrange("p (f n) -> p f n", f=8)
        for f in range(8):
            bank = ps.take()
            m = mm(bank.ap, [(up[:, k, f * P:(f + 1) * P], xnT[:, k, c * 512:(c + 1) * 512]) for k in range(2)],
                   w=[bank.w, xt, ready[0]])
            ht = act(C.activation, h[:, f, :], bank.ap, ACT.Gelu, w=[m, hb.w])
            ps.give(bank, ht)
        if prev:
            second(*prev)
        prev = (c, hb, ht)
    second(*prev)


def signs(E, n):
    pe, act, dve, pool, T, V, C, G, ps = [E[k] for k in ("pe", "act", "dve", "pool", "T", "V", "C", "G", "ps")]
    mm, X, xnT, A, dma = E["mm"], E["X"], E["xnT"], E["A"], E["dma"]
    reg = E["Wr"][E["order"][n] % 2]
    ar = E["Arena"]([(E["scr"], 0, E["NSCR"]), (reg, 0, WREG)])
    sc = ar.get(8)
    w1 = ar.get(8192)
    hr = ar.ring(4096, 2)
    raw0, w0 = ar.get(1024), ar.get(2048)
    w2 = ar.get(2048)
    raw1, raw2 = ar.get(2048), ar.get(512)
    bar = E["bars"][-1]
    t0 = dma(raw0.bitcast(U8), A["k0"], bar)
    t1 = dma(raw1.bitcast(U8), A["k1"], bar)
    t2 = dma(raw2.bitcast(U8), A["k2"], bar)
    ts = dma(sc[:, 0:3], A["s"], bar)
    k0 = raw0.bitcast(U8).rearrange("p (h n) -> p h n", h=2)
    q = dve(V.tensor_tensor, w0, k0[:, 0, :], k0[:, 1, :], ALU.subtract, w=[t0])
    r0 = dve(V.tensor_scalar, w0, w0, 2.0, None, ALU.mult, w=[q])
    r1 = dve(V.tensor_scalar, w1, raw1.bitcast(U8), 2.0, -1.0, ALU.mult, ALU.add, w=[t1])
    r2 = dve(V.tensor_scalar, w2, raw2.bitcast(U8), 2.0, -1.0, ALU.mult, ALU.add, w=[t2])
    rs = dve(V.tensor_scalar, sc[:, 4:6], sc[:, 0:2], 2.0, None, ALU.mult, w=[ts])
    w0, w1, w2 = [a.rearrange("p (k f) -> p k f", k=k) for a, k in ((w0, 2), (w1, 8), (w2, 8))]

    def relu(o, bank, s, w, f):
        if f % 2:
            return act(C.activation, o, bank.ap, ACT.Relu, scale=sc[:, 4 + s:5 + s], w=w)
        return dve(V.tensor_scalar, o, bank.ap, sc[:, 4 + s:5 + s], 0.0, ALU.mult, ALU.max, w=w)

    xts = E["inputs_of"](n)
    for c in range(4):
        E["poll"]()
        xt = xts[c]
        cur, ht = None, xt
        for s, (wm, kt) in enumerate(((w0, 2), (w1, 8))):
            hb = hr.take()
            h = hb.ap.rearrange("p (f n) -> p f n", f=8)
            es = []
            for f in range(8):
                E["poll"]()
                bank = ps.take()
                m = mm(bank.ap, [(wm[:, k, f * P:(f + 1) * P],
                                  xnT[:, k, c * 512:(c + 1) * 512] if s == 0 else cur[:, k, :]) for k in range(kt)],
                       w=[bank.w, ht, r0, r1])
                e = relu(h[:, f, :], bank, s, [m, hb.w, rs], f)
                ps.give(bank, e)
                es.append(e)
            if s:
                hr.give(pb, m)
            pb, cur, ht = hb, h, es
        for j in range(4):
            m = E["to_x"](4 * c + j, lambda k: cur[:, k, j * P:(j + 1) * P], 8, w2, [ht, r2], scale=sc[:, 2:3])
        hr.give(pb, m)
        E["finished"](n, c)


def experts(E, n):
    pe, act, dve, pool, T, V, C, G, ps = [E[k] for k in ("pe", "act", "dve", "pool", "T", "V", "C", "G", "ps")]
    mm, X, xnT, A, dma, W = E["mm"], E["X"], E["xnT"], E["A"], E["dma"], E["W"]
    reg = E["Wr"][E["order"][n] % 2]
    _, width = offsets(SPEC[n])
    ar = E["Arena"]([(E["scr"], 0, E["NSCR"]), (reg, width, WREG)])
    ring = ar.ring(2048, 4)
    hr = ar.ring(2048, 2)
    bar = E["bars"][-1]
    wt = E["wtok"][n]
    lg = ar.get(NT * 8).rearrange("p (t e) -> p t e", e=8)
    pr = ar.get(NT * 8).rearrange("p (t e) -> p t e", e=8)
    wg = ar.get(NT * 9).rearrange("p (t e) -> p t e", e=9)
    mx = ar.get(NT)
    sm = ar.get(NT)
    cmp1, cmp2 = ar.get(512), ar.get(512)
    wT = ar.get(2048)
    slots = []

    def load(e):
        b = ring.take()
        slots.append((b, dma(b.ap, A["we"][e], [bar, b.w])))

    for e in range(3):
        load(e)
    rw = W(n, "rw").rearrange("p (k e) -> p k e", k=2)
    xts = E["inputs_of"](n)
    bank = ps.take()
    for t in range(NT):
        m = mm(bank.ap[:, t * 8:t * 8 + 8], [(xnT[:, k, t * P:(t + 1) * P], rw[:, k, :]) for k in range(2)]
               + [(E["ones"][0:1, :], W(n, "rb")[0:1, :])], w=[bank.w, xts[t // 4], wt])
    lv = bank.ap[:, 0:128].rearrange("p (t e) -> p t e", e=8)
    t = dve(V.tensor_reduce, mx, lv, AX.X, ALU.max, w=[m])
    t = dve(V.tensor_tensor, lg, lv, mx.unsqueeze(2).to_broadcast([P, NT, 8]), ALU.subtract, w=[t])
    ps.give(bank, t)
    t = act(C.activation, pr, lg, ACT.Exp, w=[t])
    t = dve(V.tensor_reduce, sm, pr, AX.X, ALU.add, w=[t])
    t = dve(V.reciprocal, mx, sm, w=[t])
    t = dve(V.tensor_tensor, pr, pr, mx.unsqueeze(2).to_broadcast([P, NT, 8]), ALU.mult, w=[t])
    jgt = E["K"]("jgt").rearrange("p (e j) -> p e j", e=8)
    rk = ar.get(NT * 8).rearrange("p (t e) -> p t e", e=8)
    for g in range(2):
        c1 = cmp1.rearrange("p (t e) -> p t e", t=8)
        c2 = cmp2.rearrange("p (t e) -> p t e", t=8)
        pv = pr[:, 8 * g:8 * g + 8, :]
        for e in range(8):
            me = pv[:, :, e:e + 1].to_broadcast([P, 8, 8])
            a1, a2 = c1[:, :, 0:8], c2[:, :, 0:8]
            q = dve(V.tensor_tensor, a1, pv, me, ALU.is_gt, w=[t])
            q = dve(V.tensor_tensor, a2, pv, me, ALU.is_equal, w=[q, t])
            q = dve(V.tensor_tensor, a2, a2, jgt[:, e, :].unsqueeze(1).to_broadcast([P, 8, 8]), ALU.mult, w=[q])
            q = dve(V.tensor_tensor, a1, a1, a2, ALU.add, w=[q])
            t = dve(V.tensor_reduce, rk[:, 8 * g:8 * g + 8, e], a1, AX.X, ALU.add, w=[q])
    t1 = dve(V.memset, wg[:, :, 8:9], 1.0)
    t = dve(V.scalar_tensor_tensor, wg[:, :, 0:8], rk, 1.5, pr, ALU.is_lt, ALU.mult, w=[t])
    for g in range(4):
        bank = ps.take()
        for j in range(4):
            m = pe(T.transpose, bank.ap[0:9, j * P:(j + 1) * P], wg[:, 4 * g + j, :], E["ident"], w=[t, t1, bank.w],
                   sig=j == 3)
        wtt = dve(V.tensor_copy, wT[0:9, g * 512:(g + 1) * 512], bank.ap[0:9, :], w=[m])
        ps.give(bank, wtt)
    b1 = W(n, "b1")

    def second(e, c, hb, ht, w2):
        h = hb.ap.rearrange("p (f n) -> p f n", f=4)
        for j in range(4):
            tl = 4 * c + j
            if e < 8:
                m = E["to_x"](tl, lambda k: h[:, k, j * P:(j + 1) * P], 4, w2, [ht, t], scale=wg[:, tl, e:e + 1])
            else:
                b = ps.take()
                b2 = W(n, "b2")
                m = mm(b.ap[:, 0:D], [(h[:, k, j * P:(j + 1) * P], w2[:, k, :]) for k in range(4)]
                       + [(wT[0:9, tl * P:(tl + 1) * P], b2[0:9, :])],
                       w=[ht, wtt, b.w])
                E["xtok"][tl] = dve(V.tensor_tensor, X[:, tl, :], X[:, tl, :], b.ap[:, 0:D], ALU.add,
                                    w=[m, E["xtok"][tl]])
                ps.give(b, E["xtok"][tl])
        hr.give(hb, m)
        if e == 8:
            E["finished"](n, c)
        return m

    prev = None
    for e in range(9):
        sb_, st = slots[e]
        w1 = sb_.ap[:, 0:1024].rearrange("p (k f) -> p k f", k=2)
        w2 = sb_.ap[:, 1024:2048].rearrange("p (k f) -> p k f", k=4)
        for c in range(4):
            hb = hr.take()
            h = hb.ap.rearrange("p (f n) -> p f n", f=4)
            for f in range(4):
                E["poll"]()
                bank = ps.take()
                m = mm(bank.ap, [(w1[:, k, f * P:(f + 1) * P], xnT[:, k, c * 512:(c + 1) * 512]) for k in range(2)],
                       w=[bank.w, st, xts[c]])
                ht = act(C.activation, h[:, f, :], bank.ap, ACT.Gelu, bias=b1[:, 4 * e + f:4 * e + f + 1],
                         w=[m, hb.w])
                ps.give(bank, ht)
            if prev:
                m2 = second(*prev)
                if c == 0:
                    ring.give(slots[e - 1][0], m2)
                    if e + 2 < 9:
                        load(e + 2)
            prev = (e, c, hb, ht, w2)
    second(*prev)


def pipe(E, n, *stages):
    for s in range(n + max(l for l, _ in stages)):
        E["poll"]()
        for lag, f in stages:
            if 0 <= s - lag < n:
                f(s - lag)


def turn(E, bank, srcs, w):
    pe, T = E["pe"], E["T"]
    for i, (c, s, r, m) in enumerate(srcs):
        t = pe(T.transpose, bank.ap[0:m, c:c + r], s, E["ident"][0:r, 0:r], w=[w, bank.w], sig=i == len(srcs) - 1)
    return t


def finish_heads(E, n, b, Osb, ot_ring, Wo, bo, w, osb_give):
    inner = Osb.shape[2]
    kt = inner // P
    ob = ot_ring.take()
    ot = ob.ap.rearrange("p (k n) -> p k n", k=kt)
    toks = []
    for k in range(0, kt, 2):
        bank = E["ps"].take()
        m = turn(E, bank, [((kk * 2 + it) * P, Osb[:, it, (k + kk) * P:(k + kk + 1) * P], P, P)
                           for kk in range(2) for it in range(2)], w)
        e = E["copy"](ob.ap[:, k * S:(k + 2) * S], bank.ap, w=[m, ob.w])
        E["ps"].give(bank, e)
        toks.append(e)
    osb_give(m)
    for it in range(2):
        m = E["to_x"](2 * b + it, lambda k: ot[:, k, it * P:(it + 1) * P], kt, Wo, [toks], bias=bo)
    ot_ring.give(ob, m)
    if b % 2:
        E["finished"](n, b // 2)


def get(E):
    return [E[k] for k in ("pe", "act", "dve", "pool", "T", "V", "C", "G", "ps", "mm", "X", "xnT", "W", "Wk", "copy")]


def rope_tile(E, t, Wqk, cos_it, bufs, w):
    pe, act, dve, pool, T, V, C, G, ps, mm, X, xnT, W, Wk, copy = get(E)
    it = t % 2
    bank = ps.take()
    m = mm(bank.ap, [(xnT[:, k, t * P:(t + 1) * P], Wqk[:, k, :]) for k in range(2)], w=[bank.w, w])
    rb, tb = bufs[0].take(), bufs[1].take()
    cos = E["K"]("cos")[:, 16 * it:16 * it + 16]
    sin = E["K"]("sin")[:, 16 * it:16 * it + 16]
    v = bank.ap.rearrange("p (h d) -> p h d", d=16)
    a = rb.ap.rearrange("p (h d) -> p h d", d=16)
    c = tb.ap.rearrange("p (h d) -> p h d", d=16)
    q1 = dve(V.tensor_tensor, a, v, cos.unsqueeze(1).to_broadcast([P, 32, 16]), ALU.mult, w=[m, rb.w])
    q2 = dve(V.tensor_tensor, c[:, :, 0:8], v[:, :, 8:16], sin[:, 0:8].unsqueeze(1).to_broadcast([P, 32, 8]),
             ALU.mult, w=[m, tb.w])
    q2 = dve(V.tensor_tensor, c[:, :, 8:16], v[:, :, 0:8], sin[:, 8:16].unsqueeze(1).to_broadcast([P, 32, 8]),
             ALU.mult, w=[m])
    ps.give(bank, q2)
    q = pool(G.tensor_tensor, rb.ap, rb.ap, tb.ap, ALU.add, w=[q1, q2])
    bufs[1].give(tb, q)
    bank = ps.take()
    m = turn(E, bank, [(j * P, rb.ap[:, j * P:(j + 1) * P], P, P) for j in range(4)], [q])
    bufs[0].give(rb, m)
    return bank, m


def talking(E, n):
    pe, act, dve, pool, T, V, C, G, ps, mm, X, xnT, W, Wk, copy = get(E)
    wt = E["wtok"][n]
    ar = E["Arena"]([(E["scr"], 0, E["NSCR"])])
    Wqk, Wv, Wo = Wk(n, "Wqk", 2), Wk(n, "Wv", 2), Wk(n, "Wout", 2)
    rbufs = (ar.ring(512, 2), ar.ring(512, 2))
    qr, kr, vr = ar.ring(512, 2), ar.ring(512, 2), ar.ring(512, 2)
    qg, pr, pt, vh = ar.ring(512, 3), ar.ring(512, 4), ar.ring(512, 3), ar.ring(512, 5)
    ot = ar.ring(512, 2)
    sm = ar.ring(8, 6)
    wpre = W(n, "wpre").rearrange("p (k g) -> p k g", k=2)
    wpost = W(n, "wpost")
    xts = E["inputs_of"](n)
    st = {}

    def pro(b):
        qb, kb, vb = qr.take(), kr.take(), vr.take()
        q, k, v = [z.ap.rearrange("p (k n) -> p k n", k=2) for z in (qb, kb, vb)]
        toks = []
        for it in range(2):
            t = 2 * b + it
            bank, m = rope_tile(E, t, Wqk, None, rbufs, [xts[b // 2], wt])
            bv = bank.ap.rearrange("p (j n) -> p j n", j=4)
            e1 = act(C.activation, q[:, :, it * P:(it + 1) * P], bv[:, 0:2, :], ACT.Copy, scale=0.25, w=[m, qb.w])
            e2 = act(C.activation, k[:, :, it * P:(it + 1) * P], bv[:, 2:4, :], ACT.Copy, w=[m, kb.w])
            ps.give(bank, e1, e2)
            bank = ps.take()
            m = mm(bank.ap[:, 0:D], [(xnT[:, k2, t * P:(t + 1) * P], Wv[:, k2, :]) for k2 in range(2)], w=[bank.w])
            e3 = copy(v[:, it, :], bank.ap[:, 0:D], w=[m, vb.w])
            ps.give(bank, e3)
            toks += [e1, e2, e3]
        st[b] = dict(q=q, k=k, v=v, bufs=(qb, kb, vb), t=toks)

    def s0(u):
        b, g = divmod(u, 16)
        if g == 0 and b == 0:
            pro(0)
        if g == 8 and b + 1 < NB:
            pro(b + 1)
        s = st[b]
        gb = qg.take()
        gv = gb.ap.rearrange("p (k n) -> p k n", k=2)
        for k in range(2):
            e = dve(V.tensor_scalar, gv[:, k, :], s["q"][:, k, :], wpre[:, k, g:g + 1], None, ALU.mult,
                    w=[s["t"], gb.w])
        vb = vh.take()
        ve = pool(G.tensor_tensor, vb.ap.rearrange("p (j g d) -> p j g d", j=2, g=16),
                  s["v"].rearrange("p j (g d) -> p j g d", g=16),
                  wpost[:, 16 * g:16 * g + 16].unsqueeze(1).unsqueeze(3).to_broadcast([P, 2, 16, 16]), ALU.mult,
                  w=[s["t"], vb.w])
        bank = ps.take()
        for it in range(2):
            m = mm(bank.ap[:, it * S:(it + 1) * S],
                   [(gv[:, k, it * P:(it + 1) * P], s["k"][:, k, :]) for k in range(2)], w=[e, bank.w])
        qg.give(gb, m)
        if g == 15:
            qr.give(s["bufs"][0], e)
            kr.give(s["bufs"][1], m)
            vr.give(s["bufs"][2], ve)
        sb_ = sm.take()
        pb = pr.take()
        p = pb.ap.rearrange("p (i n) -> p i n", i=2)
        sv = bank.ap.rearrange("p (i n) -> p i n", i=2)
        r = dve(V.tensor_reduce, sb_.ap[:, 0:2], sv, AX.X, ALU.max, negate=True, w=[m, sb_.w])
        for it in range(2):
            x = act(C.activation, p[:, it, :], sv[:, it, :], ACT.Exp, bias=sb_.ap[:, it:it + 1],
                    accum_out=sb_.ap[:, 2 + it:3 + it], w=[r, pb.w])
        ps.give(bank, x)
        r = dve(V.reciprocal, sb_.ap[:, 4:6], sb_.ap[:, 2:4], w=[x])
        for it in range(2):
            x = dve(V.tensor_scalar, p[:, it, :], p[:, it, :], sb_.ap[:, 4 + it:5 + it], None, ALU.mult, w=[r])
        sm.give(sb_, x)
        s[g] = (pb, p, x, vb, ve)

    def s1(u):
        b, g = divmod(u, 16)
        pb, p, x, vb, ve = st[b][g]
        bank = ps.take()
        m = turn(E, bank, [((jt * 2 + it) * P, p[:, it, jt * P:(jt + 1) * P], P, P) for jt in range(2)
                           for it in range(2)], [x])
        pr.give(pb, m)
        tb = pt.take()
        e = copy(tb.ap, bank.ap, w=[m, tb.w])
        ps.give(bank, e)
        st[b][g] = (tb, e, vb, ve)

    def s2(u):
        b, g = divmod(u, 16)
        s = st[b]
        tb, e, vb, ve = s[g]
        if g == 0:
            s["o"] = [ps.take(), ps.take()]
        v = vb.ap.rearrange("p (j n) -> p j n", j=2)
        for f in range(2):
            m = mm(s["o"][f].ap[:, 0:S], [(v[:, j, f * P:(f + 1) * P], tb.ap[:, j * S:(j + 1) * S])
                                          for j in range(2)], w=[e, ve, s["o"][f].w], first=g == 0, last=g == 15)
        pt.give(tb, m)
        vh.give(vb, m)
        if g == 15:
            ob = ot.take()
            o = ob.ap.rearrange("p (k n) -> p k n", k=2)
            es = []
            for f in range(2):
                es.append(copy(o[:, f, :], s["o"][f].ap[:, 0:S], w=[m, ob.w]))
                ps.give(s["o"][f], es[-1])
            for it in range(2):
                m = E["to_x"](2 * b + it, lambda k: o[:, k, it * P:(it + 1) * P], 2, Wo, [es],
                              bias=W(n, "bo")[0:1, :])
            ot.give(ob, m)
            if b % 2:
                E["finished"](n, b // 2)

    pipe(E, 16 * NB, (0, s0), (2, s1), (3, s2))


def moe_heads(E, n):
    pe, act, dve, pool, T, V, C, G, ps, mm, X, xnT, W, Wk, copy = get(E)
    wt = E["wtok"][n]
    ar = E["Arena"]([(E["scr"], 0, E["NSCR"])])
    We = W(n, "We").rearrange("p (e n) -> p e n", e=4)
    Wo = Wk(n, "Wo", 2)
    pool_ = ar.get(16).rearrange("p (k b) -> p k b", k=2)
    hid = ar.get(8)
    hb_ = ar.get(1024).rearrange("p (b n) -> p b n", b=8)
    gw = ar.get(32).rearrange("p (b e) -> p b e", e=4)
    rk = ar.get(32).rearrange("p (b e) -> p b e", e=4)
    a1, a2 = [ar.get(32).rearrange("p (b e) -> p b e", e=4) for _ in range(2)]
    sm8 = ar.get(8)
    xts = E["inputs_of"](n)
    t = dve(V.tensor_reduce, pool_, xnT.rearrange("p k (b s) -> p k b s", b=8), AX.X, ALU.add, w=[xts])
    t = dve(V.tensor_scalar, pool_, pool_, 1.0 / 256, None, ALU.mult, w=[t])
    bank = ps.take()
    wg1 = Wk(n, "Wg1", 2)
    m = mm(bank.ap[:, 0:8], [(wg1[:, k, :], pool_[:, k, :]) for k in range(2)], w=[t, wt, bank.w])
    t = act(C.activation, hid, bank.ap[:, 0:8], ACT.Relu, bias=W(n, "bg1"), w=[m])
    t = dve(V.tensor_copy, hb_, hid.unsqueeze(2).to_broadcast([P, 8, P]), w=[t])
    for b in range(8):
        m = mm(bank.ap[:, 16 + 4 * b:20 + 4 * b], [(hb_[:, b, :], W(n, "Wg2")),
                                                   (E["ones"][0:1, :], W(n, "bg2")[0:1, :])], w=[t])
    lv = bank.ap[:, 16:48].rearrange("p (b e) -> p b e", e=4)
    t = dve(V.tensor_reduce, sm8, lv, AX.X, ALU.max, w=[m])
    lg = ar.get(32).rearrange("p (b e) -> p b e", e=4)
    t = dve(V.tensor_tensor, gw, lv, sm8.unsqueeze(2).to_broadcast([P, 8, 4]), ALU.subtract, w=[t])
    t = dve(V.tensor_copy, lg, lv, w=[t])
    ps.give(bank, t)
    x = act(C.activation, gw, gw, ACT.Exp, w=[t])
    jgt = E["K"]("jgt").rearrange("p (e j) -> p e j", e=8)
    for e in range(4):
        me = lg[:, :, e:e + 1].to_broadcast([P, 8, 4])
        q = dve(V.tensor_tensor, a1, lg, me, ALU.is_gt, w=[t])
        q = dve(V.tensor_tensor, a2, lg, me, ALU.is_equal, w=[q])
        q = dve(V.tensor_tensor, a2, a2, jgt[:, e, 0:4].unsqueeze(1).to_broadcast([P, 8, 4]), ALU.mult, w=[q])
        q = dve(V.tensor_tensor, a1, a1, a2, ALU.add, w=[q])
        t = dve(V.tensor_reduce, rk[:, :, e], a1, AX.X, ALU.add, w=[q])
    t = dve(V.scalar_tensor_tensor, gw, rk, 1.5, gw, ALU.is_lt, ALU.mult, w=[t, x])
    t = dve(V.tensor_reduce, sm8, gw, AX.X, ALU.add, w=[t])
    t = dve(V.reciprocal, sm8, sm8, w=[t])
    gt = dve(V.tensor_tensor, gw, gw, sm8.unsqueeze(2).to_broadcast([P, 8, 4]), ALU.mult, w=[t])

    wcr = ar.ring(1536, 1)
    bcr = ar.ring(260, 1)
    qr, vr, kmr = ar.ring(512, 2), ar.ring(512, 2), ar.ring(4096, 1)
    att = Heads16(E, n, ar, Wo, W(n, "bo")[0:1, :])
    bqk = W(n, "bqk").rearrange("p (e c) -> p e c", e=4)
    bv = W(n, "bv")[0:1, :].rearrange("p (e c) -> p e c", e=4)

    def pro(b):
        wb, bb = wcr.take(), bcr.take()
        for e in range(4):
            g = gw[:, b, e:e + 1]
            g0 = gw[0:1, b, e:e + 1]
            if e == 0:
                c1 = dve(V.tensor_scalar, wb.ap, We[:, e, :], g, None, ALU.mult, w=[gt, wb.w, wt])
                c2 = dve(V.tensor_scalar, bb.ap[:, 0:4], bqk[:, e, :], g, None, ALU.mult, w=[bb.w])
                c3 = dve(V.tensor_scalar, bb.ap[0:1, 4:260], bv[:, e, :], g0, None, ALU.mult)
            else:
                c2 = dve(V.scalar_tensor_tensor, bb.ap[:, 0:4], bqk[:, e, :], g, bb.ap[:, 0:4], ALU.mult, ALU.add,
                         w=[c2])
                c3 = dve(V.scalar_tensor_tensor, bb.ap[0:1, 4:260], bv[:, e, :], g0, bb.ap[0:1, 4:260], ALU.mult,
                         ALU.add, w=[c3])
                c1 = dve(V.scalar_tensor_tensor, wb.ap, We[:, e, :], g, wb.ap, ALU.mult, ALU.add, w=[c1])
        wc = wb.ap.rearrange("p (m k n) -> p m k n", m=3, k=2)
        qb, vb, kb = qr.take(), vr.take(), kmr.take()
        q = qb.ap.rearrange("p (k n) -> p k n", k=2)
        v = vb.ap.rearrange("p (k n) -> p k n", k=2)
        km = kb.ap.rearrange("p (k h n) -> p k h n", k=2, h=8)
        xb = xnT[:, :, b * S:(b + 1) * S]
        toks = []
        for f in range(2):
            bank = ps.take()
            m1 = mm(bank.ap[:, 0:S], [(wc[:, 0, k, f * P:(f + 1) * P], xb[:, k, :]) for k in range(2)],
                    w=[c1, c2, c3, bank.w])
            m = mm(bank.ap[:, S:2 * S], [(wc[:, 1, k, f * P:(f + 1) * P], xb[:, k, :]) for k in range(2)])
            e1 = dve(V.tensor_scalar, q[:, f, :], bank.ap[:, 0:S], bb.ap[:, f:f + 1], 0.25, ALU.add, ALU.mult,
                     w=[m, qb.w])
            kt_ = att.kraw.take()
            e2 = act(C.activation, kt_.ap, bank.ap[:, S:2 * S], ACT.Identity, bias=bb.ap[:, 2 + f:3 + f],
                     w=[m, e1, kt_.w])
            ps.give(bank, e1, e2)
            e3 = att.mask(km[:, f, :, :], kt_.ap, S, [e2, kb.w])
            att.kraw.give(kt_, e3)
            toks += [e1, e3]
        bank = ps.take()
        for it in range(2):
            m = mm(bank.ap[:, it * S:(it + 1) * S], [(xb[:, k, it * P:(it + 1) * P], wc[:, 2, k, :])
                                                     for k in range(2)]
                   + [(E["ones"][0:1, :], bb.ap[0:1, 4:260])], w=[bank.w])
        e = copy(vb.ap, bank.ap, w=[m, vb.w])
        ps.give(bank, e)
        wcr.give(wb, m)
        bcr.give(bb, m)
        return dict(q=q, v=v, km=km, t=toks + [e],
                    free=[(vr, vb)], free_qk=[(qr, qb), (kmr, kb)])

    att.run(pro)


class Heads16:

    def __init__(self, E, n, ar, Wo, bo, local=False):
        self.E, self.local, self.Wo, self.bo, self.n = E, local, Wo, bo, n
        self.kraw = ar.ring(256, 2)
        self.pr, self.pt = ar.ring(512, 4), ar.ring(512, 3)
        self.osb, self.ot = ar.ring(512, 1), ar.ring(512, 2)
        self.sm = ar.ring(8, 6)
        self.sums = ar.ring(64, 2)
        if local:
            self.g = ar.ring(512, 1)

    def mask(self, o, k, n, w):
        E = self.E
        return E["pool"](E["G"].tensor_tensor, o, k.unsqueeze(1).to_broadcast([P, 8, n]),
                         E["K"]("hm").unsqueeze(2).to_broadcast([P, 8, n]), ALU.mult, w=w)

    def run(self, pro, extra=None):
        pe, act, dve, pool, T, V, C, G, ps, mm, X, xnT, W, Wk, copy = get(self.E)
        E, local = self.E, self.local
        st = {}

        def s0(u):
            b, r = divmod(u, 16)
            if r == 0:
                st[b] = pro(b)
                st[b]["sum"] = self.sums.take()
            s = st[b]
            sb_, pb = self.sm.take(), self.pr.take()
            bank = ps.take()
            sums = s["sum"].ap[:, 0:32].rearrange("p (i h) -> p i h", i=2)
            if local:
                kt, h8 = divmod(r, 8)
                lw = [(0, 0, P, 0, r), (1, P, S, 1, r)]
                for it, c, n, _, _ in lw:
                    m = mm(bank.ap[:, c:c + n], [(s["q"][:, kt, it * P:(it + 1) * P], s["km"][:, kt, h8, 0:n])],
                           w=[s["t"], bank.w])
                r_ = dve(V.scalar_tensor_tensor, pb.ap[:, 0:384], W(self.n, "dist"), float(2.0 ** (-(r + 1) * 0.5)),
                         bank.ap[:, 0:384], ALU.mult, ALU.add, w=[m, pb.w])
                ps.give(bank, r_)
                for it, c, n, _, _ in lw:
                    q = dve(V.tensor_reduce, sb_.ap[:, it:it + 1], pb.ap[:, c:c + n], AX.X, ALU.max, negate=True,
                            w=[r_, sb_.w])
                for it, c, n, _, _ in lw:
                    x = act(C.activation, pb.ap[:, c:c + n], pb.ap[:, c:c + n], ACT.Exp, bias=sb_.ap[:, it:it + 1],
                            accum_out=sums[:, it, r:r + 1], w=[q, s["sum"].w])
            else:
                kt, r2 = divmod(r, 8)
                pair, it = divmod(r2, 2)
                m = mm(bank.ap, [(s["q"][:, kt, it * P:(it + 1) * P],
                                  s["km"][:, kt, 2 * pair:2 * pair + 2, :])], w=[s["t"], bank.w])
                sv = bank.ap.rearrange("p (i n) -> p i n", i=2)
                q = dve(V.tensor_reduce, sb_.ap[:, 0:2], sv, AX.X, ALU.max, negate=True, w=[m, sb_.w])
                for j in range(2):
                    h = 8 * kt + 2 * pair + j
                    x = act(C.activation, pb.ap[:, j * S:(j + 1) * S], sv[:, j, :], ACT.Exp,
                            bias=sb_.ap[:, j:j + 1], accum_out=sums[:, it, h:h + 1], w=[q, pb.w, s["sum"].w])
                ps.give(bank, x)
            self.sm.give(sb_, x)
            s[r] = (pb, x)
            if r == 15:
                if extra:
                    m = extra(b, s)
                for ring, buf in s["free_qk"]:
                    ring.give(buf, m)

        def s1(u):
            b, r = divmod(u, 16)
            pb, x = st[b][r]
            bank = ps.take()
            n = 3 if local else 4
            m = turn(E, bank, [(j * P, pb.ap[:, j * P:(j + 1) * P], P, P) for j in range(n)], [x])
            self.pr.give(pb, m)
            tb = self.pt.take()
            e = copy(tb.ap[:, 0:n * P], bank.ap[:, 0:n * P], w=[m, tb.w])
            ps.give(bank, e)
            st[b][r] = (tb, e, x)

        def s2(u):
            b, r = divmod(u, 16)
            s = st[b]
            tb, e, x = s[r]
            if r == 0:
                s["o"] = ps.take()
            o = s["o"].ap.rearrange("p (i n) -> p i n", i=2)
            pt = tb.ap
            if local:
                items = [(0, r, [(0, 0)]), (1, r, [(1, 0), (2, 1)])]
            else:
                kt, r2 = divmod(r, 8)
                pair, it = divmod(r2, 2)
                items = [(it, 8 * kt + 2 * pair + j, [(2 * j, 0), (2 * j + 1, 1)]) for j in range(2)]
            for it, h, parts in items:
                m = mm(o[:, it, 16 * h:16 * h + 16],
                       [(pt[:, c * P:(c + 1) * P], s["v"][:, jt, 16 * h:16 * h + 16]) for c, jt in parts],
                       w=[e, s["o"].w])
            self.pt.give(tb, m)
            if r < 15:
                return
            rs = s["sum"].ap[:, 32:64]
            q = dve(V.reciprocal, rs, s["sum"].ap[:, 0:32], w=[x])
            ob = self.osb.take()
            ov = ob.ap.rearrange("p (g d) -> p g d", d=16)
            q = dve(V.tensor_tensor, ov, s["o"].ap.rearrange("p (g d) -> p g d", d=16),
                    rs.unsqueeze(2).to_broadcast([P, 32, 16]), ALU.mult, w=[q, m, ob.w])
            ps.give(s["o"], q)
            self.sums.give(s["sum"], q)
            if local:
                q = dve(V.tensor_tensor, ob.ap, ob.ap, s["og"].ap, ALU.add, w=[q, s["og_t"]])
                ps.give(s["og"], q)
            for ring, buf in s["free"]:
                ring.give(buf, m)
            finish_heads(E, self.n, b, ob.ap.rearrange("p (i n) -> p i n", i=2), self.ot, self.Wo, self.bo, [q],
                         lambda tok: self.osb.give(ob, tok))

        pipe(E, 16 * NB, (0, s0), (2, s1), (3, s2))


def local_heads(E, n):
    pe, act, dve, pool, T, V, C, G, ps, mm, X, xnT, W, Wk, copy = get(E)
    wt = E["wtok"][n]
    ar = E["Arena"]([(E["scr"], 0, E["NSCR"])])
    Wqk, Wv, Wo = Wk(n, "Wqk", 2), Wk(n, "Wv", 2), Wk(n, "Wo", 2)
    rbufs = (ar.ring(512, 2), ar.ring(512, 1))
    qr, vr, kmr = ar.ring(512, 2), ar.ring(512, 2), ar.ring(4096, 1)
    att = Heads16(E, n, ar, Wo, None, local=True)
    pg, pgT, vg, gs = ar.get(128), ar.get(256), ar.get(256), ar.get(96)
    xts = E["inputs_of"](n)
    held = {"g": None}

    def pro(b):
        qb, vb, kb = qr.take(), vr.take(), kmr.take()
        q = qb.ap.rearrange("p (k n) -> p k n", k=2)
        v = vb.ap.rearrange("p (k n) -> p k n", k=2)
        km = kb.ap.rearrange("p (k h n) -> p k h n", k=2, h=8)
        toks = []
        for it in range(2):
            t = 2 * b + it
            bank, m = rope_tile(E, t, Wqk, None, rbufs, [xts[b // 2], wt])
            bv = bank.ap.rearrange("p (j n) -> p j n", j=4)
            e1 = act(C.activation, q[:, :, it * P:(it + 1) * P], bv[:, 0:2, :], ACT.Copy, scale=0.25, w=[m, qb.w])
            kt_ = att.kraw.take()
            e2 = act(C.activation, kt_.ap, bank.ap[:, 256:512], ACT.Copy, w=[m, kt_.w])
            ps.give(bank, e1, e2)
            kk = kt_.ap.rearrange("p (k n) -> p k n", k=2)
            for f in range(2):
                e3 = att.mask(km[:, f, :, it * P:(it + 1) * P], kk[:, f, :], P, [e2, kb.w])
            att.kraw.give(kt_, e3)
            bank = ps.take()
            m = mm(bank.ap[:, 0:D], [(xnT[:, k2, t * P:(t + 1) * P], Wv[:, k2, :]) for k2 in range(2)], w=[bank.w])
            e4 = copy(v[:, it, :], bank.ap[:, 0:D], w=[m, vb.w])
            ps.give(bank, e4)
            toks += [e1, e3, e4]
        return dict(q=q, v=v, km=km, t=toks, free=[(vr, vb)], free_qk=[(qr, qb), (kmr, kb)])

    def extra(b, s):
        hold = held["g"]
        bank = ps.take()
        for it in range(2):
            for kt in range(2):
                c = it * 64 + kt * 32
                m = mm(bank.ap[:, c:c + 32], [(s["q"][:, kt, it * P:(it + 1) * P], s["km"][:, kt, :, 0:256:64])],
                       w=[bank.w, s["t"]])
        m2 = mm(bank.ap[0:64, 128:128 + D], [(W(n, "gsel")[:, 64 * t:64 * t + 64], s["v"][:, t, :])
                                              for t in range(2)])
        sv = bank.ap[:, 0:128].rearrange("p (g j) -> p g j", j=4)
        pv = pg.rearrange("p (g j) -> p g j", j=4)
        bc = lambda a: a.unsqueeze(2).to_broadcast([P, 32, 4])
        q = dve(V.tensor_reduce, gs[:, 0:32], sv, AX.X, ALU.max, w=[m, m2, hold])
        q = dve(V.tensor_tensor, pv, sv, bc(gs[:, 0:32]), ALU.subtract, w=[q])
        q2 = dve(V.tensor_tensor, vg[0:64, :], bank.ap[0:64, 128:128 + D], W(n, "gmask", 64), ALU.mult,
                 w=[m2, hold])
        ps.give(bank, q, q2)
        q = act(C.activation, pg, pg, ACT.Exp, w=[q])
        q = dve(V.tensor_reduce, gs[:, 32:64], pv, AX.X, ALU.add, w=[q])
        q = dve(V.reciprocal, gs[:, 64:96], gs[:, 32:64], w=[q])
        q = dve(V.tensor_tensor, pv, pv, bc(gs[:, 64:96]), ALU.mult, w=[q])
        bank = ps.take()
        m = turn(E, bank, [(it * P, pg[:, it * 64:(it + 1) * 64], P, 64) for it in range(2)], [q])
        e = dve(V.tensor_copy, pgT[0:64, :], bank.ap[0:64, 0:256], w=[m])
        ps.give(bank, e)
        og = ps.take()
        for it in range(2):
            m = mm(og.ap[:, it * S:(it + 1) * S], [(pgT[0:64, it * P:(it + 1) * P], vg[0:64, :])],
                   w=[e, q2, og.w])
        held["g"] = m
        s["og"], s["og_t"] = og, m
        return m

    att.run(pro, extra)


def few_keys(E, n):
    pe, act, dve, pool, T, V, C, G, ps, mm, X, xnT, W, Wk, copy = get(E)
    wt, A, dma = E["wtok"][n], E["A"], E["dma"]
    ar = E["Arena"]([(E["scr"], 0, E["NSCR"])])
    small = n == 4
    kt = 2 if small else 8
    inner = kt * P
    dh = inner // 16
    if small:
        Wq, Wkk, Wv, Wo = [Wk(n, x, 2) for x in ("Wq", "Wk", "Wv", "Wo")]
    else:
        Wq, Wkk, Wv, Wo = Wk(n, "wq", 2), Wk(n, "wk", 2), Wk(n, "wv", 2), Wk(n, "wo", 8)
    bo = W(n, "bo")[0:1, :]
    ctxT = E["ctxT"]
    kT = ar.get(kt * 616).rearrange("p (k n) -> p k n", k=kt)
    qr = ar.ring(kt * S, 1 if not small else 2)
    vr = ar.ring(inner, 2)
    pr = ar.ring(16 * S2, 2)
    pt = ar.ring(512, 4)
    osb = ar.ring(2 * inner, 1)
    ot = ar.ring(2 * inner, 1)
    sm = ar.ring(48, 4)
    kts = []
    for f in range(kt):
        for h in range(2):
            bank = ps.take()
            m = mm(bank.ap[:, 0:308], [(Wkk[:, k, f * P:(f + 1) * P], ctxT[:, k, h * 308:(h + 1) * 308])
                                       for k in range(2)], w=[bank.w, wt, E["ctx_tok"]])
            o = kT[:, f, h * 308:(h + 1) * 308]
            if small:
                e = act(C.activation, o, bank.ap[:, 0:308], ACT.Identity, bias=W(n, "bk")[:, f:f + 1], w=[m])
            else:
                e = copy(o, bank.ap[:, 0:308], w=[m])
            ps.give(bank, e)
            kts.append(e)
    if small:
        mu = ar.get(154)
        pen = ar.get(616)
        kmr = ar.ring(2 * 8 * S2, 2)
        br = ar.ring(2 * S2, 2)
        mt = dma(mu.bitcast(U8), A["mbf"].rearrange("(a b) s -> a (b s)", a=1).partition_broadcast(P)
                 if False else A["mbf"].rearrange("b s -> (b s)").partition_broadcast(P), E["bars"][-1])
        q = dve(V.tensor_scalar, pen, mu.bitcast(U8), -3e38, 2.0, ALU.mult, ALU.mult, w=[mt])
        pen_t = q
        am = W(n, "am").rearrange("p (i s) -> p i s", i=2)
    groups = [(0, 6), (6, 12), (12, 16)]
    xts = E["inputs_of"](n)
    st = {}

    def pro(b):
        qb, vb = qr.take(), vr.take()
        q = qb.ap.rearrange("p (k n) -> p k n", k=kt)
        toks = []
        for f in range(0, kt, 2):
            bank = ps.take()
            for j in range(2):
                m = mm(bank.ap[:, j * S:(j + 1) * S],
                       [(Wq[:, k, (f + j) * P:(f + j + 1) * P], xnT[:, k, b * S:(b + 1) * S]) for k in range(2)],
                       w=[bank.w, xts[b // 2], wt])
            if small:
                for j in range(2):
                    e = dve(V.tensor_scalar, q[:, j, :], bank.ap[:, j * S:(j + 1) * S], W(n, "bq")[:, j:j + 1], 0.25,
                            ALU.add, ALU.mult, w=[m, qb.w])
            else:
                e = act(C.activation, qb.ap[:, f * S:(f + 2) * S], bank.ap, ACT.Copy, scale=0.125, w=[m, qb.w])
            ps.give(bank, e)
            toks.append(e)
        for c in range(0, inner, 512):
            n_ = min(512, inner)
            bank = ps.take()
            pairs = [(ctxT[:, k, b * S2:(b + 1) * S2], Wv[:, k, c:c + n_]) for k in range(2)]
            if small:
                pairs.append((E["ones"][0:1, 0:S2], W(n, "bv")[0:1, :]))
            m = mm(bank.ap[0:S2, 0:n_], pairs, w=[bank.w, E["ctx_tok"]])
            e = copy(vb.ap[0:S2, c:c + n_], bank.ap[0:S2, 0:n_], w=[m, vb.w])
            ps.give(bank, e)
            toks.append(e)
        s = dict(q=q, v=vb.ap, t=toks, free=[(vr, vb)], qb=qb)
        if small:
            kb, bb = kmr.take(), br.take()
            km = kb.ap.rearrange("p (k h n) -> p k h n", k=2, h=8)
            for f in range(2):
                e = pool(G.tensor_tensor, km[:, f, :, :],
                         kT[:, f, b * S2:(b + 1) * S2].unsqueeze(1).to_broadcast([P, 8, S2]),
                         E["K"]("hm").unsqueeze(2).to_broadcast([P, 8, S2]), ALU.mult, w=[kts, kb.w])
            s["t"].append(e)
            e = pool(G.tensor_tensor, bb.ap.rearrange("p (i s) -> p i s", i=2), am,
                     pen[:, b * S2:(b + 1) * S2].unsqueeze(1).to_broadcast([P, 2, S2]), ALU.add,
                     w=[pen_t, wt, bb.w])
            s["bias"] = bb.ap.rearrange("p (i s) -> p i s", i=2)
            s["bt"] = e
            s["km"] = km
            s["free"] += [(kmr, kb), (br, bb)]
        st[b] = s

    def s0(u):
        b, it = divmod(u, 2)
        if it == 0:
            pro(b)
        s = st[b]
        pb, sb_ = pr.take(), sm.take()
        p = pb.ap.rearrange("p (h n) -> p h n", h=16)
        xs = []
        for lo, hi in groups:
            bank = ps.take()
            if small:
                cuts = [(max(lo, 8 * f), min(hi, 8 * f + 8), f) for f in range(2)]
                for a, z, f in cuts:
                    if a < z:
                        m = mm(bank.ap[:, (a - lo) * S2:(z - lo) * S2],
                               [(s["q"][:, f, it * P:(it + 1) * P], s["km"][:, f, a - 8 * f:z - 8 * f, :])],
                               w=[bank.w, s["t"]])
            else:
                for par in range(2):
                    for h in range(lo, hi):
                        if h % 2 == par:
                            o = 64 * par
                            m = mm(bank.ap[:, (h - lo) * S2:(h - lo + 1) * S2],
                                   [(s["q"][o:o + 64, h // 2, it * P:(it + 1) * P],
                                     kT[o:o + 64, h // 2, b * S2:(b + 1) * S2])],
                                   w=[bank.w, s["t"], kts] + ([m] if par and h - lo < 2 else []))
            qk = m
            nh = hi - lo
            sv = bank.ap[:, 0:nh * S2].rearrange("p (h n) -> p h n", n=S2)
            pv = p[:, lo:hi, :]
            mx = sb_.ap[:, lo:hi]
            src = sv
            if small:
                q = dve(V.tensor_tensor, pv, sv, s["bias"][:, it, :].unsqueeze(1).to_broadcast([P, nh, S2]), ALU.add,
                        w=[m, s["bt"], pb.w])
                bt = q
                src = pv
                m = q
            q = dve(V.tensor_reduce, mx, src, AX.X, ALU.max, w=[m, sb_.w])
            q = dve(V.tensor_tensor, pv, src, mx.unsqueeze(2).to_broadcast([P, nh, S2]), ALU.subtract,
                    w=[q, pb.w])
            ps.give(bank, q)
            x = act(C.activation, pv, pv, ACT.Exp, w=[q])
            q = dve(V.tensor_reduce, sb_.ap[:, 16 + lo:16 + hi], pv, AX.X, ALU.add, w=[x])
            xs.append(x)
        q = dve(V.reciprocal, sb_.ap[:, 32:48], sb_.ap[:, 16:32], w=[q])
        s[it] = (pb, p, xs, sb_, q)
        if it == 1:
            qr.give(s["qb"], qk)

    def s1(u):
        b, it = divmod(u, 2)
        s = st[b]
        pb, p, xs, sb_, q = s[it]
        if it == 0:
            s["osb"] = osb.take()
        ob = s["osb"]
        ov = ob.ap.rearrange("p (i n) -> p i n", i=2)
        per = 512 // dh if not small else 16
        obank = None
        for g in range(4):
            bank = ps.take()
            m = turn(E, bank, [(j * P, p[:, 4 * g + j, :], P, S2) for j in range(4)], [xs[min(2, (4 * g + 3) // 6)]])
            tb = pt.take()
            e = copy(tb.ap[0:S2, :], bank.ap[0:S2, :], w=[m, tb.w])
            ps.give(bank, e)
            s[("t", g)] = (tb, e)
        pr.give(pb, m)
        for h in range(16):
            if h % per == 0:
                obank = ps.take()
            tb, e = s[("t", h // 4)]
            c = (h % per) * dh
            m = mm(obank.ap[:, c:c + dh], [(tb.ap[0:S2, (h % 4) * P:(h % 4 + 1) * P], s["v"][0:S2, h * dh:(h + 1) * dh])],
                   w=[e, obank.w])
            if h % 4 == 3:
                pt.give(tb, m)
            if (h + 1) % per == 0:
                lo = h + 1 - per
                z = dve(V.tensor_tensor, ov[:, it, lo * dh:(h + 1) * dh].rearrange("p (h d) -> p h d", d=dh),
                        obank.ap[:, 0:per * dh].rearrange("p (h d) -> p h d", d=dh),
                        sb_.ap[:, 32 + lo:32 + h + 1].unsqueeze(2).to_broadcast([P, per, dh]), ALU.mult,
                        w=[m, q, ob.w])
                ps.give(obank, z)
        sm.give(sb_, z)
        if it == 1:
            for ring, buf in s["free"]:
                ring.give(buf, m, z)
            finish_heads(E, n, b, ov, ot, Wo, bo, [z], lambda tok: osb.give(ob, tok))

    pipe(E, 2 * NB, (0, s0), (1, s1))


def latent_heads(E, n):
    pe, act, dve, pool, T, V, C, G, ps, mm, X, xnT, W, Wk, copy = get(E)
    wt = E["wtok"][n]
    ar = E["Arena"]([(E["scr"], 0, E["NSCR"])])
    many = n == 1
    H = 16 if many else 4
    inner = 64 * H
    kt = inner // P
    NK = 333
    cg = ar.get(1232).rearrange("p (k n) -> p k n", k=2)
    qr, kr, vr = ar.ring(kt * S, 1), ar.ring(kt * NK, 1), ar.ring(3 * inner, 2)
    pr, pt = ar.ring(672, 3), ar.ring(768, 2)
    xts = E["inputs_of"](n)
    osb = ar.ring(2 * inner, 1)
    ot = ar.ring(2 * inner, 1)
    sums = ar.ring(64, 2)
    sm = ar.ring(8, 6)
    g, bb = ("mg", "mb") if many else ("xg", "xb")
    for k in range(2):
        cgt = dve(V.tensor_scalar, cg[:, k, :], E["cnT"][:, k, :], W(n, g)[:, k:k + 1], W(n, bb)[:, k:k + 1],
                  ALU.mult, ALU.add, w=[E["ctx_tok"], wt])
    if many:
        Wq = Wk(n, "Wq", 2)
        Wkv = Wk(n, "Wkv", 2)
        Wo, bo = Wk(n, "Wout", 8), None
        vW = lambda k, c, m: Wkv[:, k, inner + c:inner + c + m]
    else:
        Wqk, Wvv = Wk(n, "Wqk", 2), Wk(n, "Wv", 2)
        Wo, bo = Wk(n, "Wo", 2), W(n, "bo")[0:1, :]
        vW = lambda k, c, m: Wvv[:, k, c:c + m]
        gq = ar.get(2)
        gqt = dve(V.tensor_scalar, gq[:, 0:1], W(n, "gq"), 0.125, None, ALU.mult, w=[wt])
        mu, pen = ar.get(154), ar.get(616)
        mt = E["dma"](mu.bitcast(U8), E["A"]["mbk"].rearrange("b s -> (b s)").partition_broadcast(P),
                      E["bars"][-1])
        pen_t = dve(V.tensor_scalar, pen, mu.bitcast(U8), -1.0, 1e30, ALU.add, ALU.mult, w=[mt])
        sqr, nrr, rsr = ar.ring(512, 2), ar.ring(512, 2), ar.ring(24, 2)
    st = {}

    def values(b, v):
        toks = []
        for j in range(3):
            rows = P if j < 2 else S2
            for c in range(0, inner, 512):
                m_ = min(512, inner)
                bank = ps.take()
                if j < 2:
                    l = lambda k: xnT[:, k, (2 * b + j) * P:(2 * b + j + 1) * P]
                else:
                    l = lambda k: cg[:, k, b * S2:(b + 1) * S2]
                m = mm(bank.ap[0:rows, 0:m_], [(l(k), vW(k, c, m_)) for k in range(2)],
                       w=[bank.w, xts[b // 2], cgt, wt])
                e = copy(v.ap[0:rows, j * inner + c:j * inner + c + m_], bank.ap[0:rows, 0:m_], w=[m, v.w])
                ps.give(bank, e)
                toks.append(e)
        return toks

    def pro(b):
        qb, kb, vb = qr.take(), kr.take(), vr.take()
        q = qb.ap.rearrange("p (k n) -> p k n", k=kt)
        k_ = kb.ap.rearrange("p (k n) -> p k n", k=kt)
        toks = values(b, vb)
        if many:
            for f in range(0, kt, 2):
                for what in range(2):
                    wm = Wq if what == 0 else Wkv
                    bank = ps.take()
                    for j in range(2):
                        m = mm(bank.ap[:, j * S:(j + 1) * S],
                               [(wm[:, k, (f + j) * P:(f + j + 1) * P], xnT[:, k, b * S:(b + 1) * S])
                                for k in range(2)], w=[bank.w])
                    if what == 0:
                        e = act(C.activation, qb.ap[:, f * S:(f + 2) * S], bank.ap, ACT.Copy, scale=0.125,
                                w=[m, qb.w])
                    else:
                        e = dve(V.tensor_copy, k_[:, f:f + 2, 0:S],
                                bank.ap.rearrange("p (k n) -> p k n", k=2), w=[m, kb.w])
                    ps.give(bank, e)
                    toks.append(e)
            for f in range(0, kt, 4):
                bank = ps.take()
                for j in range(4):
                    m = mm(bank.ap[:, j * S2:(j + 1) * S2],
                           [(Wkv[:, k, (f + j) * P:(f + j + 1) * P], cg[:, k, b * S2:(b + 1) * S2])
                            for k in range(2)], w=[bank.w, cgt])
                e = copy(k_[:, f:f + 4, S:NK], bank.ap[:, 0:4 * S2].rearrange("p (k n) -> p k n", k=4),
                         w=[m, kb.w])
                ps.give(bank, e)
                toks.append(e)
        else:
            for j in range(3):
                rows = P if j < 2 else S2
                bank = ps.take()
                lo = 0 if j < 2 else 256
                l = (lambda k: xnT[:, k, (2 * b + j) * P:(2 * b + j + 1) * P]) if j < 2 else \
                    (lambda k: cg[:, k, b * S2:(b + 1) * S2])
                m = mm(bank.ap[0:rows, lo:512], [(l(k), Wqk[:, k, lo:512]) for k in range(2)], w=[bank.w])
                s_, n_, r_ = sqr.take(), nrr.take(), rsr.take()
                nh = (512 - lo) // 64
                e = act(C.activation, s_.ap[0:rows, lo:512], bank.ap[0:rows, lo:512], ACT.Square, w=[m, s_.w])
                h8 = lambda a: a[0:rows, lo:512].rearrange("p (h d) -> p h d", d=64)
                r = r_.ap[0:rows, 0:nh]
                e1 = dve(V.tensor_reduce, r, h8(s_.ap), AX.X, ALU.add, w=[e, r_.w])
                sqr.give(s_, e1)
                e2 = act(C.activation, r, r, ACT.Sqrt, scale=1.0 / 64, w=[e1])
                e2 = dve(V.tensor_scalar, r, r, 1e-8, None, ALU.max, w=[e2])
                e2 = dve(V.reciprocal, r, r, w=[e2])
                e2 = dve(V.tensor_tensor, h8(n_.ap), h8(bank.ap), r.unsqueeze(2).to_broadcast([rows, nh, 64]),
                         ALU.mult, w=[e2, n_.w])
                rsr.give(r_, e2)
                ps.give(bank, e2)
                bank = ps.take()
                m = turn(E, bank, [(c * P, n_.ap[0:rows, c * P:(c + 1) * P], rows, P)
                                   for c in range(lo // P, 4)], [e2])
                nrr.give(n_, m)
                bv = bank.ap.rearrange("p (c n) -> p c n", c=4)
                if j < 2:
                    e3 = act(C.activation, q[:, :, j * P:(j + 1) * P], bv[:, 0:2, :], ACT.Copy, scale=gq[:, 0:1],
                             w=[m, qb.w, gqt])
                    toks.append(e3)
                kd = k_[:, :, j * P:(j + 1) * P] if j < 2 else k_[:, :, S:NK]
                e4 = act(C.activation, kd, bv[:, 2:4, 0:rows], ACT.Copy, scale=W(n, "gk")[:, 0:1], w=[m, kb.w])
                toks.append(e4)
                ps.give(bank, e4)
        st[b] = dict(q=q, k=k_, v=vb.ap.rearrange("p (j n) -> p j n", j=3), t=toks, qkb=(qb, kb), vb=vb,
                     sum=sums.take())

    def s0(u):
        b, h = divmod(u, H)
        if h == 0:
            pro(b)
        s = st[b]
        o = 64 * (h % 2)
        pb, sb_ = pr.take(), sm.take()
        su = s["sum"].ap.rearrange("p (r i h) -> p r i h", r=2, i=2)
        xs = []
        for it in range(2):
            bank = ps.take()
            ql = s["q"][o:o + 64, h // 2, it * P:(it + 1) * P]
            m = mm(bank.ap[:, 0:S], [(ql, s["k"][o:o + 64, h // 2, 0:S])], w=[bank.w, s["t"]])
            m = mm(bank.ap[:, S:NK], [(ql, s["k"][o:o + 64, h // 2, S:NK])], last=many)
            if not many:
                m = pe(T.matmul, bank.ap[:, S:NK], E["ones"][o:o + 1, :], pen[o:o + 1, b * S2:(b + 1) * S2],
                       start=False, stop=True, w=[pen_t] + ([m] if o else []))
            q = dve(V.tensor_reduce, sb_.ap[:, it:it + 1], bank.ap[:, 0:NK], AX.X, ALU.max, negate=True,
                    w=[m, sb_.w])
            x = act(C.activation, pb.ap[:, it * 336:it * 336 + NK], bank.ap[:, 0:NK], ACT.Exp,
                    bias=sb_.ap[:, it:it + 1], accum_out=su[:, 0, it, h:h + 1], w=[q, pb.w, s["sum"].w])
            ps.give(bank, x)
        sm.give(sb_, x)
        s[h] = (pb, x)
        if h == H - 1:
            qr.give(s["qkb"][0], m)
            kr.give(s["qkb"][1], m)

    def s1(u):
        b, h = divmod(u, H)
        pb, x = st[b][h]
        p = pb.ap.rearrange("p (i n) -> p i n", i=2)
        bank, bank2 = ps.take(), ps.take()
        m = turn(E, bank, [((jt * 2 + it) * P, p[:, it, jt * P:(jt + 1) * P], P, P) for jt in range(2)
                           for it in range(2)], [x])
        m2 = turn(E, bank2, [(it * P, p[:, it, S:NK], P, S2) for it in range(2)], [x])
        pr.give(pb, m2)
        tb = pt.take()
        e = dve(V.tensor_copy, tb.ap[:, 0:512], bank.ap, w=[m, tb.w])
        e2 = act(C.activation, tb.ap[0:S2, 512:768], bank2.ap[0:S2, 0:256], ACT.Copy, w=[m2, tb.w])
        ps.give(bank, e)
        ps.give(bank2, e2)
        st[b][h] = (tb, [e, e2], x)

    def s2(u):
        b, h = divmod(u, H)
        s = st[b]
        tb, e, x = s[h]
        hp = min(8, H)
        if h == 0:
            s["osb"] = osb.take()
        if h % hp == 0:
            s["o"] = [ps.take(), ps.take()]
        for it in range(2):
            c = (h % hp) * 64
            m = mm(s["o"][it].ap[:, c:c + 64],
                   [(tb.ap[:, (jt * 2 + it) * P:(jt * 2 + it + 1) * P], s["v"][:, jt, h * 64:(h + 1) * 64])
                    for jt in range(2)]
                   + [(tb.ap[0:S2, 512 + it * P:512 + (it + 1) * P], s["v"][0:S2, 2, h * 64:(h + 1) * 64])],
                   w=[e, s["o"][it].w])
        pt.give(tb, m)
        su = s["sum"].ap.rearrange("p (r i h) -> p r i h", r=2, i=2)
        ov = s["osb"].ap.rearrange("p (i n) -> p i n", i=2)
        if (h + 1) % hp == 0:
            lo = h + 1 - hp
            for it in range(2):
                q = dve(V.reciprocal, su[:, 1, it, lo:h + 1], su[:, 0, it, lo:h + 1], w=[x])
                q = dve(V.tensor_tensor, ov[:, it, lo * 64:(h + 1) * 64].rearrange("p (h d) -> p h d", d=64),
                        s["o"][it].ap[:, 0:hp * 64].rearrange("p (h d) -> p h d", d=64),
                        su[:, 1, it, lo:h + 1].unsqueeze(2).to_broadcast([P, hp, 64]), ALU.mult,
                        w=[q, m, s["osb"].w])
                ps.give(s["o"][it], q)
        if h == H - 1:
            sums.give(s["sum"], q)
            vr.give(s["vb"], m)
            finish_heads(E, n, b, ov, ot, Wo, bo, [q], lambda tok: osb.give(s["osb"], tok))

    pipe(E, H * NB, (0, s0), (2, s1), (3, s2))


def softplus(E, o, x, t1, t2, n_w):
    pe, act, dve, pool, T, V, C, G, ps, mm, X, xnT, W, Wk, copy = get(E)
    q = act(C.activation, t1, x, ACT.Abs, w=n_w)
    q = act(C.activation, t1, t1, ACT.Exp, scale=-1.0, w=[q])
    ql = act(C.activation, t2, t1, ACT.Ln, bias=E["one_ap"], w=[q, E["z_tok"]])
    qo = dve(V.scalar_tensor_tensor, t2, x, 0.0, t2, ALU.max, ALU.add, w=[ql])
    qm = dve(V.tensor_scalar, o, t1, 1.0, -1.0, ALU.add, ALU.add, w=[q, qo])
    qm = pool(G.tensor_tensor, t1, t1, o, ALU.subtract, w=[qm])
    return dve(V.tensor_tensor, o, t2, t1, ALU.add, w=[qo, qm])


def gated(E, n):
    pe, act, dve, pool, T, V, C, G, ps, mm, X, xnT, W, Wk, copy = get(E)
    wt = E["wtok"][n]
    ar = E["Arena"]([(E["scr"], 0, E["NSCR"])])
    buf = [ar.get(2048) for _ in range(8)]
    la, tz = ar.get(2), ar.get(8)
    R = ar.get(2048).rearrange("p (t d) -> p t d", t=8)
    q = dve(V.tensor_scalar, tz[:, 0:2], W(n, "lam"), -1.0, None, ALU.mult, w=[wt])
    q = softplus(E, tz[:, 6:8], tz[:, 0:2], tz[:, 2:4], tz[:, 4:6], [q])
    lat = dve(V.tensor_scalar, la, tz[:, 6:8], -0.125, None, ALU.mult, w=[q])
    Wm = {k: Wk(n, k, 2) for k in ("lin", "conv", "a", "x", "lin2", "w1", "w2", "w3")}
    col_ = lambda name, f: W(n, name)[:, f:f + 1]
    v2 = lambda a: a.rearrange("p (k n) -> p k n", k=2)

    def project(name, src, w, evac):
        toks = []
        for f in range(2):
            for c in range(2):
                bank = ps.take()
                m = mm(bank.ap, [(Wm[name][:, k, f * P:(f + 1) * P], src(k, c)) for k in range(2)], w=[bank.w, w])
                e = evac(f, c, bank, m)
                ps.give(bank, e)
                toks.append(e)
        return toks

    done = None
    for hf in range(2):
        lin, gel, xc, rt, gi, om, hs, y = [v2(b) for b in buf]
        flat = {id(v): b for v, b in zip((lin, gel, xc, rt, gi, om, hs, y), buf)}
        rt_ = []
        for c in range(2):
            stb = E["st_ring"].take()
            a = 8 * hf + 4 * c
            e = E["normalise"](R[:, 4 * c:4 * c + 4, :], X[:, a:a + 4, :], 4, P, "ln", [done], stb,
                               E["xtok"][a:a + 4])
            E["st_ring"].give(stb, e)
            rt_ += [e] * 4
        xt = [E["norm_chunk"](2 * hf + c, ["rms16"], g=W(n, "g1"), w=[wt],
                              source=(R[:, 4 * c:4 * c + 4, :], rt_[4 * c:4 * c + 4])) for c in range(2)]
        xs = lambda k, c: xnT[:, k, (2 * hf + c) * 512:(2 * hf + c + 1) * 512]
        at = lambda v, f, c: v[:, f, c * 512:(c + 1) * 512]
        t_lin = project("lin", xs, xt, lambda f, c, b, m: dve(
            V.tensor_scalar, at(lin, f, c), b.ap, col_("blin", f), None, ALU.add, w=[m, done]))
        t_gel = act(C.activation, buf[1], buf[0], ACT.Gelu, w=[t_lin, done])
        t_xc = project("conv", lambda k, c: at(lin, k, c), t_lin, lambda f, c, b, m: dve(
            V.tensor_scalar, at(xc, f, c), b.ap, col_("bconv", f), None, ALU.add, w=[m, done]))
        t_r = project("a", lambda k, c: at(xc, k, c), t_xc, lambda f, c, b, m: act(
            C.activation, at(rt, f, c), b.ap, ACT.Sigmoid, bias=col_("ba", f), w=[m, done]))
        t_i = project("x", lambda k, c: at(xc, k, c), t_xc, lambda f, c, b, m: act(
            C.activation, at(gi, f, c), b.ap, ACT.Sigmoid, bias=col_("bx", f), w=[m, done]))
        for f in range(2):
            t_a = act(C.activation, rt[:, f, :], rt[:, f, :], ACT.Exp, scale=la[:, f:f + 1], w=[t_r, lat])
        q = pool(G.tensor_tensor, buf[4], buf[4], buf[2], ALU.mult, w=[t_i, t_xc])
        o = dve(V.tensor_tensor, buf[5], buf[3], buf[3], ALU.mult, w=[t_a, done])
        z = dve(V.memset, buf[3].rearrange("p (b s) -> p b s", s=S)[:, :, 0:1], 0.0, w=[o])
        o = dve(V.tensor_scalar, buf[5], buf[5], -1.0, 1.0, ALU.mult, ALU.add, w=[o])
        o = act(C.activation, buf[5], buf[5], ACT.Sqrt, w=[o])
        o = dve(V.tensor_tensor, buf[4], buf[4], buf[5], ALU.mult, w=[o, q])
        o = dve(V.tensor_tensor_scan, buf[6], buf[3], buf[4], 0.0, ALU.mult, ALU.add, w=[o, z, done])
        o = dve(V.tensor_tensor, buf[7], buf[6], buf[1], ALU.mult, w=[o, t_gel])
        for c in range(2):
            for j in range(4):
                i = 4 * c + j
                rt_[i] = E["to_x"](i, lambda k: y[:, k, i * P:(i + 1) * P], 2, Wm["lin2"], [o],
                                   bias=W(n, "blin2")[0:1, :], onto=(R[:, i, :], [rt_[i], xt]))
                E["xtok"][8 * hf + i] = pool(G.tensor_tensor, X[:, 8 * hf + i, :], X[:, 8 * hf + i, :], R[:, i, :],
                                             ALU.add, w=[rt_[i], E["xtok"][8 * hf + i]])
        xt = [E["norm_chunk"](2 * hf + c, ["rms16"], g=W(n, "g2"),
                              source=(R[:, 4 * c:4 * c + 4, :], rt_[4 * c:4 * c + 4])) for c in range(2)]
        t_s = project("w1", xs, xt, lambda f, c, b, m: act(
            C.activation, at(gel, f, c), b.ap, ACT.Sigmoid, bias=col_("b1", f), w=[m, o]))
        t_g = act(C.activation, buf[1], buf[1], ACT.Gelu, w=[t_s])
        t_c = project("w2", xs, xt, lambda f, c, b, m: dve(
            V.scalar_tensor_tensor, at(lin, f, c), b.ap, col_("b2", f), at(gel, f, c), ALU.add, ALU.mult,
            w=[m, t_g, t_xc]))
        for t in range(8):
            m = E["to_x"](8 * hf + t, lambda k: lin[:, k, t * P:(t + 1) * P], 2, Wm["w3"], t_c,
                          bias=W(n, "b3")[0:1, :])
        done = [m, t_c, o, xt, pool.now()]
        E["finished"](n, 2 * hf)
        E["finished"](n, 2 * hf + 1)


def mamba(E, n):
    pe, act, dve, pool, T, V, C, G, ps, mm, X, xnT, W, Wk, copy = get(E)
    wt = E["wtok"][n]
    reg = E["Wr"][E["order"][n] % 2]
    _, width = offsets(SPEC[n])
    ar = E["Arena"]([(E["scr"], 0, E["NSCR"]), (reg, width, WREG)])
    u, delta, du = [ar.get(2048) for _ in range(3)]
    wide = [ar.get(2072) for _ in range(3)]
    ra, rb = Ring([w[:, 0:2048] for w in wide]), ar.ring(2048, 3)
    whole = {b: w for b, w in zip(ra.free, wide)}
    bs, cs = ar.ring(512, 2), ar.ring(512, 3)
    parts = [ar.get(256).bitcast(BF16) for _ in range(2)]
    dd = ar.get(512).rearrange("p (f m) -> p f m", f=4)
    v4 = lambda a: a.rearrange("p (f n) -> p f n", f=4)
    xts = E["inputs_of"](n)
    cd = [ar.get(512).rearrange("p (k m) -> p k m", k=4) for _ in range(4)]
    sel = ar.get(16).bitcast(BF16)
    sel = (sel, sel.unsqueeze(2).to_broadcast([P, 32, P]))
    dsum = ar.get(4)
    ident = E["ident"]
    conv = Wk(n, "conv", 4)
    for f in range(4):
        for k in range(4):
            t_cd = dve(V.tensor_scalar, cd[f][:, k, :], ident, conv[:, f, k:k + 1], None, ALU.mult,
                       w=[wt])
    t_d = dve(V.tensor_tensor, dsum, W(n, "D0"), W(n, "D1"), ALU.add)
    for f in range(4):
        t_d = dve(V.tensor_scalar, dd[:, f, :], ident, dsum[:, f:f + 1], None, ALU.mult, w=[t_d])
    t_sel = dve(V.tensor_copy, sel[0], E["K"]("sel"), w=[E["c_tok"]])
    As = []
    for d in range(2):
        a = W(n, f"A{d}")
        q = act(C.activation, a, a, ACT.Exp, w=[wt])
        t_A = dve(V.tensor_scalar, a, a, -1.0, None, ALU.mult, w=[q])
        As.append(a.rearrange("p (f n) -> p f n", f=4))
    Win, Wout = Wk(n, "Win", 2), Wk(n, "Wout", 4)
    done = []
    for c in range(4):
        xs = lambda k: xnT[:, k, c * 512:(c + 1) * 512]
        uv = v4(u)
        upb = ra.take()
        up = whole[upb].rearrange("p (f b s) -> p f b s", f=4, b=2)
        t_up = pool(G.memset, up[:, :, :, 0:3], 0.0, w=[upb.w])
        for f in range(4):
            bank = ps.take()
            m = mm(bank.ap, [(Win[:, k, f * P:(f + 1) * P], xs(k)) for k in range(2)], w=[bank.w, xts[c], wt])
            e = act(C.activation, up[:, f, :, 3:259], bank.ap.rearrange("p (b s) -> p b s", b=2), ACT.Copy,
                    w=[m, upb.w])
            ps.give(bank, e)
            bank = ps.take()
            m = mm(bank.ap, [(cd[f][:, k, :], up[:, f, :, k:k + S]) for k in range(4)], w=[bank.w, e, t_cd, t_up])
            t_u = act(C.activation, uv[:, f, :], bank.ap, ACT.Silu, bias=W(n, "bconv")[:, f:f + 1], w=[m, done])
            ps.give(bank, t_u)
        ra.give(upb, m)
        ys = [ps.take() for _ in range(4)]
        for f in range(4):
            t_y = mm(ys[f].ap, [(dd[:, f, :], uv[:, f, :])], w=[ys[f].w, t_u, t_d], last=False)
        tdir = done
        for d in range(2):
            wd, wb = Wk(n, f"Wxd{d}", 4), Wk(n, f"Wxb{d}", 4)
            a3 = rb.take()
            dtb, xbc, r1 = [a3.ap[:, 512 * i:512 * i + 512] for i in range(3)]
            tdir = [tdir, a3.w]
            bank = ps.take()
            m = mm(bank.ap[0:64, :], [(wd[:, k, :], uv[:, k, :]) for k in range(4)], w=[bank.w, t_u])
            e = copy(dtb[0:64, :], bank.ap[0:64, :], w=[m, tdir])
            ps.give(bank, e)
            bank = ps.take()
            m = mm(bank.ap[0:96, :], [(wb[:, k, :], uv[:, k, :]) for k in range(4)], w=[bank.w])
            pt = parts[d]
            q = dve(V.tensor_copy, xbc[0:96, :], bank.ap[0:96, :], w=[m, tdir])
            ps.give(bank, q)
            q = dve(V.tensor_copy, pt[0:96, :], xbc[0:96, :], w=[q, tdir])
            for lo, hi in ((32, 64), (64, 96)):
                q = dve(V.tensor_tensor, r1[lo:hi, :], xbc[lo:hi, :], pt[lo:hi, :], ALU.subtract, w=[q])
                q = dve(V.tensor_copy, pt[lo:hi, :], r1[lo:hi, :], w=[q])
            q = dve(V.tensor_tensor, r1[64:96, :], r1[64:96, :], pt[64:96, :], ALU.subtract, w=[q])
            t_p = dve(V.tensor_copy, pt[64:96, :], r1[64:96, :], w=[q])
            a1, a2 = ra.take(), rb.take()
            dv = v4(delta)
            t1 = ra.take()
            for f in range(4):
                bank = ps.take()
                m = mm(bank.ap, [(W(n, f"Wdt{d}", 64)[:, f * P:(f + 1) * P], dtb[0:64, :])], w=[bank.w, e])
                q = dve(V.tensor_scalar, v4(a1.ap)[:, f, :], bank.ap, W(n, f"bdt{d}")[:, f:f + 1], None, ALU.add,
                        w=[m, a1.w])
                ps.give(bank, q)
            t_dl = softplus(E, delta, a1.ap, t1.ap, a2.ap, [q, t1.w, a2.w, tdir])
            ra.give(a1, t_dl)
            ra.give(t1, t_dl)
            rb.give(a2, t_dl)
            rb.give(a3, t_dl, t_p)
            t_du = pool(G.tensor_tensor, du, delta, u, ALU.mult, w=[t_dl, t_u, tdir])
            hold = {}
            reset = 0 if d == 0 else S - 1

            def head(s_):
                bb, bc = ps.take(), ps.take()
                m = mm(bb.ap, [(sel[1][0:96, s_, :], parts[d][0:96, :])], w=[bb.w, t_p, t_sel])
                m2 = mm(bc.ap, [(sel[1][0:96, 16 + s_, :], parts[d][0:96, :])], w=[bc.w])
                da, db, b_, c_ = ra.take(), rb.take(), bs.take(), cs.take()
                e = act(C.activation, b_.ap, bb.ap, ACT.Copy, w=[m, b_.w])
                ps.give(bb, e)
                e2 = act(C.activation, c_.ap, bc.ap, ACT.Copy, w=[m2, c_.w])
                ps.give(bc, e2)
                for f in range(4):
                    x = act(C.activation, v4(da.ap)[:, f, :], v4(delta)[:, f, :], ACT.Exp,
                            scale=As[d][:, f, s_:s_ + 1], w=[t_dl, da.w, t_A])
                z = pool(G.memset, da.ap.rearrange("p (b s) -> p b s", s=S)[:, :, reset:reset + 1], 0.0, w=[x])
                g = pool(G.tensor_tensor, v4(db.ap), v4(du), b_.ap.unsqueeze(1).to_broadcast([P, 4, 512]),
                         ALU.mult, w=[e, t_du, db.w])
                bs.give(b_, g)
                hold[s_] = (da, db, c_, e2, z, g)

            def tail(s_):
                da, db, bc, m2, z, g = hold[s_]
                r = slice(None, None, 1 if d == 0 else -1)
                q = dve(V.tensor_tensor_scan, db.ap[:, r], da.ap[:, r], db.ap[:, r], 0.0, ALU.mult, ALU.add,
                        w=[z, g])
                q = dve(V.tensor_tensor, v4(da.ap), v4(db.ap), bc.ap.unsqueeze(1).to_broadcast([P, 4, 512]),
                        ALU.mult, w=[q, m2])
                cs.give(bc, q)
                for f in range(4):
                    m = mm(ys[f].ap, [(ident, v4(da.ap)[:, f, :])], w=[q], first=False,
                           last=(d == 1 and s_ == 15))
                ra.give(da, m)
                rb.give(db, q)
                return m

            for s_ in range(18):
                E["poll"]()
                if s_ < 16:
                    head(s_)
                if s_ > 1:
                    m = tail(s_ - 2)
            tdir = [m, pool.now(), act.now(), dve.now()]
        rs_, yb = ra.take(), rb.take()
        for f in range(4):
            bank = ps.take()
            mr = mm(bank.ap, [(Win[:, k, 512 + f * P:512 + (f + 1) * P], xs(k)) for k in range(2)], w=[bank.w])
            e = act(C.activation, v4(rs_.ap)[:, f, :], bank.ap, ACT.Silu, w=[mr, rs_.w])
            ps.give(bank, e)
            q = dve(V.scalar_tensor_tensor, v4(yb.ap)[:, f, :], ys[f].ap, 0.5, v4(rs_.ap)[:, f, :], ALU.mult,
                    ALU.mult, w=[m, e, yb.w])
            ps.give(ys[f], q)
        for j in range(4):
            mo = E["to_x"](4 * c + j, lambda k: v4(yb.ap)[:, k, j * P:(j + 1) * P], 4, Wout, [q])
        ra.give(rs_, q)
        rb.give(yb, mo)
        E["finished"](n, c)
        done = tdir


SUB = {0: mamba, 1: latent_heads, 2: experts, 3: talking, 4: few_keys, 5: moe_heads, 6: local_heads,
       7: latent_heads, 8: signs, 9: gated, 10: few_keys, 11: ternary}


def kl(w):
    k = w.shape[0] // P
    return w.reshape(k, P, -1).transpose(1, 0, 2).reshape(P, -1)


def col(v):
    return v.reshape(-1, P).T


def row(v, at=0):
    v = v.reshape(-1)
    a = np.zeros((P, v.size), v.dtype)
    a[at] = v
    return a


def top(w):
    a = np.zeros((P, w.shape[1]), w.dtype)
    a[:w.shape[0]] = w
    return a


def constants():
    c = {}
    p = np.arange(P)
    c["ident"] = np.eye(P)
    c["sel"] = (p[:, None] % 32 == np.arange(32)[None, :])
    c["hm"] = (p[:, None] // 16 == np.arange(8)[None, :])
    inv = (np.float32(1.0) / np.float32(10000.0) ** (np.arange(8, dtype=np.float32) / np.float32(8))).astype(np.float32)
    ang = np.arange(256, dtype=np.float32)[:, None] * inv[None, :]
    cos, sin = np.cos(ang.astype(np.float64)), np.sin(ang.astype(np.float64))
    two = lambda a: a.reshape(2, P, 16).transpose(1, 0, 2).reshape(P, 32)
    c["cos"] = two(np.concatenate([cos, cos], 1))
    c["sin"] = two(np.concatenate([-sin, sin], 1))
    c["jgt"] = np.broadcast_to((np.arange(8)[None, :] < np.arange(8)[:, None]).reshape(1, 64), (P, 64))
    c["one"] = np.ones((P, P))
    return np.concatenate([np.asarray(c[n], np.float32).reshape(P, w) for n, w in CONST], 1)


def window_constants():
    p = np.arange(P)
    i0, j0 = p[:, None], np.arange(128)[None, :]
    i1, j1 = p[:, None] + 128, np.arange(256)[None, :]
    part = lambda i, j: np.where((i >= j) & (i - j <= 64), (j - i).astype(np.float64), -1e33)
    dist = np.concatenate([part(i0, j0), part(i1, j1)], 1)
    r = np.arange(64)
    gsel = np.concatenate([(p[:, None] + 128 * t == 64 * (r[None, :] % 4)) for t in range(2)], 1)
    gmask = (p[:, None] // 4 == np.arange(256)[None, :] // 16)
    return [np.asarray(a, np.float32) for a in (dist, gsel, gmask)]


def blocks(n, a):
    if n == 0:
        bc = lambda w: np.concatenate([w[64:96]] * 3, 0).T
        return [kl(a["W_in"].T), top(a["fWdt"].T), top(a["bWdt"].T), kl(a["W_out"].T), kl(a["fWx"][:64].T),
                kl(a["bWx"][:64].T), kl(bc(a["fWx"])), kl(bc(a["bWx"])), kl(a["W_conv"].reshape(512, 4)),
                col(a["b_conv"]), col(a["fD"]), col(a["bD"]), col(a["fbdt"]), col(a["bbdt"]), kl(a["fA_log"]),
                kl(a["bA_log"])]
    if n == 1:
        return [kl(a["Wq"]), kl(a["Wkv"]), kl(a["Wout"]), col(a["ln_m_g"]), col(a["ln_m_b"]), col(a["ln_l_g"]),
                col(a["ln_l_b"])]
    if n == 2:
        b2 = top(a["rb2"])
        b2[8] = a["sb2"]
        return [kl(a["router_w"]), row(a["router_b"]), np.concatenate([col(a["rb1"].reshape(-1)), col(a["sb1"])], 1),
                b2]
    if n == 3:
        w = a["w_qkv"]
        return [kl(w[:, :512]), kl(w[:, 512:]), kl(a["w_out"].T), kl(np.repeat(a["w_pre"].T, 16, 0)),
                np.broadcast_to(a["w_post"].T.reshape(1, 256), (P, 256)), row(a["b_out"])]
    if n == 4:
        return [kl(a["Wq"].T), kl(a["Wk"].T), kl(a["Wv"].T), kl(a["Wo"].T), col(a["bq"]), col(a["bk"]), row(a["bv"]),
                row(a["bo"]), kl(a["fside"])]
    if n == 5:
        we = np.concatenate([np.concatenate([kl(a[m][e]) for m in ("Wq", "Wk", "Wv")], 1) for e in range(4)], 1)
        bqk = np.concatenate([np.concatenate([col(a["bq"][e]), col(a["bk"][e])], 1) for e in range(4)], 1)
        return [we, kl(a["Wo"]), kl(a["Wg1"]), kl(a["Wg2"]), col(a["bg1"]), row(a["bg2"]), bqk, row(a["bv"]),
                row(a["bo"])]
    if n == 6:
        c = window_constants()
        return [kl(np.concatenate([a["Wq"], a["Wk"]], 1)), kl(a["Wv"]), kl(a["Wo"])] + c
    if n == 7:
        return [kl(np.concatenate([a["W_q"], a["W_kv"][:, :256]], 1)), kl(a["W_kv"][:, 256:]), kl(a["W_out"]),
                col(a["ln_x_g"]), col(a["ln_x_b"]), col(a["ln_l_g"]), col(a["ln_l_b"]),
                col(np.concatenate([a["q_gamma"]] * 2)), col(np.concatenate([a["k_gamma"]] * 2)), row(a["b_out"])]
    if n == 9:
        ws = ["W_lin", "W_conv", "Wa", "Wx", "W_lin2", "W1", "W2", "W3"]
        bs = ["b_lin", "b_conv", "ba", "bx", "b1", "b2"]
        return [kl(a[w].T) for w in ws] + [col(a[b]) for b in bs] + [row(a["b_lin2"]), row(a["b3"]), col(a["g1"]),
                                                                     col(a["g2"]), col(a["Lam"])]
    if n == 10:
        return [kl(a[w].reshape(256, 1024)) for w in ("wq", "wk", "wv")] + [kl(a["wo"].reshape(1024, 256)),
                                                                          row(a["bo"])]
    if n == 11:
        return [kl(a["w_up"].T), kl(a["w_down"].T)]
    return None


NAMES = {0: "L0_attn_", 1: "L0_xattn_", 2: "L0_ffn_", 3: "L1_attn_", 4: "L1_xattn_", 5: "L1_ffn_", 6: "L2_attn_",
         7: "L2_xattn_", 8: "L2_ffn_", 9: "L3_attn_", 10: "L3_xattn_", 11: "L3_ffn_"}


def kernel(**inputs):
    import numpy as _np
    import concourse.bacc as _bacc
    from concourse import mybir as _mybir
    from concourse.bass_utils import run_bass_kernel_spmd as _run

    inp = {k: _np.asarray(v) for k, v in inputs.items()}
    arrays = {"const": constants(), "x": inp["x"], "ctx": inp["ctx_1024"]}
    for n in LAYERS:
        a = {k[len(NAMES[n]):]: v for k, v in inp.items() if k.startswith(NAMES[n])}
        a["fside"] = inp["fside_SxS2_0"]
        b = blocks(n, a)
        if b is not None:
            for (name, w), arr in zip(SPEC[n], b):
                assert arr.shape == (P, w), (n, name, arr.shape)
            arrays[f"w{n}"] = _np.concatenate(b, 1)
        if n == 2:
            arrays["we"] = _np.stack([_np.concatenate([kl(a["rw1"][e]), kl(a["rw2"][e])], 1) for e in range(8)]
                                     + [_np.concatenate([kl(a["sw1"]), kl(a["sw2"])], 1)])
        if n == 4:
            arrays["mbf"] = inp["mask_BxS2_bf0"]
        if n == 7:
            arrays["mbk"] = inp["mask_BxS2_bk0"]
        if n == 8:
            arrays["k0"] = kl(a["k0"])
            arrays["k1"] = kl(a["k1"])
            arrays["k2"] = kl(a["k2"])
            arrays["s"] = _np.broadcast_to(_np.stack([a["s0"], a["s1"], a["s2"]]).reshape(1, 3), (P, 3))
    nc = _bacc.Bacc("TRN2", target_bir_lowering=False, num_devices=1)
    maps, A = {}, {}
    for name, arr in arrays.items():
        arr = _np.ascontiguousarray(arr)
        maps[f"in_{name}"] = arr
        A[name] = nc.dram_tensor(f"in_{name}", arr.shape, _mybir.dt.from_np(arr.dtype), kind="ExternalInput").ap()
    out = nc.dram_tensor("out_0", (NB, S, D), F32, kind="ExternalOutput").ap()
    build(nc, A, out)
    r = _run(nc, [maps], core_ids=[0])
    return r.results[0]["out_0"]
```

```python
from contextlib import ExitStack

import concourse.bass as bass
import numpy as np
from concourse import mybir

LAYERS = [0, 1, 2, 3, 4, 5, 6, 7, 8, 9, 10, 11]

P = 128
NB = 8
S = 256
D = 256
NT = 16
S2 = 77
WREG = 8448
F32 = mybir.dt.float32
BF16 = mybir.dt.bfloat16
U8 = mybir.dt.uint8
ALU = mybir.AluOpType
ACT = mybir.ActivationFunctionType
AX = mybir.AxisListType

SPEC = {
    0: [("Win", 2048), ("Wdt0", 512), ("Wdt1", 512), ("Wout", 1024), ("Wxd0", 256), ("Wxd1", 256),
        ("Wxb0", 384), ("Wxb1", 384), ("conv", 16), ("bconv", 4), ("D0", 4), ("D1", 4), ("bdt0", 4), ("bdt1", 4),
        ("A0", 64), ("A1", 64)],
    1: [("Wq", 2048), ("Wkv", 4096), ("Wout", 2048), ("mg", 2), ("mb", 2), ("lg", 2), ("lb", 2)],
    2: [("rw", 16), ("rb", 8), ("b1", 36), ("b2", 256)],
    3: [("Wqk", 1024), ("Wv", 512), ("Wout", 512), ("wpre", 32), ("wpost", 256), ("bo", 256)],
    4: [("Wq", 512), ("Wk", 512), ("Wv", 512), ("Wo", 512), ("bq", 2), ("bk", 2), ("bv", 256), ("bo", 256),
        ("am", 154)],
    5: [("We", 6144), ("Wo", 512), ("Wg1", 256), ("Wg2", 4), ("bg1", 1), ("bg2", 4), ("bqk", 16), ("bv", 1024),
        ("bo", 256)],
    6: [("Wqk", 1024), ("Wv", 512), ("Wo", 512), ("dist", 384), ("gsel", 128), ("gmask", 256)],
    7: [("Wqk", 1024), ("Wv", 512), ("Wo", 512), ("xg", 2), ("xb", 2), ("lg", 2), ("lb", 2), ("gq", 1), ("gk", 1),
        ("bo", 256)],
    8: [],
    9: [("lin", 512), ("conv", 512), ("a", 512), ("x", 512), ("lin2", 512), ("w1", 512), ("w2", 512), ("w3", 512),
        ("blin", 2), ("bconv", 2), ("ba", 2), ("bx", 2), ("b1", 2), ("b2", 2), ("blin2", 256), ("b3", 256),
        ("g1", 2), ("g2", 2), ("lam", 2)],
    10: [("wq", 2048), ("wk", 2048), ("wv", 2048), ("wo", 2048), ("bo", 256)],
    11: [("up", 2048), ("down", 2048)],
}
CONST = [("ident", 128), ("sel", 32), ("hm", 8), ("cos", 32), ("sin", 32), ("jgt", 64), ("one", 128), ("lg1", 2), ("lb1", 2)]


def offsets(spec):
    at, out = 0, {}
    for name, n in spec:
        out[name] = (at, n)
        at += n
    return out, at


class Line:

    def __init__(self, sem):
        self.sem, self.n, self.items, self.seen = sem, 0, [], {}

    def wait(self, toks):
        for t in toks:
            if t is None or t == ():
                continue
            if isinstance(t, list):
                self.wait(t)
                continue
            sem, value = t
            if self.seen.get(id(sem), 0) < value:
                self.seen[id(sem)] = value
                self.items.append((sem, value))

    def __call__(self, f, *args, w=(), sig=True, **kw):
        self.wait(list(w))
        self.n += 1 if sig else 0
        self.items.append((f, args, kw, self.sem if sig else None, 1))
        return (self.sem, self.n)

    def now(self):
        return (self.sem, self.n)

    def play(self, eng):
        for it in self.items:
            if len(it) == 2:
                eng.wait_ge(it[0], it[1])
                continue
            f, args, kw, sem, by = it
            ins = f(*args, **kw)
            if sem is not None:
                ins.then_inc(sem, by)


class Buf:
    def __init__(self, ap):
        self.ap, self.w = ap, []


class Ring:

    def __init__(self, aps):
        self.free = [Buf(a) for a in aps]

    def take(self):
        return self.free.pop(0)

    def give(self, b, *toks):
        b.w = list(toks)
        self.free.append(b)


def build(nc, A, out):
    ctx = ExitStack()
    with ctx:
        def sb(name, n, dt=F32):
            return ctx.enter_context(nc.sbuf_tensor(name, [P, n], dt))

        pe, act, dve, pool, sp = [Line(ctx.enter_context(nc.semaphore("s_" + n)))
                                  for n in ("pe", "act", "dve", "pool", "sp")]
        T, V, C, G = nc.tensor, nc.vector, nc.scalar, nc.gpsimd

        dsem = [ctx.enter_context(nc.semaphore(f"dma{i}")) for i in range(32)]
        dcount = [0]

        def dma(dst, src, w=()):
            i = dcount[0]
            dcount[0] += 1
            sem, k = dsem[i % 32], i // 32
            sp.wait([(sem, 16 * k)] if k else [])
            sp.wait(list(w))
            sp.items.append((nc.sync.dma_start, (dst, src), {}, sem, 16))
            return (sem, 16 * (k + 1))

        X = sb("X", NT * D)[:, :].rearrange("p (t d) -> p t d", t=NT)
        xnT = sb("xnT", 2 * 2048)[:, :].rearrange("p (k n) -> p k n", k=2)
        XNr = sb("XNr", 2 * 1024)
        stat = sb("stat", 2 * 64)
        Wr = [sb("W0", WREG), sb("W1", WREG)]
        coff, cw = offsets(CONST)
        cst = sb("cst", cw)
        ctxT = sb("ctxT", 2 * 616)[:, :].rearrange("p (k n) -> p k n", k=2)
        cnT = sb("cnT", 2 * 616)[:, :].rearrange("p (k n) -> p k n", k=2)
        NSCR = 23040
        scr = sb("scr", NSCR)
        PS = ctx.enter_context(nc.psum_tensor("PS", [P, 8, 512], F32))
        ps = Ring([PS[:, i, :] for i in range(8)])
        xn_ring = Ring([XNr[:, i * 1024:(i + 1) * 1024].rearrange("p (t d) -> p t d", t=4) for i in range(2)])
        st_ring = Ring([stat[:, i * 64:(i + 1) * 64] for i in range(2)])

        def K(name, rows=P):
            o, n = coff[name]
            return cst[0:rows, o:o + n]

        ident = K("ident")
        ones = K("one")

        class Arena:
            def __init__(self, segs):
                self.segs = list(segs)

            def get(self, n):
                for i, (t, lo, hi) in enumerate(self.segs):
                    if hi - lo >= n:
                        self.segs[i] = (t, lo + n, hi)
                        return t[:, lo:lo + n]
                raise ValueError(f"arena: {n} of {[(b - a) for _, a, b in self.segs]}")

            def ring(self, n, count):
                return Ring([self.get(n) for _ in range(count)])

        c_tok = dma(cst[:, :], A["const"])
        xv = A["x"].rearrange("b (h p) d -> p (b h) d", p=P)
        xtok = [None] * NT
        for c in range(4):
            t = dma(X[:, 4 * c:4 * c + 4, :], xv[:, 4 * c:4 * c + 4, :])
            for j in range(4):
                xtok[4 * c + j] = t

        bars = []

        def barrier():
            toks = [e.now() for e in (pe, act, dve, pool) if e.n]
            for e in (pe, act, dve, pool):
                e.wait(toks)
            bars.append(toks)
            return toks

        wtok = {}

        def load_weights(n, w):
            off, width = offsets(SPEC[n])
            if width:
                wtok[n] = dma(Wr[order[n] % 2][:, 0:width], A[f"w{n}"], w)

        order = {n: i for i, n in enumerate(LAYERS)}

        def W(n, name, rows=P):
            off, _ = offsets(SPEC[n])
            o, k = off[name]
            return Wr[order[n] % 2][0:rows, o:o + k]

        def Wk(n, name, kt):
            return W(n, name).rearrange("p (k f) -> p k f", k=kt)

        def mm(o, pairs, w=(), first=True, last=True, sig=True):
            for i, (l, r) in enumerate(pairs):
                t = pe(T.matmul, o, l, r, start=(first and i == 0), stop=(last and i == len(pairs) - 1),
                       w=w if i == 0 else (), sig=sig and i == len(pairs) - 1)
            return t

        flip = [0]

        def copy(o, i, w=(), on=None):
            if on is None:
                flip[0] ^= 1
                on = act if flip[0] else dve
            if on is act:
                return act(C.activation, o, i, ACT.Copy, w=w)
            return on(V.tensor_copy, o, i, w=w)

        cz = sb("cz", 8)
        z_tok = dve(V.memset, cz[:, 0:1], 1e-5)
        z_tok = dve(V.memset, cz[:, 1:2], 1.0)
        eps_ap = cz[:, 0:1]
        one_ap = cz[:, 1:2]

        def normalise_steps(dst, src, n, rows, kind, w, st, tile_w=None):
            mv = st.ap[0:rows, 0:2 * n].rearrange("p (t s) -> p t s", s=2)
            bs = st.ap[0:rows, 8:8 + 6 * n].rearrange("p (t s) -> p t s", s=6)
            sd = st.ap[0:rows, 40:40 + n]
            rs = st.ap[0:rows, 48:48 + n]
            ms = st.ap[0:rows, 56:56 + n]
            for j in range(n):
                wj = w if tile_w is None else [w, tile_w[j]]
                t = dve(V.bn_stats, bs[:, j, :], src[:, j, :], w=[st.w, wj])
            for j in range(n):
                t = dve(V.bn_aggr, mv[:, j, :], bs[:, j, :], w=[t])
            yield None
            if kind == "ln":
                t = act(C.activation, sd, mv[:, :, 1], ACT.Sqrt, bias=eps_ap[0:rows], w=[t, z_tok])
                yield None
                t = dve(V.reciprocal, rs, sd, w=[t])
                for j in range(n):
                    t = dve(V.tensor_scalar, dst[:, j, :], src[:, j, :], mv[:, j, 0:1], rs[:, j:j + 1],
                            ALU.subtract, ALU.mult, w=[t])
            else:
                t = dve(V.tensor_tensor, ms, mv[:, :, 0], mv[:, :, 0], ALU.mult, w=[t])
                t = dve(V.tensor_tensor, ms, ms, mv[:, :, 1], ALU.add, w=[t])
                yield None
                if kind == "rms16":
                    t = act(C.activation, sd, ms, ACT.Sqrt, scale=256.0, w=[t])
                    yield None
                    t = dve(V.tensor_scalar, sd, sd, 1e-12, 0.0625, ALU.max, ALU.mult, w=[t])
                else:
                    t = act(C.activation, sd, ms, ACT.Sqrt, w=[t])
                    yield None
                    t = dve(V.tensor_scalar, sd, sd, 1e-8, None, ALU.add, w=[t])
                t = dve(V.reciprocal, rs, sd, w=[t])
                for j in range(n):
                    t = dve(V.tensor_scalar, dst[:, j, :], src[:, j, :], rs[:, j:j + 1], None, ALU.mult, w=[t])
            yield t

        def normalise(*args):
            for t in normalise_steps(*args):
                pass
            return t

        def norm_steps(c, toks, kinds, g=None, b=None, w=(), source=None):
            xb, st = xn_ring.take(), st_ring.take()
            src, t = X[:, 4 * c:4 * c + 4, :], [xb.w, w]
            tw = xtok[4 * c:4 * c + 4]
            if source is not None:
                src, tw = source
            for kind in kinds:
                for r in normalise_steps(xb.ap, src, 4, P, kind, [t], st, tw):
                    yield
                t = r
                src, tw = xb.ap, None
            st_ring.give(st, t)
            for k in range(2):
                bank = ps.take()
                for j in range(4):
                    tt = pe(T.transpose, bank.ap[:, j * P:(j + 1) * P], xb.ap[:, j, k * P:(k + 1) * P], ident,
                            w=[t, bank.w, c_tok], sig=j == 3)
                o = xnT[:, k, c * 512:(c + 1) * 512]
                if g is not None:
                    e = act(C.activation, o, bank.ap, ACT.Identity, scale=g[:, k:k + 1],
                            bias=b[:, k:k + 1] if b is not None else 0.0, w=[tt, w])
                else:
                    e = copy(o, bank.ap, w=[tt])
                ps.give(bank, e)
                toks.append(e)
            xn_ring.give(xb, tt)

        def norm_chunk(c, kinds, **kw):
            toks = []
            for _ in norm_steps(c, toks, kinds, **kw):
                pass
            return toks

        NORM = {1: (["ln", "ln"], "lg", "lb"), 7: (["ln", "ln"], "lg", "lb"), 11: (["ln", "rms"],)}
        ahead = {}
        running = []

        def start_norm(n, c):
            kinds, *gb = NORM.get(n, (["ln"],))
            toks = []
            if n == 1:
                kw = dict(g=K("lg1"), b=K("lb1"), w=[c_tok])
            else:
                kw = dict(g=W(n, gb[0]), b=W(n, gb[1]), w=[wtok[n]]) if gb else {}
            running.append(norm_steps(c, toks, kinds, **kw))
            ahead[(n, c)] = toks

        def poll():
            for g in list(running):
                if next(g, "end") == "end":
                    running.remove(g)

        def finished(n, c):
            i = order[n] + 1
            if i < len(LAYERS) and LAYERS[i] != 9:
                while len(running) >= 2:
                    poll()
                start_norm(LAYERS[i], c)

        def inputs_of(n, chunks=range(4)):
            for c in chunks:
                if (n, c) not in ahead:
                    while len(running) >= 2:
                        poll()
                    start_norm(n, c)
                    if c % 2:
                        while running:
                            poll()
            while running:
                poll()
            return [ahead[(n, c)] for c in chunks]

        def to_x(t, yT, kt, Wo, w, bias=None, scale=None, onto=None):
            bank = ps.take()
            pairs = [(yT(k), Wo[:, k, :]) for k in range(kt)]
            if bias is not None:
                pairs.append((ones[0:1, :], bias))
            m = mm(bank.ap[:, 0:D], pairs, w=[w, bank.w])
            if onto is not None:
                e = dve(V.tensor_tensor, onto[0], onto[0], bank.ap[:, 0:D], ALU.add, w=[m, onto[1]])
                ps.give(bank, e)
                return e
            if scale is None:
                xtok[t] = dve(V.tensor_tensor, X[:, t, :], X[:, t, :], bank.ap[:, 0:D], ALU.add, w=[m, xtok[t]])
            else:
                xtok[t] = dve(V.scalar_tensor_tensor, X[:, t, :], bank.ap[:, 0:D], scale, X[:, t, :], ALU.mult,
                              ALU.add, w=[m, xtok[t]])
            ps.give(bank, xtok[t])
            return m

        env = dict(nc=nc, T=T, V=V, C=C, G=G, pe=pe, act=act, dve=dve, pool=pool, dma=dma, X=X, xnT=xnT, ps=ps, A=A,
                   K=K, ident=ident, ones=ones, Arena=Arena, W=W, Wk=Wk, mm=mm, copy=copy, one_ap=one_ap,
                   eps_ap=eps_ap, z_tok=z_tok, normalise=normalise, norm_chunk=norm_chunk, to_x=to_x, xtok=xtok,
                   wtok=wtok, scr=scr, NSCR=NSCR, Wr=Wr, order=order, c_tok=c_tok, ctxT=ctxT, cnT=cnT,
                   barrier=barrier, XNr=XNr, poll=poll, start_norm=start_norm, ahead=ahead, finished=finished, inputs_of=inputs_of, st_ring=st_ring, xn_ring=xn_ring, PS=PS, bars=bars)
        env["ctx_tok"] = None
        if any(n in LAYERS for n in (1, 4, 7, 10)):
            env["ctx_tok"] = load_context(env)
        load_weights(LAYERS[0], [])
        for i, n in enumerate(LAYERS):
            b = barrier()
            after = LAYERS[i + 1] if i + 1 < len(LAYERS) else None
            env["late_weights"] = lambda w: load_weights(after, w) if after is not None else None
            if n != 0:
                env["late_weights"](b)
            SUB[n](env, n)
        dones = []
        for c in range(4):
            ov = out.rearrange("b (h p) d -> p (b h) d", p=P)
            dones.append(dma(ov[:, 4 * c:4 * c + 4, :], X[:, 4 * c:4 * c + 4, :], xtok[4 * c:4 * c + 4]))
        sp.wait(dones)
        for i, s in enumerate(dsem):
            n = (dcount[0] - i + 31) // 32
            if n > 0:
                sp.wait([(s, 16 * n)])
        block = ctx.enter_context(nc.Block())
        block.sync(lambda e: sp.play(e))
        block.tensor(lambda e: pe.play(e))
        block.scalar(lambda e: act.play(e))
        block.vector(lambda e: dve.play(e))
        block.gpsimd(lambda e: pool.play(e))


def load_context(E):
    pe, T, V, dve, ps, dma = E["pe"], E["T"], E["V"], E["dve"], E["ps"], E["dma"]
    ar = E["Arena"]([(E["scr"], 0, E["NSCR"])])
    raw = ar.get(8 * D).rearrange("p (t d) -> p t d", t=8)
    nrm = ar.get(8 * D).rearrange("p (t d) -> p t d", t=8)
    ld = dma(raw[0:S2, :, :], E["A"]["ctx"].rearrange("b s d -> s b d"))
    st = E["st_ring"].take()
    toks = []
    t = []
    for h in range(2):
        t = E["normalise"](nrm[0:S2, 4 * h:4 * h + 4, :], raw[0:S2, 4 * h:4 * h + 4, :], 4, S2, "ln", [ld, t], st)
    E["st_ring"].give(st, t)
    for src, dst, w in ((raw, E["ctxT"], ld), (nrm, E["cnT"], t)):
        for k in range(2):
            for h in range(2):
                bank = ps.take()
                for j in range(4):
                    m = pe(T.transpose, bank.ap[:, j * S2:(j + 1) * S2], src[0:S2, 4 * h + j, k * P:(k + 1) * P],
                           E["ident"][0:S2, 0:S2], w=[w, bank.w, E["c_tok"]], sig=j == 3)
                e = E["copy"](dst[:, k, 4 * h * S2:4 * (h + 1) * S2], bank.ap[:, 0:4 * S2], w=[m])
                ps.give(bank, e)
                toks.append(e)
    return toks


def ternary(E, n):
    pe, act, dve, pool, T, V, C, ps = E["pe"], E["act"], E["dve"], E["pool"], E["T"], E["V"], E["C"], E["ps"]
    mm, X, xnT, wt = E["mm"], E["X"], E["xnT"], E["wtok"][n]
    ar = E["Arena"]([(E["scr"], 0, E["NSCR"])])
    small = ar.get(16)
    tmp = [ar.get(2048) for _ in range(3)]
    ready = []
    t = None
    for m, name in enumerate(("up", "down")):
        w = E["W"](n, name)
        q = dve(V.tensor_reduce, tmp[0][:, 0:64], w.rearrange("p (a b) -> p a b", a=64), AX.X, ALU.add,
                apply_absolute_value=True, w=[wt, t])
        q = dve(V.tensor_reduce, small[:, m:m + 1], tmp[0][:, 0:64], AX.X, ALU.add, w=[q])
        bank = ps.take()
        q = mm(bank.ap[:, 0:1], [(E["ones"], small[:, m:m + 1])], w=[q, bank.w])
        th = small[:, 4 + m:5 + m]
        q = dve(V.tensor_scalar, th, bank.ap[:, 0:1], 0.5 / (1024 * 256), None, ALU.mult, w=[q])
        ps.give(bank, q)
        a, s, g = tmp
        q1 = act(C.activation, a, w, ACT.Abs, w=[wt, t, q])
        q2 = act(C.activation, s, w, ACT.Sign, w=[wt, t])
        q = dve(V.scalar_tensor_tensor, g, a, th, s, ALU.is_gt, ALU.mult, w=[q, q1, q2, t])
        q = dve(V.tensor_tensor, g, g, w, ALU.subtract, w=[q])
        t = dve(V.tensor_tensor, w, w, g, ALU.add, w=[q])
        ready.append(t)
    up = E["Wk"](n, "up", 2)
    down = E["Wk"](n, "down", 8)
    hs = ar.ring(4096, 2)
    sq = ar.ring(4096, 1)
    prev = None

    def second(c, hb, ht):
        h = hb.ap.rearrange("p (f n) -> p f n", f=8)
        qb = sq.take()
        q = qb.ap.rearrange("p (f n) -> p f n", f=8)
        qt = pool(E["G"].tensor_tensor, qb.ap, hb.ap, hb.ap, ALU.mult, w=[ht, qb.w])
        for j in range(4):
            tl = 4 * c + j
            bank = ps.take()
            s1 = mm(bank.ap[:, 0:D], [(h[:, k, j * P:(j + 1) * P], down[:, k, :]) for k in range(8)],
                    w=[bank.w, ht, ready[1]])
            s2 = mm(bank.ap[:, 256:257], [(q[:, k, j * P:(j + 1) * P], E["ones"][:, 0:1]) for k in range(8)], w=[qt])
            r = small[:, 8 + 2 * (tl % 2):9 + 2 * (tl % 2)]
            r2 = small[:, 9 + 2 * (tl % 2):10 + 2 * (tl % 2)]
            u = act(C.activation, r, bank.ap[:, 256:257], ACT.Sqrt, scale=1.0 / 1024, w=[s2, E["xtok"][tl - 2]])
            u = dve(V.tensor_scalar, r, r, 1e-8, None, ALU.add, w=[u])
            u = dve(V.reciprocal, r2, r, w=[u])
            E["xtok"][tl] = dve(V.scalar_tensor_tensor, X[:, tl, :], bank.ap[:, 0:D], r2, X[:, tl, :], ALU.mult,
                                ALU.add, w=[u, s1, E["xtok"][tl]])
            ps.give(bank, E["xtok"][tl])
        sq.give(qb, s2)
        hs.give(hb, s1, qt)

    xts = E["inputs_of"](n)
    for c in range(4):
        xt = xts[c]
        hb = hs.take()
        h = hb.ap.rearrange("p (f n) -> p f n", f=8)
        for f in range(8):
            bank = ps.take()
            m = mm(bank.ap, [(up[:, k, f * P:(f + 1) * P], xnT[:, k, c * 512:(c + 1) * 512]) for k in range(2)],
                   w=[bank.w, xt, ready[0]])
            ht = act(C.activation, h[:, f, :], bank.ap, ACT.Gelu, w=[m, hb.w])
            ps.give(bank, ht)
        if prev:
            second(*prev)
        prev = (c, hb, ht)
    second(*prev)


def signs(E, n):
    pe, act, dve, pool, T, V, C, G, ps = [E[k] for k in ("pe", "act", "dve", "pool", "T", "V", "C", "G", "ps")]
    mm, X, xnT, A, dma = E["mm"], E["X"], E["xnT"], E["A"], E["dma"]
    reg = E["Wr"][E["order"][n] % 2]
    ar = E["Arena"]([(E["scr"], 0, E["NSCR"]), (reg, 0, WREG)])
    sc = ar.get(8)
    w1 = ar.get(8192)
    hr = ar.ring(4096, 2)
    raw0, w0 = ar.get(1024), ar.get(2048)
    w2 = ar.get(2048)
    raw1, raw2 = ar.get(2048), ar.get(512)
    bar = E["bars"][-1]
    t0 = dma(raw0.bitcast(U8), A["k0"], bar)
    t1 = dma(raw1.bitcast(U8), A["k1"], bar)
    t2 = dma(raw2.bitcast(U8), A["k2"], bar)
    ts = dma(sc[:, 0:3], A["s"], bar)
    k0 = raw0.bitcast(U8).rearrange("p (h n) -> p h n", h=2)
    q = dve(V.tensor_tensor, w0, k0[:, 0, :], k0[:, 1, :], ALU.subtract, w=[t0])
    r0 = dve(V.tensor_scalar, w0, w0, 2.0, None, ALU.mult, w=[q])
    r1 = dve(V.tensor_scalar, w1, raw1.bitcast(U8), 2.0, -1.0, ALU.mult, ALU.add, w=[t1])
    r2 = dve(V.tensor_scalar, w2, raw2.bitcast(U8), 2.0, -1.0, ALU.mult, ALU.add, w=[t2])
    rs = dve(V.tensor_scalar, sc[:, 4:6], sc[:, 0:2], 2.0, None, ALU.mult, w=[ts])
    w0, w1, w2 = [a.rearrange("p (k f) -> p k f", k=k) for a, k in ((w0, 2), (w1, 8), (w2, 8))]

    def relu(o, bank, s, w, f):
        if f % 2:
            return act(C.activation, o, bank.ap, ACT.Relu, scale=sc[:, 4 + s:5 + s], w=w)
        return dve(V.tensor_scalar, o, bank.ap, sc[:, 4 + s:5 + s], 0.0, ALU.mult, ALU.max, w=w)

    xts = E["inputs_of"](n)
    for c in range(4):
        E["poll"]()
        xt = xts[c]
        cur, ht = None, xt
        for s, (wm, kt) in enumerate(((w0, 2), (w1, 8))):
            hb = hr.take()
            h = hb.ap.rearrange("p (f n) -> p f n", f=8)
            es = []
            for f in range(8):
                E["poll"]()
                bank = ps.take()
                m = mm(bank.ap, [(wm[:, k, f * P:(f + 1) * P],
                                  xnT[:, k, c * 512:(c + 1) * 512] if s == 0 else cur[:, k, :]) for k in range(kt)],
                       w=[bank.w, ht, r0, r1])
                e = relu(h[:, f, :], bank, s, [m, hb.w, rs], f)
                ps.give(bank, e)
                es.append(e)
            if s:
                hr.give(pb, m)
            pb, cur, ht = hb, h, es
        for j in range(4):
            m = E["to_x"](4 * c + j, lambda k: cur[:, k, j * P:(j + 1) * P], 8, w2, [ht, r2], scale=sc[:, 2:3])
        hr.give(pb, m)
        E["finished"](n, c)


def experts(E, n):
    pe, act, dve, pool, T, V, C, G, ps = [E[k] for k in ("pe", "act", "dve", "pool", "T", "V", "C", "G", "ps")]
    mm, X, xnT, A, dma, W = E["mm"], E["X"], E["xnT"], E["A"], E["dma"], E["W"]
    reg = E["Wr"][E["order"][n] % 2]
    _, width = offsets(SPEC[n])
    ar = E["Arena"]([(E["scr"], 0, E["NSCR"]), (reg, width, WREG)])
    ring = ar.ring(2048, 4)
    hr = ar.ring(2048, 2)
    bar = E["bars"][-1]
    wt = E["wtok"][n]
    lg = ar.get(NT * 8).rearrange("p (t e) -> p t e", e=8)
    pr = ar.get(NT * 8).rearrange("p (t e) -> p t e", e=8)
    wg = ar.get(NT * 9).rearrange("p (t e) -> p t e", e=9)
    mx = ar.get(NT)
    sm = ar.get(NT)
    cmp1, cmp2 = ar.get(512), ar.get(512)
    wT = ar.get(2048)
    slots = []

    def load(e):
        b = ring.take()
        slots.append((b, dma(b.ap, A["we"][e], [bar, b.w])))

    for e in range(3):
        load(e)
    rw = W(n, "rw").rearrange("p (k e) -> p k e", k=2)
    xts = E["inputs_of"](n)
    bank = ps.take()
    for t in range(NT):
        m = mm(bank.ap[:, t * 8:t * 8 + 8], [(xnT[:, k, t * P:(t + 1) * P], rw[:, k, :]) for k in range(2)]
               + [(E["ones"][0:1, :], W(n, "rb")[0:1, :])], w=[bank.w, xts[t // 4], wt])
    lv = bank.ap[:, 0:128].rearrange("p (t e) -> p t e", e=8)
    t = dve(V.tensor_reduce, mx, lv, AX.X, ALU.max, w=[m])
    t = dve(V.tensor_tensor, lg, lv, mx.unsqueeze(2).to_broadcast([P, NT, 8]), ALU.subtract, w=[t])
    ps.give(bank, t)
    t = act(C.activation, pr, lg, ACT.Exp, w=[t])
    t = dve(V.tensor_reduce, sm, pr, AX.X, ALU.add, w=[t])
    t = dve(V.reciprocal, mx, sm, w=[t])
    t = dve(V.tensor_tensor, pr, pr, mx.unsqueeze(2).to_broadcast([P, NT, 8]), ALU.mult, w=[t])
    jgt = E["K"]("jgt").rearrange("p (e j) -> p e j", e=8)
    rk = ar.get(NT * 8).rearrange("p (t e) -> p t e", e=8)
    for g in range(2):
        c1 = cmp1.rearrange("p (t e) -> p t e", t=8)
        c2 = cmp2.rearrange("p (t e) -> p t e", t=8)
        pv = pr[:, 8 * g:8 * g + 8, :]
        for e in range(8):
            me = pv[:, :, e:e + 1].to_broadcast([P, 8, 8])
            a1, a2 = c1[:, :, 0:8], c2[:, :, 0:8]
            q = dve(V.tensor_tensor, a1, pv, me, ALU.is_gt, w=[t])
            q = dve(V.tensor_tensor, a2, pv, me, ALU.is_equal, w=[q, t])
            q = dve(V.tensor_tensor, a2, a2, jgt[:, e, :].unsqueeze(1).to_broadcast([P, 8, 8]), ALU.mult, w=[q])
            q = dve(V.tensor_tensor, a1, a1, a2, ALU.add, w=[q])
            t = dve(V.tensor_reduce, rk[:, 8 * g:8 * g + 8, e], a1, AX.X, ALU.add, w=[q])
    t1 = dve(V.memset, wg[:, :, 8:9], 1.0)
    t = dve(V.scalar_tensor_tensor, wg[:, :, 0:8], rk, 1.5, pr, ALU.is_lt, ALU.mult, w=[t])
    for g in range(4):
        bank = ps.take()
        for j in range(4):
            m = pe(T.transpose, bank.ap[0:9, j * P:(j + 1) * P], wg[:, 4 * g + j, :], E["ident"], w=[t, t1, bank.w],
                   sig=j == 3)
        wtt = dve(V.tensor_copy, wT[0:9, g * 512:(g + 1) * 512], bank.ap[0:9, :], w=[m])
        ps.give(bank, wtt)
    b1 = W(n, "b1")

    def second(e, c, hb, ht, w2):
        h = hb.ap.rearrange("p (f n) -> p f n", f=4)
        for j in range(4):
            tl = 4 * c + j
            if e < 8:
                m = E["to_x"](tl, lambda k: h[:, k, j * P:(j + 1) * P], 4, w2, [ht, t], scale=wg[:, tl, e:e + 1])
            else:
                b = ps.take()
                b2 = W(n, "b2")
                m = mm(b.ap[:, 0:D], [(h[:, k, j * P:(j + 1) * P], w2[:, k, :]) for k in range(4)]
                       + [(wT[0:9, tl * P:(tl + 1) * P], b2[0:9, :])],
                       w=[ht, wtt, b.w])
                E["xtok"][tl] = dve(V.tensor_tensor, X[:, tl, :], X[:, tl, :], b.ap[:, 0:D], ALU.add,
                                    w=[m, E["xtok"][tl]])
                ps.give(b, E["xtok"][tl])
        hr.give(hb, m)
        if e == 8:
            E["finished"](n, c)
        return m

    prev = None
    for e in range(9):
        sb_, st = slots[e]
        w1 = sb_.ap[:, 0:1024].rearrange("p (k f) -> p k f", k=2)
        w2 = sb_.ap[:, 1024:2048].rearrange("p (k f) -> p k f", k=4)
        for c in range(4):
            hb = hr.take()
            h = hb.ap.rearrange("p (f n) -> p f n", f=4)
            for f in range(4):
                E["poll"]()
                bank = ps.take()
                m = mm(bank.ap, [(w1[:, k, f * P:(f + 1) * P], xnT[:, k, c * 512:(c + 1) * 512]) for k in range(2)],
                       w=[bank.w, st, xts[c]])
                ht = act(C.activation, h[:, f, :], bank.ap, ACT.Gelu, bias=b1[:, 4 * e + f:4 * e + f + 1],
                         w=[m, hb.w])
                ps.give(bank, ht)
            if prev:
                m2 = second(*prev)
                if c == 0:
                    ring.give(slots[e - 1][0], m2)
                    if e + 2 < 9:
                        load(e + 2)
            prev = (e, c, hb, ht, w2)
    second(*prev)


def pipe(E, n, *stages):
    for s in range(n + max(l for l, _ in stages)):
        E["poll"]()
        for lag, f in stages:
            if 0 <= s - lag < n:
                f(s - lag)


class Behind:

    def __init__(self, pro):
        self.pro, self.made, self.run = pro, {}, None

    def start(self, b):
        if b < NB:
            self.run = (b, self.pro(b))

    def step(self):
        if self.run:
            b, g = self.run
            r = next(g, "end")
            if r == "end":
                self.run = None
            elif r is not None:
                self.made[b] = r

    def end(self):
        while self.run:
            self.step()


def turn(E, bank, srcs, w):
    pe, T = E["pe"], E["T"]
    for i, (c, s, r, m) in enumerate(srcs):
        t = pe(T.transpose, bank.ap[0:m, c:c + r], s, E["ident"][0:r, 0:r], w=[w, bank.w], sig=i == len(srcs) - 1)
    return t


def finish_heads(E, n, b, Osb, ot_ring, Wo, bo, w, osb_give):
    inner = Osb.shape[2]
    kt = inner // P
    ob = ot_ring.take()
    ot = ob.ap.rearrange("p (k n) -> p k n", k=kt)
    toks = []
    for k in range(0, kt, 2):
        bank = E["ps"].take()
        m = turn(E, bank, [((kk * 2 + it) * P, Osb[:, it, (k + kk) * P:(k + kk + 1) * P], P, P)
                           for kk in range(2) for it in range(2)], w)
        e = E["copy"](ob.ap[:, k * S:(k + 2) * S], bank.ap, w=[m, ob.w])
        E["ps"].give(bank, e)
        toks.append(e)
    osb_give(m)
    for it in range(2):
        m = E["to_x"](2 * b + it, lambda k: ot[:, k, it * P:(it + 1) * P], kt, Wo, [toks], bias=bo)
    ot_ring.give(ob, m)
    if b % 2:
        E["finished"](n, b // 2)


def get(E):
    return [E[k] for k in ("pe", "act", "dve", "pool", "T", "V", "C", "G", "ps", "mm", "X", "xnT", "W", "Wk", "copy")]


def rope_tile(E, t, Wqk, bufs, w):
    pe, act, dve, pool, T, V, C, G, ps, mm, X, xnT, W, Wk, copy = get(E)
    it = t % 2
    bank = ps.take()
    m = mm(bank.ap, [(xnT[:, k, t * P:(t + 1) * P], Wqk[:, k, :]) for k in range(2)], w=[bank.w, w])
    rb, tb = bufs[0].take(), bufs[1].take()
    cos = E["K"]("cos")[:, 16 * it:16 * it + 16]
    sin = E["K"]("sin")[:, 16 * it:16 * it + 16]
    v = bank.ap.rearrange("p (h d) -> p h d", d=16)
    a = rb.ap.rearrange("p (h d) -> p h d", d=16)
    c = tb.ap.rearrange("p (h d) -> p h d", d=16)
    q1 = dve(V.tensor_tensor, a, v, cos.unsqueeze(1).to_broadcast([P, 32, 16]), ALU.mult, w=[m, rb.w])
    q2 = dve(V.tensor_tensor, c[:, :, 0:8], v[:, :, 8:16], sin[:, 0:8].unsqueeze(1).to_broadcast([P, 32, 8]),
             ALU.mult, w=[m, tb.w])
    q2 = dve(V.tensor_tensor, c[:, :, 8:16], v[:, :, 0:8], sin[:, 8:16].unsqueeze(1).to_broadcast([P, 32, 8]),
             ALU.mult, w=[m])
    ps.give(bank, q2)
    q = pool(G.tensor_tensor, rb.ap, rb.ap, tb.ap, ALU.add, w=[q1, q2])
    bufs[1].give(tb, q)

    def turned():
        bank = ps.take()
        m = turn(E, bank, [(j * P, rb.ap[:, j * P:(j + 1) * P], P, P) for j in range(4)], [q])
        bufs[0].give(rb, m)
        return bank, m
    return turned


def talking(E, n):
    pe, act, dve, pool, T, V, C, G, ps, mm, X, xnT, W, Wk, copy = get(E)
    wt = E["wtok"][n]
    ar = E["Arena"]([(E["scr"], 0, E["NSCR"])])
    Wqk, Wv, Wo = Wk(n, "Wqk", 2), Wk(n, "Wv", 2), Wk(n, "Wout", 2)
    rbufs = (ar.ring(512, 2), ar.ring(512, 2))
    qr, kr, vr = ar.ring(512, 2), ar.ring(512, 2), ar.ring(512, 2)
    qg, pr, pt, vh = ar.ring(512, 4), ar.ring(512, 4), ar.ring(512, 3), ar.ring(512, 6)
    ot = ar.ring(512, 2)
    sm = ar.ring(8, 6)
    wpre = W(n, "wpre").rearrange("p (k g) -> p k g", k=2)
    wpost = W(n, "wpost")
    xts = E["inputs_of"](n)
    st = {}

    def pro(b):
        qb, kb, vb = qr.take(), kr.take(), vr.take()
        q, k, v = [z.ap.rearrange("p (k n) -> p k n", k=2) for z in (qb, kb, vb)]
        toks = []
        for it in range(2):
            t = 2 * b + it
            turned = rope_tile(E, t, Wqk, rbufs, [xts[b // 2], wt])
            yield
            yield
            yield
            bank, m = turned()
            bv = bank.ap.rearrange("p (j n) -> p j n", j=4)
            e1 = act(C.activation, q[:, :, it * P:(it + 1) * P], bv[:, 0:2, :], ACT.Copy, scale=0.25, w=[m, qb.w])
            e2 = act(C.activation, k[:, :, it * P:(it + 1) * P], bv[:, 2:4, :], ACT.Copy, w=[m, kb.w])
            ps.give(bank, e1, e2)
            bank = ps.take()
            m = mm(bank.ap[:, 0:D], [(xnT[:, k2, t * P:(t + 1) * P], Wv[:, k2, :]) for k2 in range(2)], w=[bank.w])
            e3 = copy(v[:, it, :], bank.ap[:, 0:D], w=[m, vb.w])
            ps.give(bank, e3)
            toks += [e1, e2, e3]
            yield
        yield dict(q=q, k=k, v=v, bufs=(qb, kb, vb), t=toks)

    next_ = Behind(pro)
    st = next_.made

    def sa(u):
        b, g = divmod(u, 16)
        if g == 0:
            if b == 0:
                next_.start(0)
            next_.end()
        if g == 1:
            next_.start(b + 1)
        next_.step()
        s = st[b]
        gb = qg.take()
        gv = gb.ap.rearrange("p (k n) -> p k n", k=2)
        for k in range(2):
            e = dve(V.tensor_scalar, gv[:, k, :], s["q"][:, k, :], wpre[:, k, g:g + 1], None, ALU.mult,
                    w=[s["t"], gb.w])
        vb = vh.take()
        ve = pool(G.tensor_tensor, vb.ap.rearrange("p (j g d) -> p j g d", j=2, g=16),
                  s["v"].rearrange("p j (g d) -> p j g d", g=16),
                  wpost[:, 16 * g:16 * g + 16].unsqueeze(1).unsqueeze(3).to_broadcast([P, 2, 16, 16]), ALU.mult,
                  w=[s["t"], vb.w])
        s[g] = (gb, gv, e, vb, ve)

    def s0(u):
        b, g = divmod(u, 16)
        s = st[b]
        gb, gv, e, vb, ve = s[g]
        bank = ps.take()
        for it in range(2):
            m = mm(bank.ap[:, it * S:(it + 1) * S],
                   [(gv[:, k, it * P:(it + 1) * P], s["k"][:, k, :]) for k in range(2)], w=[e, bank.w])
        qg.give(gb, m)
        if g == 15:
            qr.give(s["bufs"][0], e)
            kr.give(s["bufs"][1], m)
            vr.give(s["bufs"][2], ve)
        sb_ = sm.take()
        pb = pr.take()
        p = pb.ap.rearrange("p (i n) -> p i n", i=2)
        sv = bank.ap.rearrange("p (i n) -> p i n", i=2)
        r = dve(V.tensor_reduce, sb_.ap[:, 0:2], sv, AX.X, ALU.max, negate=True, w=[m, sb_.w])
        for it in range(2):
            x = act(C.activation, p[:, it, :], sv[:, it, :], ACT.Exp, bias=sb_.ap[:, it:it + 1],
                    accum_out=sb_.ap[:, 2 + it:3 + it], w=[r, pb.w])
        ps.give(bank, x)
        s[g] = (sb_, pb, p, x, vb, ve)

    def sn(u):
        b, g = divmod(u, 16)
        s = st[b]
        sb_, pb, p, x, vb, ve = s[g]
        r = dve(V.reciprocal, sb_.ap[:, 4:6], sb_.ap[:, 2:4], w=[x])
        for it in range(2):
            x = dve(V.tensor_scalar, p[:, it, :], p[:, it, :], sb_.ap[:, 4 + it:5 + it], None, ALU.mult, w=[r])
        sm.give(sb_, x)
        s[g] = (pb, p, x, vb, ve)

    def s1(u):
        b, g = divmod(u, 16)
        pb, p, x, vb, ve = st[b][g]
        bank = ps.take()
        m = turn(E, bank, [((jt * 2 + it) * P, p[:, it, jt * P:(jt + 1) * P], P, P) for jt in range(2)
                           for it in range(2)], [x])
        pr.give(pb, m)
        tb = pt.take()
        e = copy(tb.ap, bank.ap, w=[m, tb.w])
        ps.give(bank, e)
        st[b][g] = (tb, e, vb, ve)

    def s2(u):
        b, g = divmod(u, 16)
        s = st[b]
        tb, e, vb, ve = s[g]
        if g == 0:
            s["o"] = [ps.take(), ps.take()]
        v = vb.ap.rearrange("p (j n) -> p j n", j=2)
        for f in range(2):
            m = mm(s["o"][f].ap[:, 0:S], [(v[:, j, f * P:(f + 1) * P], tb.ap[:, j * S:(j + 1) * S])
                                          for j in range(2)], w=[e, ve, s["o"][f].w], first=g == 0, last=g == 15)
        pt.give(tb, m)
        vh.give(vb, m)
        if g == 15:
            ob = ot.take()
            o = ob.ap.rearrange("p (k n) -> p k n", k=2)
            es = []
            for f in range(2):
                es.append(copy(o[:, f, :], s["o"][f].ap[:, 0:S], w=[m, ob.w]))
                ps.give(s["o"][f], es[-1])
            for it in range(2):
                m = E["to_x"](2 * b + it, lambda k: o[:, k, it * P:(it + 1) * P], 2, Wo, [es],
                              bias=W(n, "bo")[0:1, :])
            ot.give(ob, m)
            if b % 2:
                E["finished"](n, b // 2)

    pipe(E, 16 * NB, (0, sa), (1, s0), (2, sn), (3, s1), (4, s2))


def moe_heads(E, n):
    pe, act, dve, pool, T, V, C, G, ps, mm, X, xnT, W, Wk, copy = get(E)
    wt = E["wtok"][n]
    ar = E["Arena"]([(E["scr"], 0, E["NSCR"])])
    We = W(n, "We").rearrange("p (e n) -> p e n", e=4)
    Wo = Wk(n, "Wo", 2)
    pool_ = ar.get(16).rearrange("p (k b) -> p k b", k=2)
    hid = ar.get(8)
    hb_ = ar.get(1024).rearrange("p (b n) -> p b n", b=8)
    gw = ar.get(32).rearrange("p (b e) -> p b e", e=4)
    rk = ar.get(32).rearrange("p (b e) -> p b e", e=4)
    a1, a2 = [ar.get(32).rearrange("p (b e) -> p b e", e=4) for _ in range(2)]
    sm8 = ar.get(8)
    xts = E["inputs_of"](n)
    t = dve(V.tensor_reduce, pool_, xnT.rearrange("p k (b s) -> p k b s", b=8), AX.X, ALU.add, w=[xts])
    t = dve(V.tensor_scalar, pool_, pool_, 1.0 / 256, None, ALU.mult, w=[t])
    bank = ps.take()
    wg1 = Wk(n, "Wg1", 2)
    m = mm(bank.ap[:, 0:8], [(wg1[:, k, :], pool_[:, k, :]) for k in range(2)], w=[t, wt, bank.w])
    t = act(C.activation, hid, bank.ap[:, 0:8], ACT.Relu, bias=W(n, "bg1"), w=[m])
    t = dve(V.tensor_copy, hb_, hid.unsqueeze(2).to_broadcast([P, 8, P]), w=[t])
    for b in range(8):
        m = mm(bank.ap[:, 16 + 4 * b:20 + 4 * b], [(hb_[:, b, :], W(n, "Wg2")),
                                                   (E["ones"][0:1, :], W(n, "bg2")[0:1, :])], w=[t])
    lv = bank.ap[:, 16:48].rearrange("p (b e) -> p b e", e=4)
    t = dve(V.tensor_reduce, sm8, lv, AX.X, ALU.max, w=[m])
    lg = ar.get(32).rearrange("p (b e) -> p b e", e=4)
    t = dve(V.tensor_tensor, gw, lv, sm8.unsqueeze(2).to_broadcast([P, 8, 4]), ALU.subtract, w=[t])
    t = dve(V.tensor_copy, lg, lv, w=[t])
    ps.give(bank, t)
    x = act(C.activation, gw, gw, ACT.Exp, w=[t])
    jgt = E["K"]("jgt").rearrange("p (e j) -> p e j", e=8)
    for e in range(4):
        me = lg[:, :, e:e + 1].to_broadcast([P, 8, 4])
        q = dve(V.tensor_tensor, a1, lg, me, ALU.is_gt, w=[t])
        q = dve(V.tensor_tensor, a2, lg, me, ALU.is_equal, w=[q])
        q = dve(V.tensor_tensor, a2, a2, jgt[:, e, 0:4].unsqueeze(1).to_broadcast([P, 8, 4]), ALU.mult, w=[q])
        q = dve(V.tensor_tensor, a1, a1, a2, ALU.add, w=[q])
        t = dve(V.tensor_reduce, rk[:, :, e], a1, AX.X, ALU.add, w=[q])
    t = dve(V.scalar_tensor_tensor, gw, rk, 1.5, gw, ALU.is_lt, ALU.mult, w=[t, x])
    t = dve(V.tensor_reduce, sm8, gw, AX.X, ALU.add, w=[t])
    t = dve(V.reciprocal, sm8, sm8, w=[t])
    gt = dve(V.tensor_tensor, gw, gw, sm8.unsqueeze(2).to_broadcast([P, 8, 4]), ALU.mult, w=[t])

    wcr = ar.ring(1536, 1)
    bcr = ar.ring(260, 1)
    qr, vr, kmr = ar.ring(512, 2), ar.ring(512, 2), ar.ring(4096, 2)
    att = Heads16(E, n, ar, Wo, W(n, "bo")[0:1, :])
    bqk = W(n, "bqk").rearrange("p (e c) -> p e c", e=4)
    bv = W(n, "bv")[0:1, :].rearrange("p (e c) -> p e c", e=4)

    def pro(b):
        wb, bb = wcr.take(), bcr.take()
        for e in range(4):
            g = gw[:, b, e:e + 1]
            g0 = gw[0:1, b, e:e + 1]
            if e == 0:
                c1 = [dve(V.tensor_scalar, wb.ap[:, c:c + 768], We[:, e, c:c + 768], g, None, ALU.mult,
                          w=[gt, wb.w, wt]) for c in (0, 768)]
                c2 = dve(V.tensor_scalar, bb.ap[:, 0:4], bqk[:, e, :], g, None, ALU.mult, w=[bb.w])
                c3 = dve(V.tensor_scalar, bb.ap[0:1, 4:260], bv[:, e, :], g0, None, ALU.mult)
            else:
                c2 = dve(V.scalar_tensor_tensor, bb.ap[:, 0:4], bqk[:, e, :], g, bb.ap[:, 0:4], ALU.mult, ALU.add,
                         w=[c2])
                c3 = dve(V.scalar_tensor_tensor, bb.ap[0:1, 4:260], bv[:, e, :], g0, bb.ap[0:1, 4:260], ALU.mult,
                         ALU.add, w=[c3])
                for i, c in enumerate((0, 768)):
                    c1[i] = dve(V.scalar_tensor_tensor, wb.ap[:, c:c + 768], We[:, e, c:c + 768], g,
                                wb.ap[:, c:c + 768], ALU.mult, ALU.add, w=[c1[i]])
                    yield
            yield
        wc = wb.ap.rearrange("p (m k n) -> p m k n", m=3, k=2)
        qb, vb, kb = qr.take(), vr.take(), kmr.take()
        q = qb.ap.rearrange("p (k n) -> p k n", k=2)
        v = vb.ap.rearrange("p (k n) -> p k n", k=2)
        km = kb.ap.rearrange("p (k h n) -> p k h n", k=2, h=8)
        xb = xnT[:, :, b * S:(b + 1) * S]
        toks = []
        for f in range(2):
            bank = ps.take()
            m1 = mm(bank.ap[:, 0:S], [(wc[:, 0, k, f * P:(f + 1) * P], xb[:, k, :]) for k in range(2)],
                    w=[c1, c2, c3, bank.w])
            m = mm(bank.ap[:, S:2 * S], [(wc[:, 1, k, f * P:(f + 1) * P], xb[:, k, :]) for k in range(2)])
            e1 = dve(V.tensor_scalar, q[:, f, :], bank.ap[:, 0:S], bb.ap[:, f:f + 1], 0.25, ALU.add, ALU.mult,
                     w=[m, qb.w])
            kt_ = att.kraw.take()
            e2 = act(C.activation, kt_.ap, bank.ap[:, S:2 * S], ACT.Identity, bias=bb.ap[:, 2 + f:3 + f],
                     w=[m, e1, kt_.w])
            ps.give(bank, e1, e2)
            e3 = att.mask(km[:, f, :, :], kt_.ap, S, [e2, kb.w])
            att.kraw.give(kt_, e3)
            toks += [e1, e3]
            yield
        bank = ps.take()
        for it in range(2):
            m = mm(bank.ap[:, it * S:(it + 1) * S], [(xb[:, k, it * P:(it + 1) * P], wc[:, 2, k, :])
                                                     for k in range(2)]
                   + [(E["ones"][0:1, :], bb.ap[0:1, 4:260])], w=[bank.w])
        e = copy(vb.ap, bank.ap, w=[m, vb.w])
        ps.give(bank, e)
        wcr.give(wb, m)
        bcr.give(bb, m)
        yield dict(q=q, v=v, km=km, t=toks + [e],
                    free=[(vr, vb)], free_qk=[(qr, qb), (kmr, kb)])

    att.run(pro)


class Heads16:

    def __init__(self, E, n, ar, Wo, bo, local=False):
        self.E, self.local, self.Wo, self.bo, self.n = E, local, Wo, bo, n
        self.kraw = ar.ring(256, 2)
        self.pr, self.pt = ar.ring(512, 5), ar.ring(512, 4)
        self.osb, self.ot = ar.ring(512, 1), ar.ring(512, 2)
        self.sm = ar.ring(8, 8)
        self.sums = ar.ring(64, 3)
        if local:
            self.g = ar.ring(512, 1)

    def mask(self, o, k, n, w):
        E = self.E
        return E["pool"](E["G"].tensor_tensor, o, k.unsqueeze(1).to_broadcast([P, 8, n]),
                         E["K"]("hm").unsqueeze(2).to_broadcast([P, 8, n]), ALU.mult, w=w)

    def run(self, pro, extra=None):
        pe, act, dve, pool, T, V, C, G, ps, mm, X, xnT, W, Wk, copy = get(self.E)
        E, local = self.E, self.local
        st = {}
        next_ = Behind(pro)

        def s0(u):
            b, r = divmod(u, 16)
            if r == 0:
                if b == 0:
                    next_.start(0)
                next_.end()
                st[b] = next_.made[b]
                st[b]["sum"] = self.sums.take()
            if r == (5 if local else 1):
                next_.start(b + 1)
            next_.step()
            s = st[b]
            sb_, pb = self.sm.take(), self.pr.take()
            bank = ps.take()
            sums = s["sum"].ap[:, 0:32].rearrange("p (i h) -> p i h", i=2)
            if local:
                kt, h8 = divmod(r, 8)
                lw = [(0, 0, P, 0, r), (1, P, S, 1, r)]
                for it, c, n, _, _ in lw:
                    m = mm(bank.ap[:, c:c + n], [(s["q"][:, kt, it * P:(it + 1) * P], s["km"][:, kt, h8, 0:n])],
                           w=[s["t"], bank.w])
                r_ = dve(V.scalar_tensor_tensor, pb.ap[:, 0:384], W(self.n, "dist"), float(2.0 ** (-(r + 1) * 0.5)),
                         bank.ap[:, 0:384], ALU.mult, ALU.add, w=[m, pb.w])
                ps.give(bank, r_)
                for it, c, n, _, _ in lw:
                    q = dve(V.tensor_reduce, sb_.ap[:, it:it + 1], pb.ap[:, c:c + n], AX.X, ALU.max, negate=True,
                            w=[r_, sb_.w])
                for it, c, n, _, _ in lw:
                    x = act(C.activation, pb.ap[:, c:c + n], pb.ap[:, c:c + n], ACT.Exp, bias=sb_.ap[:, it:it + 1],
                            accum_out=sums[:, it, r:r + 1], w=[q, s["sum"].w])
            else:
                kt, r2 = divmod(r, 8)
                pair, it = divmod(r2, 2)
                m = mm(bank.ap, [(s["q"][:, kt, it * P:(it + 1) * P],
                                  s["km"][:, kt, 2 * pair:2 * pair + 2, :])], w=[s["t"], bank.w])
                sv = bank.ap.rearrange("p (i n) -> p i n", i=2)
                q = dve(V.tensor_reduce, sb_.ap[:, 0:2], sv, AX.X, ALU.max, negate=True, w=[m, sb_.w])
                for j in range(2):
                    h = 8 * kt + 2 * pair + j
                    x = act(C.activation, pb.ap[:, j * S:(j + 1) * S], sv[:, j, :], ACT.Exp,
                            bias=sb_.ap[:, j:j + 1], accum_out=sums[:, it, h:h + 1], w=[q, pb.w, s["sum"].w])
                ps.give(bank, x)
            self.sm.give(sb_, x)
            s[r] = (pb, x)
            if r == 15:
                if extra:
                    m = extra(b, s)
                for ring, buf in s["free_qk"]:
                    ring.give(buf, m)

        def s1(u):
            b, r = divmod(u, 16)
            pb, x = st[b][r]
            bank = ps.take()
            n = 3 if local else 4
            m = turn(E, bank, [(j * P, pb.ap[:, j * P:(j + 1) * P], P, P) for j in range(n)], [x])
            self.pr.give(pb, m)
            tb = self.pt.take()
            e = copy(tb.ap[:, 0:n * P], bank.ap[:, 0:n * P], w=[m, tb.w])
            ps.give(bank, e)
            st[b][r] = (tb, e, x)

        def s2(u):
            b, r = divmod(u, 16)
            s = st[b]
            tb, e, x = s[r]
            if r == 0:
                s["o"] = ps.take()
            o = s["o"].ap.rearrange("p (i n) -> p i n", i=2)
            pt = tb.ap
            if local:
                items = [(0, r, [(0, 0)]), (1, r, [(1, 0), (2, 1)])]
            else:
                kt, r2 = divmod(r, 8)
                pair, it = divmod(r2, 2)
                items = [(it, 8 * kt + 2 * pair + j, [(2 * j, 0), (2 * j + 1, 1)]) for j in range(2)]
            for it, h, parts in items:
                m = mm(o[:, it, 16 * h:16 * h + 16],
                       [(pt[:, c * P:(c + 1) * P], s["v"][:, jt, 16 * h:16 * h + 16]) for c, jt in parts],
                       w=[e, s["o"].w])
            self.pt.give(tb, m)
            if r < 15:
                return
            rs = s["sum"].ap[:, 32:64]
            q = dve(V.reciprocal, rs, s["sum"].ap[:, 0:32], w=[x])
            ob = self.osb.take()
            ov = ob.ap.rearrange("p (g d) -> p g d", d=16)
            q = dve(V.tensor_tensor, ov, s["o"].ap.rearrange("p (g d) -> p g d", d=16),
                    rs.unsqueeze(2).to_broadcast([P, 32, 16]), ALU.mult, w=[q, m, ob.w])
            ps.give(s["o"], q)
            self.sums.give(s["sum"], q)
            if local:
                q = dve(V.tensor_tensor, ob.ap, ob.ap, s["og"].ap, ALU.add, w=[q, s["og_t"]])
                ps.give(s["og"], q)
            for ring, buf in s["free"]:
                ring.give(buf, m)
            finish_heads(E, self.n, b, ob.ap.rearrange("p (i n) -> p i n", i=2), self.ot, self.Wo, self.bo, [q],
                         lambda tok: self.osb.give(ob, tok))

        pipe(E, 16 * NB, (0, s0), (3, s1), (5, s2))


def local_heads(E, n):
    pe, act, dve, pool, T, V, C, G, ps, mm, X, xnT, W, Wk, copy = get(E)
    wt = E["wtok"][n]
    ar = E["Arena"]([(E["scr"], 0, E["NSCR"])])
    Wqk, Wv, Wo = Wk(n, "Wqk", 2), Wk(n, "Wv", 2), Wk(n, "Wo", 2)
    rbufs = (ar.ring(512, 2), ar.ring(512, 1))
    qr, vr, kmr = ar.ring(512, 2), ar.ring(512, 2), ar.ring(4096, 2)
    att = Heads16(E, n, ar, Wo, None, local=True)
    pg, pgT, vg, gs = ar.get(128), ar.get(256), ar.get(256), ar.get(96)
    xts = E["inputs_of"](n)
    held = {"g": None}

    def pro(b):
        qb, vb, kb = qr.take(), vr.take(), kmr.take()
        q = qb.ap.rearrange("p (k n) -> p k n", k=2)
        v = vb.ap.rearrange("p (k n) -> p k n", k=2)
        km = kb.ap.rearrange("p (k h n) -> p k h n", k=2, h=8)
        toks = []
        for it in range(2):
            t = 2 * b + it
            turned = rope_tile(E, t, Wqk, rbufs, [xts[b // 2], wt])
            yield
            yield
            yield
            bank, m = turned()
            bv = bank.ap.rearrange("p (j n) -> p j n", j=4)
            e1 = act(C.activation, q[:, :, it * P:(it + 1) * P], bv[:, 0:2, :], ACT.Copy, scale=0.25, w=[m, qb.w])
            kt_ = att.kraw.take()
            e2 = act(C.activation, kt_.ap, bank.ap[:, 256:512], ACT.Copy, w=[m, kt_.w])
            ps.give(bank, e1, e2)
            kk = kt_.ap.rearrange("p (k n) -> p k n", k=2)
            for f in range(2):
                e3 = att.mask(km[:, f, :, it * P:(it + 1) * P], kk[:, f, :], P, [e2, kb.w])
            att.kraw.give(kt_, e3)
            bank = ps.take()
            m = mm(bank.ap[:, 0:D], [(xnT[:, k2, t * P:(t + 1) * P], Wv[:, k2, :]) for k2 in range(2)], w=[bank.w])
            e4 = copy(v[:, it, :], bank.ap[:, 0:D], w=[m, vb.w])
            ps.give(bank, e4)
            toks += [e1, e3, e4]
            yield
        yield dict(q=q, v=v, km=km, t=toks, free=[(vr, vb)], free_qk=[(qr, qb), (kmr, kb)])

    def extra(b, s):
        hold = held["g"]
        bank = ps.take()
        for it in range(2):
            for kt in range(2):
                c = it * 64 + kt * 32
                m = mm(bank.ap[:, c:c + 32], [(s["q"][:, kt, it * P:(it + 1) * P], s["km"][:, kt, :, 0:256:64])],
                       w=[bank.w, s["t"]])
        m2 = mm(bank.ap[0:64, 128:128 + D], [(W(n, "gsel")[:, 64 * t:64 * t + 64], s["v"][:, t, :])
                                              for t in range(2)])
        sv = bank.ap[:, 0:128].rearrange("p (g j) -> p g j", j=4)
        pv = pg.rearrange("p (g j) -> p g j", j=4)
        bc = lambda a: a.unsqueeze(2).to_broadcast([P, 32, 4])
        q = dve(V.tensor_reduce, gs[:, 0:32], sv, AX.X, ALU.max, w=[m, m2, hold])
        q = dve(V.tensor_tensor, pv, sv, bc(gs[:, 0:32]), ALU.subtract, w=[q])
        q2 = dve(V.tensor_tensor, vg[0:64, :], bank.ap[0:64, 128:128 + D], W(n, "gmask", 64), ALU.mult,
                 w=[m2, hold])
        ps.give(bank, q, q2)
        q = act(C.activation, pg, pg, ACT.Exp, w=[q])
        q = dve(V.tensor_reduce, gs[:, 32:64], pv, AX.X, ALU.add, w=[q])
        q = dve(V.reciprocal, gs[:, 64:96], gs[:, 32:64], w=[q])
        q = dve(V.tensor_tensor, pv, pv, bc(gs[:, 64:96]), ALU.mult, w=[q])
        bank = ps.take()
        m = turn(E, bank, [(it * P, pg[:, it * 64:(it + 1) * 64], P, 64) for it in range(2)], [q])
        e = dve(V.tensor_copy, pgT[0:64, :], bank.ap[0:64, 0:256], w=[m])
        ps.give(bank, e)
        og = ps.take()
        for it in range(2):
            m = mm(og.ap[:, it * S:(it + 1) * S], [(pgT[0:64, it * P:(it + 1) * P], vg[0:64, :])],
                   w=[e, q2, og.w])
        held["g"] = m
        s["og"], s["og_t"] = og, m
        return m

    att.run(pro, extra)


def few_keys(E, n):
    pe, act, dve, pool, T, V, C, G, ps, mm, X, xnT, W, Wk, copy = get(E)
    wt, A, dma = E["wtok"][n], E["A"], E["dma"]
    ar = E["Arena"]([(E["scr"], 0, E["NSCR"])])
    small = n == 4
    kt = 2 if small else 8
    inner = kt * P
    dh = inner // 16
    if small:
        Wq, Wkk, Wv, Wo = [Wk(n, x, 2) for x in ("Wq", "Wk", "Wv", "Wo")]
    else:
        Wq, Wkk, Wv, Wo = Wk(n, "wq", 2), Wk(n, "wk", 2), Wk(n, "wv", 2), Wk(n, "wo", 8)
    bo = W(n, "bo")[0:1, :]
    ctxT = E["ctxT"]
    kT = ar.get(kt * 616).rearrange("p (k n) -> p k n", k=kt)
    qr = ar.ring(kt * S, 2)
    if not small:
        for qb in qr.free:
            v_ = qb.ap.rearrange("p (k o n) -> p k o n", k=kt, o=2)
            z1 = pool(G.memset, v_[64:P, :, 0, :], 0.0)
            zero = [z1, pool(G.memset, v_[0:64, :, 1, :], 0.0)]
    vr = ar.ring(inner, 2)
    pr = ar.ring(16 * S2, 2)
    pt = ar.ring(512, 4)
    osb = ar.ring(2 * inner, 1)
    ot = ar.ring(2 * inner, 1)
    sm = ar.ring(48, 4)
    kts = []
    for f in range(kt):
        for h in range(2):
            bank = ps.take()
            m = mm(bank.ap[:, 0:308], [(Wkk[:, k, f * P:(f + 1) * P], ctxT[:, k, h * 308:(h + 1) * 308])
                                       for k in range(2)], w=[bank.w, wt, E["ctx_tok"]])
            o = kT[:, f, h * 308:(h + 1) * 308]
            if small:
                e = act(C.activation, o, bank.ap[:, 0:308], ACT.Identity, bias=W(n, "bk")[:, f:f + 1], w=[m])
            else:
                e = copy(o, bank.ap[:, 0:308], w=[m])
            ps.give(bank, e)
            kts.append(e)
    if small:
        mu = ar.get(154)
        pen = ar.get(616)
        kmr = ar.ring(2 * 8 * S2, 2)
        br = ar.ring(2 * S2, 2)
        mt = dma(mu.bitcast(U8), A["mbf"].rearrange("(a b) s -> a (b s)", a=1).partition_broadcast(P)
                 if False else A["mbf"].rearrange("b s -> (b s)").partition_broadcast(P), E["bars"][-1])
        q = dve(V.tensor_scalar, pen, mu.bitcast(U8), -3e38, 2.0, ALU.mult, ALU.mult, w=[mt])
        pen_t = q
        am = W(n, "am").rearrange("p (i s) -> p i s", i=2)
    groups = [(0, 6), (6, 12), (12, 16)]
    xts = E["inputs_of"](n)
    st = {}

    def pro(b):
        vb = vr.take()
        toks = []
        if small:
            qb = qr.take()
            q = qb.ap.rearrange("p (k n) -> p k n", k=kt)
            bank = ps.take()
            f = 0
            for j in range(2):
                m = mm(bank.ap[:, j * S:(j + 1) * S],
                       [(Wq[:, k, (f + j) * P:(f + j + 1) * P], xnT[:, k, b * S:(b + 1) * S]) for k in range(2)],
                       w=[bank.w, xts[b // 2], wt])
            for j in range(2):
                e = dve(V.tensor_scalar, q[:, j, :], bank.ap[:, j * S:(j + 1) * S], W(n, "bq")[:, j:j + 1], 0.25,
                        ALU.add, ALU.mult, w=[m, qb.w])
            ps.give(bank, e)
            toks.append(e)
        for c in range(0, inner, 512):
            n_ = min(512, inner)
            bank = ps.take()
            pairs = [(ctxT[:, k, b * S2:(b + 1) * S2], Wv[:, k, c:c + n_]) for k in range(2)]
            if small:
                pairs.append((E["ones"][0:1, 0:S2], W(n, "bv")[0:1, :]))
            m = mm(bank.ap[0:S2, 0:n_], pairs, w=[bank.w, E["ctx_tok"]])
            e = copy(vb.ap[0:S2, c:c + n_], bank.ap[0:S2, 0:n_], w=[m, vb.w])
            ps.give(bank, e)
            toks.append(e)
        s = dict(v=vb.ap, t=toks, free=[(vr, vb)])
        if small:
            s.update(q=q, qb=qb)
            kb, bb = kmr.take(), br.take()
            km = kb.ap.rearrange("p (k h n) -> p k h n", k=2, h=8)
            for f in range(2):
                e = pool(G.tensor_tensor, km[:, f, :, :],
                         kT[:, f, b * S2:(b + 1) * S2].unsqueeze(1).to_broadcast([P, 8, S2]),
                         E["K"]("hm").unsqueeze(2).to_broadcast([P, 8, S2]), ALU.mult, w=[kts, kb.w])
            s["t"].append(e)
            e = pool(G.tensor_tensor, bb.ap.rearrange("p (i s) -> p i s", i=2), am,
                     pen[:, b * S2:(b + 1) * S2].unsqueeze(1).to_broadcast([P, 2, S2]), ALU.add,
                     w=[pen_t, wt, bb.w])
            s["bias"] = bb.ap.rearrange("p (i s) -> p i s", i=2)
            s["bt"] = e
            s["km"] = km
            s["free"] += [(kmr, kb), (br, bb)]
        st[b] = s

    def sq(u):
        b, it = divmod(u, 2)
        if it == 0:
            pro(b)
        qb = qr.take()
        q = qb.ap.rearrange("p (k o n) -> p k o n", k=kt, o=2)
        toks = []
        for f in (0, 4):
            bank = ps.take()
            for j in range(4):
                m = mm(bank.ap[:, j * P:(j + 1) * P],
                       [(Wq[:, k, (f + j) * P:(f + j + 1) * P], xnT[:, k, u * P:(u + 1) * P]) for k in range(2)],
                       w=[bank.w, xts[b // 2], wt])
            bv = bank.ap.rearrange("p (k n) -> p k n", k=4)
            for o in (0, 64):
                toks.append(act(C.activation, q[o:o + 64, f:f + 4, o // 64, :], bv[o:o + 64], ACT.Copy, scale=0.125,
                                w=[m, qb.w, zero]))
            ps.give(bank, toks[-1])
        st[b]["q", it] = (qb, q, toks)

    def s0(u):
        b, it = divmod(u, 2)
        if (small and u == 0) or (small and it == 1 and b + 1 < NB):
            pro(b + it)
        s = st[b]
        pb, sb_ = pr.take(), sm.take()
        p = pb.ap.rearrange("p (h n) -> p h n", h=16)
        xs = []
        for lo, hi in groups:
            bank = ps.take()
            if small:
                cuts = [(max(lo, 8 * f), min(hi, 8 * f + 8), f) for f in range(2)]
                for a, z, f in cuts:
                    if a < z:
                        m = mm(bank.ap[:, (a - lo) * S2:(z - lo) * S2],
                               [(s["q"][:, f, it * P:(it + 1) * P], s["km"][:, f, a - 8 * f:z - 8 * f, :])],
                               w=[bank.w, s["t"]])
            else:
                qb, q_, qt = s["q", it]
                for h in range(lo, hi):
                    m = mm(bank.ap[:, (h - lo) * S2:(h - lo + 1) * S2],
                           [(q_[:, h // 2, h % 2, :], kT[:, h // 2, b * S2:(b + 1) * S2])],
                           w=[bank.w, qt, s["t"], kts])
            qk = m
            nh = hi - lo
            sv = bank.ap[:, 0:nh * S2].rearrange("p (h n) -> p h n", n=S2)
            pv = p[:, lo:hi, :]
            mx = sb_.ap[:, lo:hi]
            src = sv
            if small:
                q = dve(V.tensor_tensor, pv, sv, s["bias"][:, it, :].unsqueeze(1).to_broadcast([P, nh, S2]), ALU.add,
                        w=[m, s["bt"], pb.w])
                bt = q
                src = pv
                m = q
            q = dve(V.tensor_reduce, mx, src, AX.X, ALU.max, w=[m, sb_.w])
            q = dve(V.tensor_tensor, pv, src, mx.unsqueeze(2).to_broadcast([P, nh, S2]), ALU.subtract,
                    w=[q, pb.w])
            ps.give(bank, q)
            x = act(C.activation, pv, pv, ACT.Exp, w=[q])
            xs.append(x)
        s[it] = (pb, p, xs, sb_)
        if not small:
            qr.give(qb, qk)
        elif it == 1:
            qr.give(s["qb"], qk)

    def s1(u):
        b, it = divmod(u, 2)
        s = st[b]
        pb, p, xs, sb_ = s[it]
        for (lo, hi), x in zip(groups, xs):
            q = dve(V.tensor_reduce, sb_.ap[:, 16 + lo:16 + hi], p[:, lo:hi, :], AX.X, ALU.add, w=[x])
        q = dve(V.reciprocal, sb_.ap[:, 32:48], sb_.ap[:, 16:32], w=[q])
        for g in range(4):
            bank = ps.take()
            m = turn(E, bank, [(j * P, p[:, 4 * g + j, :], P, S2) for j in range(4)], [xs[min(2, (4 * g + 3) // 6)]])
            tb = pt.take()
            e = copy(tb.ap[0:S2, :], bank.ap[0:S2, :], w=[m, tb.w])
            ps.give(bank, e)
            s[("t", g)] = (tb, e)
        pr.give(pb, m, q)
        s["r", it] = q

    def s2(u):
        b, it = divmod(u, 2)
        s = st[b]
        sb_, q = s[it][3], s["r", it]
        if it == 0:
            s["osb"] = osb.take()
        ob = s["osb"]
        ov = ob.ap.rearrange("p (i n) -> p i n", i=2)
        per = 512 // dh if not small else 16
        obank = None
        for h in range(16):
            if h % per == 0:
                obank = ps.take()
            tb, e = s[("t", h // 4)]
            c = (h % per) * dh
            m = mm(obank.ap[:, c:c + dh], [(tb.ap[0:S2, (h % 4) * P:(h % 4 + 1) * P], s["v"][0:S2, h * dh:(h + 1) * dh])],
                   w=[e, obank.w])
            if h % 4 == 3:
                pt.give(tb, m)
            if (h + 1) % per == 0:
                lo = h + 1 - per
                z = dve(V.tensor_tensor, ov[:, it, lo * dh:(h + 1) * dh].rearrange("p (h d) -> p h d", d=dh),
                        obank.ap[:, 0:per * dh].rearrange("p (h d) -> p h d", d=dh),
                        sb_.ap[:, 32 + lo:32 + h + 1].unsqueeze(2).to_broadcast([P, per, dh]), ALU.mult,
                        w=[m, q, ob.w])
                ps.give(obank, z)
        sm.give(sb_, z)
        if it == 1:
            for ring, buf in s["free"]:
                ring.give(buf, m, z)
            finish_heads(E, n, b, ov, ot, Wo, bo, [z], lambda tok: osb.give(ob, tok))

    if small:
        pipe(E, 2 * NB, (1, s1), (0, s0), (1, s2))
    else:
        pipe(E, 2 * NB, (2, s1), (1, s0), (2, s2), (0, sq))


def latent_heads(E, n):
    pe, act, dve, pool, T, V, C, G, ps, mm, X, xnT, W, Wk, copy = get(E)
    wt = E["wtok"][n]
    ar = E["Arena"]([(E["scr"], 0, E["NSCR"])])
    many = n == 1
    H = 16 if many else 4
    inner = 64 * H
    kt = inner // P
    NK = 333
    cg = ar.get(1232).rearrange("p (k n) -> p k n", k=2)
    nq = 1 if many else 2
    qr, kr, vr = ar.ring(2 * kt * S, nq), ar.ring(kt * NK, nq), ar.ring(3 * inner, 2 if many else 3)
    pr, pt = ar.ring(672, 3), ar.ring(768, 2)
    xts = E["inputs_of"](n)
    osb = ar.ring(2 * inner, 1)
    ot = ar.ring(2 * inner, 1)
    sums = ar.ring(64, 2)
    sm = ar.ring(8, 6)
    g, bb = ("mg", "mb") if many else ("xg", "xb")
    for k in range(2):
        cgt = dve(V.tensor_scalar, cg[:, k, :], E["cnT"][:, k, :], W(n, g)[:, k:k + 1], W(n, bb)[:, k:k + 1],
                  ALU.mult, ALU.add, w=[E["ctx_tok"], wt])
    if many:
        Wq = Wk(n, "Wq", 2)
        Wkv = Wk(n, "Wkv", 2)
        Wo, bo = Wk(n, "Wout", 8), None
        vW = lambda k, c, m: Wkv[:, k, inner + c:inner + c + m]
    else:
        Wqk, Wvv = Wk(n, "Wqk", 2), Wk(n, "Wv", 2)
        Wo, bo = Wk(n, "Wo", 2), W(n, "bo")[0:1, :]
        vW = lambda k, c, m: Wvv[:, k, c:c + m]
        gq = ar.get(2)
        gqt = dve(V.tensor_scalar, gq[:, 0:1], W(n, "gq"), 0.125, None, ALU.mult, w=[wt])
        mu, pen = ar.get(154), ar.get(616)
        mt = E["dma"](mu.bitcast(U8), E["A"]["mbk"].rearrange("b s -> (b s)").partition_broadcast(P),
                      E["bars"][-1])
        pen_t = dve(V.tensor_scalar, pen, mu.bitcast(U8), -1.0, 1e30, ALU.add, ALU.mult, w=[mt])
        sqr, nrr, rsr = ar.ring(512, 2), ar.ring(512, 2), ar.ring(24, 2)
    for qb in qr.free:
        v_ = qb.ap.rearrange("p (k o n) -> p k o n", k=kt, o=2)
        z1 = pool(G.memset, v_[64:P, :, 0, :], 0.0)
        z2 = pool(G.memset, v_[0:64, :, 1, :], 0.0)
    zero = [z1, z2]

    def values(b, v):
        for j in range(3):
            rows = P if j < 2 else S2
            for c in range(0, inner, 512):
                m_ = min(512, inner)
                bank = ps.take()
                if j < 2:
                    l = lambda k: xnT[:, k, (2 * b + j) * P:(2 * b + j + 1) * P]
                else:
                    l = lambda k: cg[:, k, b * S2:(b + 1) * S2]
                m = mm(bank.ap[0:rows, 0:m_], [(l(k), vW(k, c, m_)) for k in range(2)],
                       w=[bank.w, xts[b // 2], cgt, wt])
                e = copy(v.ap[0:rows, j * inner + c:j * inner + c + m_], bank.ap[0:rows, 0:m_], w=[m, v.w])
                ps.give(bank, e)
                yield e

    qk_end = [[] for _ in range(kt)]

    def pro(b):
        vb = vr.take()
        vt, ft = [], {}
        made = dict(v=vb.ap.rearrange("p (j n) -> p j n", j=3), vt=vt, ft=ft, vb=vb)
        for e in values(b, vb):
            vt.append(e)
            yield
        if many:
            qb, kb = qk1
        else:
            qb, kb = qr.take(), kr.take()
        q = qb.ap.rearrange("p (k o n) -> p k o n", k=kt, o=2)
        k_ = kb.ap.rearrange("p (k n) -> p k n", k=kt)
        made.update(q=q, k=k_, qkb=(qb, kb))
        toks = []
        if many:
            yield made
            for f in range(kt):
                wf = slice(f * P, (f + 1) * P)
                bank = ps.take()
                m = mm(bank.ap[:, 0:S], [(Wq[:, k, wf], xnT[:, k, b * S:(b + 1) * S]) for k in range(2)],
                       w=[bank.w, zero])
                e = [act(C.activation, q[o:o + 64, f, o // 64, :], bank.ap[o:o + 64, 0:S], ACT.Copy, scale=0.125,
                         w=[m, qk_end[f]]) for o in (0, 64)]
                ps.give(bank, e)
                bank = ps.take()
                m = mm(bank.ap[:, 0:S], [(Wkv[:, k, wf], xnT[:, k, b * S:(b + 1) * S]) for k in range(2)],
                       w=[bank.w])
                m = mm(bank.ap[:, S:NK], [(Wkv[:, k, wf], cg[:, k, b * S2:(b + 1) * S2]) for k in range(2)],
                       w=[cgt])
                e2 = dve(V.tensor_copy, k_[:, f, :], bank.ap[:, 0:NK], w=[m, qk_end[f]])
                ps.give(bank, e2)
                ft[f] = [e, e2]
                yield
        else:
            for j in range(3):
                rows = P if j < 2 else S2
                bank = ps.take()
                lo = 0 if j < 2 else 256
                l = (lambda k: xnT[:, k, (2 * b + j) * P:(2 * b + j + 1) * P]) if j < 2 else \
                    (lambda k: cg[:, k, b * S2:(b + 1) * S2])
                m = mm(bank.ap[0:rows, lo:512], [(l(k), Wqk[:, k, lo:512]) for k in range(2)], w=[bank.w])
                s_, n_, r_ = sqr.take(), nrr.take(), rsr.take()
                nh = (512 - lo) // 64
                e = act(C.activation, s_.ap[0:rows, lo:512], bank.ap[0:rows, lo:512], ACT.Square, w=[m, s_.w])
                h8 = lambda a: a[0:rows, lo:512].rearrange("p (h d) -> p h d", d=64)
                r = r_.ap[0:rows, 0:nh]
                e1 = dve(V.tensor_reduce, r, h8(s_.ap), AX.X, ALU.add, w=[e, r_.w])
                sqr.give(s_, e1)
                e2 = act(C.activation, r, r, ACT.Sqrt, scale=1.0 / 64, w=[e1])
                e2 = dve(V.tensor_scalar, r, r, 1e-8, None, ALU.max, w=[e2])
                e2 = dve(V.reciprocal, r, r, w=[e2])
                e2 = dve(V.tensor_tensor, h8(n_.ap), h8(bank.ap), r.unsqueeze(2).to_broadcast([rows, nh, 64]),
                         ALU.mult, w=[e2, n_.w])
                rsr.give(r_, e2)
                ps.give(bank, e2)
                bank = ps.take()
                m = turn(E, bank, [(c * P, n_.ap[0:rows, c * P:(c + 1) * P], rows, P)
                                   for c in range(lo // P, 4)], [e2])
                nrr.give(n_, m)
                bv = bank.ap.rearrange("p (c n) -> p c n", c=4)
                if j < 2:
                    for o in (0, 64):
                        e3 = act(C.activation, q[o:o + 64, :, o // 64, j * P:(j + 1) * P], bv[o:o + 64, 0:2, :],
                                 ACT.Copy, scale=gq[o:o + 64, 0:1], w=[m, qb.w, gqt, zero])
                    toks.append(e3)
                kd = k_[:, :, j * P:(j + 1) * P] if j < 2 else k_[:, :, S:NK]
                e4 = act(C.activation, kd, bv[:, 2:4, 0:rows], ACT.Copy, scale=W(n, "gk")[:, 0:1], w=[m, kb.w])
                toks.append(e4)
                ps.give(bank, e4)
                yield
            for f in range(kt):
                ft[f] = toks
            yield made

    next_ = Behind(pro)
    st = next_.made
    qk1 = (qr.take(), kr.take()) if many else None

    def s0(u):
        b, h = divmod(u, H)
        if u == 0:
            next_.start(0)
            next_.end()
        if not many and h == 0:
            next_.end()
        if h == (4 if many else 0):
            next_.start(b + 1)
        for _ in range(1 if many else 3):
            next_.step()
        s = st[b]
        if h == 0:
            s["sum"] = sums.take()
        pb, sb_ = pr.take(), sm.take()
        su = s["sum"].ap.rearrange("p (r i h) -> p r i h", r=2, i=2)
        xs = []
        for it in range(2):
            bank = ps.take()
            ql = s["q"][:, h // 2, h % 2, it * P:(it + 1) * P]
            if many:
                m = mm(bank.ap[:, 0:NK], [(ql, s["k"][:, h // 2, :])], w=[bank.w, s["ft"][h // 2]])
            else:
                m = mm(bank.ap[:, 0:S], [(ql, s["k"][:, h // 2, 0:S])], w=[bank.w, s["ft"][h // 2]])
                m = mm(bank.ap[:, S:NK], [(ql, s["k"][:, h // 2, S:NK]),
                                          (E["ones"][0:1, :], pen[0:1, b * S2:(b + 1) * S2])], w=[pen_t])
            q = dve(V.tensor_reduce, sb_.ap[:, it:it + 1], bank.ap[:, 0:NK], AX.X, ALU.max, negate=True,
                    w=[m, sb_.w])
            x = act(C.activation, pb.ap[:, it * 336:it * 336 + NK], bank.ap[:, 0:NK], ACT.Exp,
                    bias=sb_.ap[:, it:it + 1], accum_out=su[:, 0, it, h:h + 1], w=[q, pb.w, s["sum"].w])
            ps.give(bank, x)
        sm.give(sb_, x)
        s[h] = (pb, x)
        qk_end[h // 2] = m
        if h == H - 1 and not many:
            qr.give(s["qkb"][0], m)
            kr.give(s["qkb"][1], m)

    def s1(u):
        b, h = divmod(u, H)
        pb, x = st[b][h]
        p = pb.ap.rearrange("p (i n) -> p i n", i=2)
        bank, bank2 = ps.take(), ps.take()
        m = turn(E, bank, [((jt * 2 + it) * P, p[:, it, jt * P:(jt + 1) * P], P, P) for jt in range(2)
                           for it in range(2)], [x])
        m2 = turn(E, bank2, [(it * P, p[:, it, S:NK], P, S2) for it in range(2)], [x])
        pr.give(pb, m2)
        tb = pt.take()
        e = dve(V.tensor_copy, tb.ap[:, 0:512], bank.ap, w=[m, tb.w])
        e2 = act(C.activation, tb.ap[0:S2, 512:768], bank2.ap[0:S2, 0:256], ACT.Copy, w=[m2, tb.w])
        ps.give(bank, e)
        ps.give(bank2, e2)
        st[b][h] = (tb, [e, e2], x)

    def s2(u):
        b, h = divmod(u, H)
        s = st[b]
        tb, e, x = s[h]
        hp = min(8, H)
        if h == 0:
            s["osb"] = osb.take()
        if h % hp == 0:
            s["o"] = [ps.take(), ps.take()]
        for it in range(2):
            c = (h % hp) * 64
            m = mm(s["o"][it].ap[:, c:c + 64],
                   [(tb.ap[:, (jt * 2 + it) * P:(jt * 2 + it + 1) * P], s["v"][:, jt, h * 64:(h + 1) * 64])
                    for jt in range(2)]
                   + [(tb.ap[0:S2, 512 + it * P:512 + (it + 1) * P], s["v"][0:S2, 2, h * 64:(h + 1) * 64])],
                   w=[e, s["vt"], s["o"][it].w])
        pt.give(tb, m)
        su = s["sum"].ap.rearrange("p (r i h) -> p r i h", r=2, i=2)
        ov = s["osb"].ap.rearrange("p (i n) -> p i n", i=2)
        if (h + 1) % hp == 0:
            lo = h + 1 - hp
            for it in range(2):
                q = dve(V.reciprocal, su[:, 1, it, lo:h + 1], su[:, 0, it, lo:h + 1], w=[x])
                q = dve(V.tensor_tensor, ov[:, it, lo * 64:(h + 1) * 64].rearrange("p (h d) -> p h d", d=64),
                        s["o"][it].ap[:, 0:hp * 64].rearrange("p (h d) -> p h d", d=64),
                        su[:, 1, it, lo:h + 1].unsqueeze(2).to_broadcast([P, hp, 64]), ALU.mult,
                        w=[q, m, s["osb"].w])
                ps.give(s["o"][it], q)
        if h == H - 1:
            sums.give(s["sum"], q)
            vr.give(s["vb"], m)
            finish_heads(E, n, b, ov, ot, Wo, bo, [q], lambda tok: osb.give(s["osb"], tok))

    pipe(E, H * NB, (0, s0), (2, s1), (3, s2))


def softplus(E, o, x, t1, t2, n_w):
    pe, act, dve, pool, T, V, C, G, ps, mm, X, xnT, W, Wk, copy = get(E)
    q = act(C.activation, t1, x, ACT.Abs, w=n_w)
    q = act(C.activation, t1, t1, ACT.Exp, scale=-1.0, w=[q])
    ql = act(C.activation, t2, t1, ACT.Ln, bias=E["one_ap"], w=[q, E["z_tok"]])
    qo = dve(V.scalar_tensor_tensor, t2, x, 0.0, t2, ALU.max, ALU.add, w=[ql])
    qm = dve(V.tensor_scalar, o, t1, 1.0, -1.0, ALU.add, ALU.add, w=[q, qo])
    qm = pool(G.tensor_tensor, t1, t1, o, ALU.subtract, w=[qm])
    return dve(V.tensor_tensor, o, t2, t1, ALU.add, w=[qo, qm])


def gated(E, n):
    pe, act, dve, pool, T, V, C, G, ps, mm, X, xnT, W, Wk, copy = get(E)
    wt = E["wtok"][n]
    ar = E["Arena"]([(E["scr"], 0, E["NSCR"])])
    buf = [ar.get(2048) for _ in range(8)]
    la, tz = ar.get(2), ar.get(8)
    R = ar.get(2048).rearrange("p (t d) -> p t d", t=8)
    q = dve(V.tensor_scalar, tz[:, 0:2], W(n, "lam"), -1.0, None, ALU.mult, w=[wt])
    q = softplus(E, tz[:, 6:8], tz[:, 0:2], tz[:, 2:4], tz[:, 4:6], [q])
    lat = dve(V.tensor_scalar, la, tz[:, 6:8], -0.125, None, ALU.mult, w=[q])
    Wm = {k: Wk(n, k, 2) for k in ("lin", "conv", "a", "x", "lin2", "w1", "w2", "w3")}
    col_ = lambda name, f: W(n, name)[:, f:f + 1]
    v2 = lambda a: a.rearrange("p (k n) -> p k n", k=2)

    def project(name, src, w, evac):
        toks = []
        for f in range(2):
            for c in range(2):
                bank = ps.take()
                m = mm(bank.ap, [(Wm[name][:, k, f * P:(f + 1) * P], src(k, c)) for k in range(2)], w=[bank.w, w])
                e = evac(f, c, bank, m)
                ps.give(bank, e)
                toks.append(e)
        return toks

    done = None
    for hf in range(2):
        lin, gel, xc, rt, gi, om, hs, y = [v2(b) for b in buf]
        flat = {id(v): b for v, b in zip((lin, gel, xc, rt, gi, om, hs, y), buf)}
        rt_ = []
        for c in range(2):
            stb = E["st_ring"].take()
            a = 8 * hf + 4 * c
            e = E["normalise"](R[:, 4 * c:4 * c + 4, :], X[:, a:a + 4, :], 4, P, "ln", [done], stb,
                               E["xtok"][a:a + 4])
            E["st_ring"].give(stb, e)
            rt_ += [e] * 4
        xt = [E["norm_chunk"](2 * hf + c, ["rms16"], g=W(n, "g1"), w=[wt],
                              source=(R[:, 4 * c:4 * c + 4, :], rt_[4 * c:4 * c + 4])) for c in range(2)]
        xs = lambda k, c: xnT[:, k, (2 * hf + c) * 512:(2 * hf + c + 1) * 512]
        at = lambda v, f, c: v[:, f, c * 512:(c + 1) * 512]
        t_lin = project("lin", xs, xt, lambda f, c, b, m: dve(
            V.tensor_scalar, at(lin, f, c), b.ap, col_("blin", f), None, ALU.add, w=[m, done]))
        t_gel = act(C.activation, buf[1], buf[0], ACT.Gelu, w=[t_lin, done])
        t_xc = project("conv", lambda k, c: at(lin, k, c), t_lin, lambda f, c, b, m: dve(
            V.tensor_scalar, at(xc, f, c), b.ap, col_("bconv", f), None, ALU.add, w=[m, done]))
        t_r = project("a", lambda k, c: at(xc, k, c), t_xc, lambda f, c, b, m: act(
            C.activation, at(rt, f, c), b.ap, ACT.Sigmoid, bias=col_("ba", f), w=[m, done]))
        t_i = project("x", lambda k, c: at(xc, k, c), t_xc, lambda f, c, b, m: act(
            C.activation, at(gi, f, c), b.ap, ACT.Sigmoid, bias=col_("bx", f), w=[m, done]))
        for f in range(2):
            t_a = act(C.activation, rt[:, f, :], rt[:, f, :], ACT.Exp, scale=la[:, f:f + 1], w=[t_r, lat])
        q = pool(G.tensor_tensor, buf[4], buf[4], buf[2], ALU.mult, w=[t_i, t_xc])
        o = dve(V.tensor_tensor, buf[5], buf[3], buf[3], ALU.mult, w=[t_a, done])
        z = dve(V.memset, buf[3].rearrange("p (b s) -> p b s", s=S)[:, :, 0:1], 0.0, w=[o])
        o = dve(V.tensor_scalar, buf[5], buf[5], -1.0, 1.0, ALU.mult, ALU.add, w=[o])
        o = act(C.activation, buf[5], buf[5], ACT.Sqrt, w=[o])
        o = dve(V.tensor_tensor, buf[4], buf[4], buf[5], ALU.mult, w=[o, q])
        o = dve(V.tensor_tensor_scan, buf[6], buf[3], buf[4], 0.0, ALU.mult, ALU.add, w=[o, z, done])
        o = dve(V.tensor_tensor, buf[7], buf[6], buf[1], ALU.mult, w=[o, t_gel])
        for c in range(2):
            for j in range(4):
                i = 4 * c + j
                rt_[i] = E["to_x"](i, lambda k: y[:, k, i * P:(i + 1) * P], 2, Wm["lin2"], [o],
                                   bias=W(n, "blin2")[0:1, :], onto=(R[:, i, :], [rt_[i], xt]))
                E["xtok"][8 * hf + i] = pool(G.tensor_tensor, X[:, 8 * hf + i, :], X[:, 8 * hf + i, :], R[:, i, :],
                                             ALU.add, w=[rt_[i], E["xtok"][8 * hf + i]])
        xt = [E["norm_chunk"](2 * hf + c, ["rms16"], g=W(n, "g2"),
                              source=(R[:, 4 * c:4 * c + 4, :], rt_[4 * c:4 * c + 4])) for c in range(2)]
        t_s = project("w1", xs, xt, lambda f, c, b, m: act(
            C.activation, at(gel, f, c), b.ap, ACT.Sigmoid, bias=col_("b1", f), w=[m, o]))
        t_g = act(C.activation, buf[1], buf[1], ACT.Gelu, w=[t_s])
        t_c = project("w2", xs, xt, lambda f, c, b, m: dve(
            V.scalar_tensor_tensor, at(lin, f, c), b.ap, col_("b2", f), at(gel, f, c), ALU.add, ALU.mult,
            w=[m, t_g, t_xc]))
        for t in range(8):
            m = E["to_x"](8 * hf + t, lambda k: lin[:, k, t * P:(t + 1) * P], 2, Wm["w3"], t_c,
                          bias=W(n, "b3")[0:1, :])
        done = [m, t_c, o, xt, pool.now()]
        E["finished"](n, 2 * hf)
        E["finished"](n, 2 * hf + 1)


def mamba(E, n):
    pe, act, dve, pool, T, V, C, G, ps, mm, X, xnT, W, Wk, copy = get(E)
    wt = E["wtok"][n]
    mine = E["order"][n] % 2
    _, width = offsets(SPEC[n])
    ar = E["Arena"]([(E["scr"], 0, E["NSCR"]), (E["Wr"][mine], width, WREG)])
    other = E["Arena"]([(E["Wr"][1 - mine], 0, WREG)])
    u, cd = other.get(2048), other.get(2048).rearrange("p (f k m) -> p f k m", f=4, k=4)
    deltas, dus = [[other.get(2048), ar.get(2048)] for _ in range(2)]
    ra, rb = ar.ring(2048, 3), ar.ring(2048, 3)
    bs, cs = ar.ring(512, 2), ar.ring(512, 3)
    tt = ar.get(4096)
    parts = [ar.get(256).bitcast(BF16) for _ in range(2)]
    dd = ar.get(512).rearrange("p (f m) -> p f m", f=4)
    sel = ar.get(16).bitcast(BF16)
    sel_c = sel.unsqueeze(2).to_broadcast([P, 32, P])
    dsum = ar.get(4)
    t1, t2 = tt[:, 0:2048], tt[:, 2048:4096]
    up = tt[:, 0:2072].rearrange("p (f b s) -> p f b s", f=4, b=2)
    dtb, xbc, r1 = [tt[:, 2560 + 512 * i:3072 + 512 * i] for i in range(3)]
    v4 = lambda a: a.rearrange("p (f n) -> p f n", f=4)
    uv = v4(u)
    E["inputs_of"](n, [0])
    xts = E["ahead"]
    ident = E["ident"]
    conv = Wk(n, "conv", 4)
    for f in range(4):
        for k in range(4):
            t_cd = dve(V.tensor_scalar, cd[:, f, k, :], ident, conv[:, f, k:k + 1], None, ALU.mult,
                       w=[wt])
    t_d = dve(V.tensor_tensor, dsum, W(n, "D0"), W(n, "D1"), ALU.add)
    for f in range(4):
        t_d = dve(V.tensor_scalar, dd[:, f, :], ident, dsum[:, f:f + 1], None, ALU.mult, w=[t_d])
    t_sel = dve(V.tensor_copy, sel, E["K"]("sel"), w=[E["c_tok"]])
    As = []
    for d in range(2):
        a = W(n, f"A{d}")
        q = act(C.activation, a, a, ACT.Exp, w=[wt])
        t_A = dve(V.tensor_scalar, a, a, -1.0, None, ALU.mult, w=[q])
        As.append(a.rearrange("p (f n) -> p f n", f=4))
    Win, Wout = Wk(n, "Win", 2), Wk(n, "Wout", 4)
    last = {"exp": [[], []], "g": [[], []], "sel": [[], []], "u": [], "tt": []}

    def ready(k):
        c, d = divmod(k, 2)
        xs = lambda k: xnT[:, k, c * 512:(c + 1) * 512]
        if d == 0:
            t_up = pool(G.memset, up[:, :, :, 0:3], 0.0, w=[last["tt"]])
            ups = []
            for f in range(4):
                bank = ps.take()
                m = mm(bank.ap, [(Win[:, k, f * P:(f + 1) * P], xs(k)) for k in range(2)], w=[bank.w, xts[(n, c)], wt])
                e = act(C.activation, up[:, f, :, 3:259], bank.ap.rearrange("p (b s) -> p b s", b=2), ACT.Copy,
                        w=[m, last["tt"]])
                ps.give(bank, e)
                ups.append(e)
                if f % 2:
                    yield
            for f in range(4):
                bank = ps.take()
                m = mm(bank.ap, [(cd[:, f, k, :], up[:, f, :, k:k + S]) for k in range(4)],
                       w=[bank.w, ups[f], t_cd, t_up])
                e = act(C.activation, uv[:, f, :], bank.ap, ACT.Identity, bias=W(n, "bconv")[:, f:f + 1],
                        w=[m, last["u"]])
                ps.give(bank, e)
                if f % 2:
                    yield
            last["tt"] = [m]
            last["u_made"] = act(C.activation, u, u, ACT.Silu, w=[e])
            yield
        t_u = last["u_made"]
        wd, wb = Wk(n, f"Wxd{d}", 4), Wk(n, f"Wxb{d}", 4)
        bank = ps.take()
        m = mm(bank.ap[0:64, :], [(wd[:, k, :], uv[:, k, :]) for k in range(4)], w=[bank.w, t_u])
        e_dt = act(C.activation, dtb[0:64, :], bank.ap[0:64, :], ACT.Copy, w=[m, last["tt"]])
        ps.give(bank, e_dt)
        yield
        bank = ps.take()
        m = mm(bank.ap[0:96, :], [(wb[:, k, :], uv[:, k, :]) for k in range(4)], w=[bank.w])
        m_u = m
        pt = parts[d]
        q = act(C.activation, xbc[0:96, :], bank.ap[0:96, :], ACT.Copy, w=[m, last["tt"]])
        ps.give(bank, q)
        q = dve(V.tensor_copy, pt[0:96, :], xbc[0:96, :], w=[q, last["sel"][d]])
        for lo, hi in ((32, 64), (64, 96)):
            q = dve(V.tensor_tensor, r1[lo:hi, :], xbc[lo:hi, :], pt[lo:hi, :], ALU.subtract, w=[q, last["tt"]])
            q = dve(V.tensor_copy, pt[lo:hi, :], r1[lo:hi, :], w=[q])
        yield
        q = dve(V.tensor_tensor, r1[64:96, :], r1[64:96, :], pt[64:96, :], ALU.subtract, w=[q])
        t_p = dve(V.tensor_copy, pt[64:96, :], r1[64:96, :], w=[q])
        delta, du = deltas[d], dus[d]
        for f in range(4):
            bank = ps.take()
            m = mm(bank.ap, [(W(n, f"Wdt{d}", 64)[:, f * P:(f + 1) * P], dtb[0:64, :])], w=[bank.w, e_dt])
            e = act(C.activation, v4(delta)[:, f, :], bank.ap, ACT.Identity, bias=W(n, f"bdt{d}")[:, f:f + 1],
                    w=[m, last["g"][d]])
            ps.give(bank, e)
            if f % 2:
                yield
        q = act(C.activation, t1, delta, ACT.Abs, w=[e, last["tt"]])
        yield
        q = act(C.activation, t1, t1, ACT.Exp, scale=-1.0, w=[q])
        yield
        ql = act(C.activation, t2, t1, ACT.Ln, bias=E["one_ap"], w=[q, E["z_tok"], m, t_p])
        yield
        qo = dve(V.scalar_tensor_tensor, t2, delta, 0.0, t2, ALU.max, ALU.add, w=[ql])
        qm = dve(V.tensor_scalar, delta, t1, 1.0, -1.0, ALU.add, ALU.add, w=[q, qo])
        qm = pool(G.tensor_tensor, t1, t1, delta, ALU.subtract, w=[qm, ql])
        yield
        yield
        t_dl = dve(V.tensor_tensor, delta, t2, t1, ALU.add, w=[qo, qm])
        last["tt"] = [t_dl]
        yield
        t_du = pool(G.tensor_tensor, du, delta, u, ALU.mult, w=[t_dl, t_u, last["g"][d]])
        last["u"] = [t_du, m_u]
        yield dict(t_p=t_p, t_dl=t_dl, t_du=t_du)

    def gate(c):
        for f in range(4):
            bank = ps.take()
            m = mm(bank.ap, [(Win[:, k, 512 + f * P:512 + (f + 1) * P], xnT[:, k, c * 512:(c + 1) * 512])
                             for k in range(2)], w=[bank.w])
            e = act(C.activation, v4(t1)[:, f, :], bank.ap, ACT.Copy, w=[m, last["tt"]])
            ps.give(bank, e)
            if f % 2:
                yield
        yield act(C.activation, t1, t1, ACT.Silu, w=[e])

    made, hold, ys, gated_ = {}, {}, {}, {}

    def behind(k):
        if k + 1 < 2 * NB // 2:
            for r in ready(k + 1):
                if r:
                    made[k + 1] = r
                yield
        else:
            E["late_weights"]([pe.now(), act.now(), dve.now(), pool.now()])
        if k % 2:
            for r in gate(k // 2):
                if r:
                    gated_[k // 2] = r
                yield

    def head(k, s_):
        d = k % 2
        mk = made[k]
        delta, du = deltas[d], dus[d]
        bb, bc = ps.take(), ps.take()
        m = mm(bb.ap, [(sel_c[0:96, s_, :], parts[d][0:96, :])], w=[bb.w, mk["t_p"], t_sel])
        m2 = mm(bc.ap, [(sel_c[0:96, 16 + s_, :], parts[d][0:96, :])], w=[bc.w])
        da, db, b_, c_ = ra.take(), rb.take(), bs.take(), cs.take()
        e = act(C.activation, b_.ap, bb.ap, ACT.Copy, w=[m, b_.w])
        ps.give(bb, e)
        e2 = act(C.activation, c_.ap, bc.ap, ACT.Copy, w=[m2, c_.w])
        ps.give(bc, e2)
        for f in range(4):
            x = act(C.activation, v4(da.ap)[:, f, :], v4(delta)[:, f, :], ACT.Exp,
                    scale=As[d][:, f, s_:s_ + 1], w=[mk["t_dl"], da.w, t_A])
        g = pool(G.tensor_tensor, v4(db.ap), v4(du), b_.ap.unsqueeze(1).to_broadcast([P, 4, 512]),
                 ALU.mult, w=[e, mk["t_du"], db.w])
        bs.give(b_, g)
        reset = 0 if d == 0 else S - 1
        z = pool(G.memset, da.ap.rearrange("p (b s) -> p b s", s=S)[:, :, reset:reset + 1], 0.0, w=[x])
        hold[16 * k + s_] = (da, db, c_, e2, z, g)
        if s_ == 15:
            last["g"][d], last["sel"][d] = [x, g], [m2]

    def tail(k, s_):
        d = k % 2
        c = k // 2
        if k % 2 == 0 and s_ == 0:
            ys[c] = [ps.take() for _ in range(4)]
            for f in range(4):
                m = mm(ys[c][f].ap, [(dd[:, f, :], uv[:, f, :])], w=[ys[c][f].w, last["u_made"], t_d], last=False)
        da, db, bc, m2, z, g = hold.pop(16 * k + s_)
        r = slice(None, None, 1 if d == 0 else -1)
        q = dve(V.tensor_tensor_scan, db.ap[:, r], da.ap[:, r], db.ap[:, r], 0.0, ALU.mult, ALU.add,
                w=[z, g])
        q = dve(V.tensor_tensor, v4(da.ap), v4(db.ap), bc.ap.unsqueeze(1).to_broadcast([P, 4, 512]),
                ALU.mult, w=[q, m2])
        cs.give(bc, q)
        for f in range(4):
            m = mm(ys[c][f].ap, [(ident, v4(da.ap)[:, f, :])], w=[q], first=False,
                   last=(d == 1 and s_ == 15))
        ra.give(da, m)
        rb.give(db, q)
        if k % 2 and s_ == 15:
            y = v4(t2)
            for f in range(4):
                q = dve(V.scalar_tensor_tensor, y[:, f, :], ys[c][f].ap, 0.5, v4(t1)[:, f, :], ALU.mult,
                        ALU.mult, w=[m, gated_[c], last["tt"]])
                ps.give(ys[c][f], q)
            for j in range(4):
                mo = E["to_x"](4 * c + j, lambda k: y[:, k, j * P:(j + 1) * P], 4, Wout, [q])
            last["tt"] = [q, mo]
            E["finished"](n, c)

    for r in ready(0):
        if r:
            made[0] = r
    run = iter(())
    N = 16 * 8
    for i in range(N + 2):
        E["poll"]()
        if i % 16 == 0 and i < N:
            for _ in run:
                pass
        if i < N:
            head(*divmod(i, 16))
        if i > 1:
            tail(*divmod(i - 2, 16))
        if i % 32 == 4 and i + 32 < N:
            E["start_norm"](n, i // 32 + 1)
        if i % 16 == 1 and i < N:
            run = behind(i // 16)
        next(run, None)
    for _ in run:
        pass


SUB = {0: mamba, 1: latent_heads, 2: experts, 3: talking, 4: few_keys, 5: moe_heads, 6: local_heads,
       7: latent_heads, 8: signs, 9: gated, 10: few_keys, 11: ternary}


def kl(w):
    k = w.shape[0] // P
    return w.reshape(k, P, -1).transpose(1, 0, 2).reshape(P, -1)


def col(v):
    return v.reshape(-1, P).T


def row(v, at=0):
    v = v.reshape(-1)
    a = np.zeros((P, v.size), v.dtype)
    a[at] = v
    return a


def top(w):
    a = np.zeros((P, w.shape[1]), w.dtype)
    a[:w.shape[0]] = w
    return a


def constants(g, b):
    c = {}
    p = np.arange(P)
    c["ident"] = np.eye(P)
    c["sel"] = (p[:, None] % 32 == np.arange(32)[None, :])
    c["hm"] = (p[:, None] // 16 == np.arange(8)[None, :])
    inv = (np.float32(1.0) / np.float32(10000.0) ** (np.arange(8, dtype=np.float32) / np.float32(8))).astype(np.float32)
    ang = np.arange(256, dtype=np.float32)[:, None] * inv[None, :]
    cos, sin = np.cos(ang.astype(np.float64)), np.sin(ang.astype(np.float64))
    two = lambda a: a.reshape(2, P, 16).transpose(1, 0, 2).reshape(P, 32)
    c["cos"] = two(np.concatenate([cos, cos], 1))
    c["sin"] = two(np.concatenate([-sin, sin], 1))
    c["jgt"] = np.broadcast_to((np.arange(8)[None, :] < np.arange(8)[:, None]).reshape(1, 64), (P, 64))
    c["one"] = np.ones((P, P))
    c["lg1"], c["lb1"] = [np.zeros((P, 2)) if a is None else a for a in (g, b)]
    return np.concatenate([np.asarray(c[n], np.float32).reshape(P, w) for n, w in CONST], 1)


def window_constants():
    p = np.arange(P)
    i0, j0 = p[:, None], np.arange(128)[None, :]
    i1, j1 = p[:, None] + 128, np.arange(256)[None, :]
    part = lambda i, j: np.where((i >= j) & (i - j <= 64), (j - i).astype(np.float64), -1e33)
    dist = np.concatenate([part(i0, j0), part(i1, j1)], 1)
    r = np.arange(64)
    gsel = np.concatenate([(p[:, None] + 128 * t == 64 * (r[None, :] % 4)) for t in range(2)], 1)
    gmask = (p[:, None] // 4 == np.arange(256)[None, :] // 16)
    return [np.asarray(a, np.float32) for a in (dist, gsel, gmask)]


def blocks(n, a):
    if n == 0:
        bc = lambda w: np.concatenate([w[64:96]] * 3, 0).T
        return [kl(a["W_in"].T), top(a["fWdt"].T), top(a["bWdt"].T), kl(a["W_out"].T), kl(a["fWx"][:64].T),
                kl(a["bWx"][:64].T), kl(bc(a["fWx"])), kl(bc(a["bWx"])), kl(a["W_conv"].reshape(512, 4)),
                col(a["b_conv"]), col(a["fD"]), col(a["bD"]), col(a["fbdt"]), col(a["bbdt"]), kl(a["fA_log"]),
                kl(a["bA_log"])]
    if n == 1:
        return [kl(a["Wq"]), kl(a["Wkv"]), kl(a["Wout"]), col(a["ln_m_g"]), col(a["ln_m_b"]), col(a["ln_l_g"]),
                col(a["ln_l_b"])]
    if n == 2:
        b2 = top(a["rb2"])
        b2[8] = a["sb2"]
        return [kl(a["router_w"]), row(a["router_b"]), np.concatenate([col(a["rb1"].reshape(-1)), col(a["sb1"])], 1),
                b2]
    if n == 3:
        w = a["w_qkv"]
        return [kl(w[:, :512]), kl(w[:, 512:]), kl(a["w_out"].T), kl(np.repeat(a["w_pre"].T, 16, 0)),
                np.broadcast_to(a["w_post"].T.reshape(1, 256), (P, 256)), row(a["b_out"])]
    if n == 4:
        return [kl(a["Wq"].T), kl(a["Wk"].T), kl(a["Wv"].T), kl(a["Wo"].T), col(a["bq"]), col(a["bk"]), row(a["bv"]),
                row(a["bo"]), kl(a["fside"])]
    if n == 5:
        we = np.concatenate([np.concatenate([kl(a[m][e]) for m in ("Wq", "Wk", "Wv")], 1) for e in range(4)], 1)
        bqk = np.concatenate([np.concatenate([col(a["bq"][e]), col(a["bk"][e])], 1) for e in range(4)], 1)
        return [we, kl(a["Wo"]), kl(a["Wg1"]), kl(a["Wg2"]), col(a["bg1"]), row(a["bg2"]), bqk, row(a["bv"]),
                row(a["bo"])]
    if n == 6:
        c = window_constants()
        return [kl(np.concatenate([a["Wq"], a["Wk"]], 1)), kl(a["Wv"]), kl(a["Wo"])] + c
    if n == 7:
        return [kl(np.concatenate([a["W_q"], a["W_kv"][:, :256]], 1)), kl(a["W_kv"][:, 256:]), kl(a["W_out"]),
                col(a["ln_x_g"]), col(a["ln_x_b"]), col(a["ln_l_g"]), col(a["ln_l_b"]),
                col(np.concatenate([a["q_gamma"]] * 2)), col(np.concatenate([a["k_gamma"]] * 2)), row(a["b_out"])]
    if n == 9:
        ws = ["W_lin", "W_conv", "Wa", "Wx", "W_lin2", "W1", "W2", "W3"]
        bs = ["b_lin", "b_conv", "ba", "bx", "b1", "b2"]
        return [kl(a[w].T) for w in ws] + [col(a[b]) for b in bs] + [row(a["b_lin2"]), row(a["b3"]), col(a["g1"]),
                                                                     col(a["g2"]), col(a["Lam"])]
    if n == 10:
        return [kl(a[w].reshape(256, 1024)) for w in ("wq", "wk", "wv")] + [kl(a["wo"].reshape(1024, 256)),
                                                                          row(a["bo"])]
    if n == 11:
        return [kl(a["w_up"].T), kl(a["w_down"].T)]
    return None


NAMES = {0: "L0_attn_", 1: "L0_xattn_", 2: "L0_ffn_", 3: "L1_attn_", 4: "L1_xattn_", 5: "L1_ffn_", 6: "L2_attn_",
         7: "L2_xattn_", 8: "L2_ffn_", 9: "L3_attn_", 10: "L3_xattn_", 11: "L3_ffn_"}


def kernel(**inputs):
    import numpy as _np
    import concourse.bacc as _bacc
    from concourse import mybir as _mybir
    from concourse.bass_utils import run_bass_kernel_spmd as _run

    inp = {k: _np.asarray(v) for k, v in inputs.items()}
    g = [col(inp["L0_xattn_" + k]) if "L0_xattn_" + k in inp else None for k in ("ln_l_g", "ln_l_b")]
    arrays = {"const": constants(*g), "x": inp["x"], "ctx": inp["ctx_1024"]}
    for n in LAYERS:
        a = {k[len(NAMES[n]):]: v for k, v in inp.items() if k.startswith(NAMES[n])}
        a["fside"] = inp["fside_SxS2_0"]
        b = blocks(n, a)
        if b is not None:
            for (name, w), arr in zip(SPEC[n], b):
                assert arr.shape == (P, w), (n, name, arr.shape)
            arrays[f"w{n}"] = _np.concatenate(b, 1)
        if n == 2:
            arrays["we"] = _np.stack([_np.concatenate([kl(a["rw1"][e]), kl(a["rw2"][e])], 1) for e in range(8)]
                                     + [_np.concatenate([kl(a["sw1"]), kl(a["sw2"])], 1)])
        if n == 4:
            arrays["mbf"] = inp["mask_BxS2_bf0"]
        if n == 7:
            arrays["mbk"] = inp["mask_BxS2_bk0"]
        if n == 8:
            arrays["k0"] = kl(a["k0"])
            arrays["k1"] = kl(a["k1"])
            arrays["k2"] = kl(a["k2"])
            arrays["s"] = _np.broadcast_to(_np.stack([a["s0"], a["s1"], a["s2"]]).reshape(1, 3), (P, 3))
    nc = _bacc.Bacc("TRN2", target_bir_lowering=False, num_devices=1)
    maps, A = {}, {}
    for name, arr in arrays.items():
        arr = _np.ascontiguousarray(arr)
        maps[f"in_{name}"] = arr
        A[name] = nc.dram_tensor(f"in_{name}", arr.shape, _mybir.dt.from_np(arr.dtype), kind="ExternalInput").ap()
    out = nc.dram_tensor("out_0", (NB, S, D), F32, kind="ExternalOutput").ap()
    build(nc, A, out)
    r = _run(nc, [maps], core_ids=[0])
    return r.results[0]["out_0"]
```

```python
from contextlib import ExitStack

import concourse.bass as bass
import numpy as np
from concourse import mybir

LAYERS = [0, 1, 2, 3, 4, 5, 6, 7, 8, 9, 10, 11]

P = 128
NB = 8
S = 256
D = 256
NT = 16
S2 = 77
WREG = 8448
F32 = mybir.dt.float32
FR = mybir.dt.float32r
BF16 = mybir.dt.bfloat16
U8 = mybir.dt.uint8
ALU = mybir.AluOpType
ACT = mybir.ActivationFunctionType
AX = mybir.AxisListType

SPEC = {
    0: [("Win", 2048), ("Wdt0", 512), ("Wdt1", 512), ("Wout", 1024), ("Wxd0", 256), ("Wxd1", 256),
        ("Wxb0", 384), ("Wxb1", 384), ("conv", 16), ("bconv", 4), ("D0", 4), ("D1", 4), ("bdt0", 4), ("bdt1", 4),
        ("A0", 64), ("A1", 64)],
    1: [("Wq", 2048), ("Wkv", 4096), ("Wout", 2048), ("mg", 2), ("mb", 2), ("lg", 2), ("lb", 2)],
    2: [("rw", 16), ("rb", 8), ("b1", 36), ("b2", 256)],
    3: [("Wqk", 1024), ("Wv", 512), ("Wout", 512), ("wpre", 32), ("wpost", 256), ("bo", 256)],
    4: [("Wq", 512), ("Wk", 512), ("Wv", 512), ("Wo", 512), ("bq", 2), ("bk", 2), ("bv", 256), ("bo", 256),
        ("am", 154)],
    5: [("We", 6144), ("Wo", 512), ("Wg1", 256), ("Wg2", 4), ("bg1", 1), ("bg2", 4), ("bqk", 16), ("bv", 1024),
        ("bo", 256)],
    6: [("Wqk", 1024), ("Wv", 512), ("Wo", 512), ("dist", 384), ("gsel", 128), ("gmask", 256)],
    7: [("Wqk", 1024), ("Wv", 512), ("Wo", 512), ("xg", 2), ("xb", 2), ("lg", 2), ("lb", 2), ("gq", 1), ("gk", 1),
        ("bo", 256)],
    8: [],
    9: [("lin", 512), ("conv", 512), ("a", 512), ("x", 512), ("lin2", 512), ("w1", 512), ("w2", 512), ("w3", 512),
        ("blin", 2), ("bconv", 2), ("ba", 2), ("bx", 2), ("b1", 2), ("b2", 2), ("blin2", 256), ("b3", 256),
        ("g1", 2), ("g2", 2), ("lam", 2)],
    10: [("wq", 2048), ("wk", 2048), ("wv", 2048), ("wo", 2048), ("bo", 256)],
    11: [("up", 2048), ("down", 2048)],
}
CONST = [("ident", 128), ("sel", 32), ("hm", 8), ("cos", 32), ("sin", 32), ("jgt", 64), ("one", 128), ("lg1", 2), ("lb1", 2)]


def offsets(spec):
    at, out = 0, {}
    for name, n in spec:
        out[name] = (at, n)
        at += n
    return out, at


class Line:

    def __init__(self, sem):
        self.sem, self.n, self.items, self.seen = sem, 0, [], {}

    def wait(self, toks):
        for t in toks:
            if t is None or t == ():
                continue
            if isinstance(t, list):
                self.wait(t)
                continue
            sem, value = t
            if self.seen.get(id(sem), 0) < value:
                self.seen[id(sem)] = value
                self.items.append((sem, value))

    def __call__(self, f, *args, w=(), sig=True, **kw):
        self.wait(list(w))
        self.n += 1 if sig else 0
        self.items.append((f, args, kw, self.sem if sig else None, 1))
        return (self.sem, self.n)

    def now(self):
        return (self.sem, self.n)

    def play(self, eng):
        for it in self.items:
            if len(it) == 2:
                eng.wait_ge(it[0], it[1])
                continue
            f, args, kw, sem, by = it
            ins = f(*args, **kw)
            if sem is not None:
                ins.then_inc(sem, by)


class Buf:
    def __init__(self, ap):
        self.ap, self.w = ap, []


class Ring:

    def __init__(self, aps):
        self.free = [Buf(a) for a in aps]

    def take(self):
        return self.free.pop(0)

    def give(self, b, *toks):
        b.w = list(toks)
        self.free.append(b)


def build(nc, A, out):
    ctx = ExitStack()
    with ctx:
        def sb(name, n, dt=F32):
            return ctx.enter_context(nc.sbuf_tensor(name, [P, n], dt))

        pe, act, dve, pool, sp = [Line(ctx.enter_context(nc.semaphore("s_" + n)))
                                  for n in ("pe", "act", "dve", "pool", "sp")]
        T, V, C, G = nc.tensor, nc.vector, nc.scalar, nc.gpsimd

        dsem = [ctx.enter_context(nc.semaphore(f"dma{i}")) for i in range(32)]
        dcount = [0]

        def dma(dst, src, w=()):
            i = dcount[0]
            dcount[0] += 1
            sem, k = dsem[i % 32], i // 32
            sp.wait([(sem, 16 * k)] if k else [])
            sp.wait(list(w))
            sp.items.append((nc.sync.dma_start, (dst, src), {}, sem, 16))
            return (sem, 16 * (k + 1))

        X = sb("X", NT * D)[:, :].rearrange("p (t d) -> p t d", t=NT)
        xnT = sb("xnT", 2 * 2048)[:, :].rearrange("p (k n) -> p k n", k=2)
        XNr = sb("XNr", 2 * 1024)
        stat = sb("stat", 2 * 64)
        coff, cw = offsets(CONST)
        cst = sb("cst", cw)
        ctxT = sb("ctxT", 2 * 616)[:, :].rearrange("p (k n) -> p k n", k=2)
        cnT = sb("cnT", 2 * 616)[:, :].rearrange("p (k n) -> p k n", k=2)
        cz = sb("cz", 8)
        NSCR = 23040
        Wr = [None, sb("W1", WREG)]
        above = []

        def overlay(level, *parts):
            while len(above) > level:
                above.pop().close()
            above.append(ExitStack())
            return [above[-1].enter_context(nc.sbuf_tensor(name, [P, k], dt)) for name, k, dt in parts]

        Wr[0], = overlay(0, ("W0", WREG, F32))
        scr, = overlay(1, ("scr", NSCR, F32))
        PS = ctx.enter_context(nc.psum_tensor("PS", [P, 8, 512], F32))
        ps = Ring([PS[:, i, :] for i in range(8)])
        xn_ring = Ring([XNr[:, i * 1024:(i + 1) * 1024].rearrange("p (t d) -> p t d", t=4) for i in range(2)])
        st_ring = Ring([stat[:, i * 64:(i + 1) * 64] for i in range(2)])

        def K(name, rows=P):
            o, n = coff[name]
            return cst[0:rows, o:o + n]

        ident = K("ident")
        ones = K("one")

        class Arena:
            def __init__(self, segs):
                self.segs = list(segs)

            def get(self, n):
                for i, (t, lo, hi) in enumerate(self.segs):
                    if hi - lo >= n:
                        self.segs[i] = (t, lo + n, hi)
                        return t[:, lo:lo + n]
                raise ValueError(f"arena: {n} of {[(b - a) for _, a, b in self.segs]}")

            def ring(self, n, count):
                return Ring([self.get(n) for _ in range(count)])

        c_tok = dma(cst[:, :], A["const"])
        xv = A["x"].rearrange("b (h p) d -> p (b h) d", p=P)
        xtok = [None] * NT
        for c in range(4):
            t = dma(X[:, 4 * c:4 * c + 4, :], xv[:, 4 * c:4 * c + 4, :])
            for j in range(4):
                xtok[4 * c + j] = t

        bars = []

        def barrier():
            toks = [e.now() for e in (pe, act, dve, pool) if e.n]
            for e in (pe, act, dve, pool):
                e.wait(toks)
            bars.append(toks)
            return toks

        wtok = {}

        def load_weights(n, w):
            off, width = offsets(SPEC[n])
            if width:
                wtok[n] = dma(Wr[order[n] % 2][:, 0:width], A[f"w{n}"], w)

        order = {n: i for i, n in enumerate(LAYERS)}

        def W(n, name, rows=P):
            off, _ = offsets(SPEC[n])
            o, k = off[name]
            return Wr[order[n] % 2][0:rows, o:o + k]

        def Wk(n, name, kt):
            return W(n, name).rearrange("p (k f) -> p k f", k=kt)

        def mm(o, pairs, w=(), first=True, last=True, sig=True):
            for i, (l, r) in enumerate(pairs):
                t = pe(T.matmul, o, l, r, start=(first and i == 0), stop=(last and i == len(pairs) - 1),
                       w=w if i == 0 else (), sig=sig and i == len(pairs) - 1)
            return t

        flip = [0]

        def copy(o, i, w=(), on=None):
            if on is None:
                flip[0] ^= 1
                on = act if flip[0] else dve
            if on is act:
                return act(C.activation, o, i, ACT.Copy, w=w)
            return on(V.tensor_copy, o, i, w=w)

        z_tok = dve(V.memset, cz[:, 0:1], 1e-5)
        z_tok = dve(V.memset, cz[:, 1:2], 1.0)
        eps_ap = cz[:, 0:1]
        one_ap = cz[:, 1:2]

        def normalise_steps(dst, src, n, rows, kind, w, st, tile_w=None):
            mv = st.ap[0:rows, 0:2 * n].rearrange("p (t s) -> p t s", s=2)
            bs = st.ap[0:rows, 8:8 + 6 * n].rearrange("p (t s) -> p t s", s=6)
            sd = st.ap[0:rows, 40:40 + n]
            rs = st.ap[0:rows, 48:48 + n]
            ms = st.ap[0:rows, 56:56 + n]
            for j in range(n):
                wj = w if tile_w is None else [w, tile_w[j]]
                t = dve(V.bn_stats, bs[:, j, :], src[:, j, :], w=[st.w, wj])
            for j in range(n):
                t = dve(V.bn_aggr, mv[:, j, :], bs[:, j, :], w=[t])
            yield None
            if kind == "ln":
                t = act(C.activation, sd, mv[:, :, 1], ACT.Sqrt, bias=eps_ap[0:rows], w=[t, z_tok])
                yield None
                t = dve(V.reciprocal, rs, sd, w=[t])
                for j in range(n):
                    t = dve(V.tensor_scalar, dst[:, j, :], src[:, j, :], mv[:, j, 0:1], rs[:, j:j + 1],
                            ALU.subtract, ALU.mult, w=[t])
            else:
                t = dve(V.tensor_tensor, ms, mv[:, :, 0], mv[:, :, 0], ALU.mult, w=[t])
                t = dve(V.tensor_tensor, ms, ms, mv[:, :, 1], ALU.add, w=[t])
                yield None
                if kind == "rms16":
                    t = act(C.activation, sd, ms, ACT.Sqrt, scale=256.0, w=[t])
                    yield None
                    t = dve(V.tensor_scalar, sd, sd, 1e-12, 0.0625, ALU.max, ALU.mult, w=[t])
                else:
                    t = act(C.activation, sd, ms, ACT.Sqrt, w=[t])
                    yield None
                    t = dve(V.tensor_scalar, sd, sd, 1e-8, None, ALU.add, w=[t])
                t = dve(V.reciprocal, rs, sd, w=[t])
                for j in range(n):
                    t = dve(V.tensor_scalar, dst[:, j, :], src[:, j, :], rs[:, j:j + 1], None, ALU.mult, w=[t])
            yield t

        def normalise(*args):
            for t in normalise_steps(*args):
                pass
            return t

        def norm_steps(c, toks, kinds, g=None, b=None, w=(), source=None):
            while not (xn_ring.free and st_ring.free):
                yield
            xb, st = xn_ring.take(), st_ring.take()
            src, t = X[:, 4 * c:4 * c + 4, :], [xb.w, w]
            tw = xtok[4 * c:4 * c + 4]
            if source is not None:
                src, tw = source
            for kind in kinds:
                for r in normalise_steps(xb.ap, src, 4, P, kind, [t], st, tw):
                    yield
                t = r
                src, tw = xb.ap, None
            st_ring.give(st, t)
            for k in range(2):
                bank = ps.take()
                for j in range(4):
                    tt = pe(T.transpose, bank.ap[:, j * P:(j + 1) * P], xb.ap[:, j, k * P:(k + 1) * P], ident,
                            w=[t, bank.w, c_tok], sig=j == 3)
                o = xnT[:, k, c * 512:(c + 1) * 512]
                if g is not None:
                    e = act(C.activation, o, bank.ap, ACT.Identity, scale=g[:, k:k + 1],
                            bias=b[:, k:k + 1] if b is not None else 0.0, w=[tt, w])
                else:
                    e = copy(o, bank.ap, w=[tt])
                ps.give(bank, e)
                toks.append(e)
            xn_ring.give(xb, tt)

        def norm_chunk(c, kinds, **kw):
            toks = []
            for _ in norm_steps(c, toks, kinds, **kw):
                pass
            return toks

        NORM = {1: (["ln", "ln"], "lg", "lb"), 7: (["ln", "ln"], "lg", "lb"), 11: (["ln", "rms"],)}
        ahead = {}
        running = []

        def start_norm(n, c):
            kinds, *gb = NORM.get(n, (["ln"],))
            toks = []
            if n == 1:
                kw = dict(g=K("lg1"), b=K("lb1"), w=[c_tok])
            else:
                kw = dict(g=W(n, gb[0]), b=W(n, gb[1]), w=[wtok[n]]) if gb else {}
            running.append(norm_steps(c, toks, kinds, **kw))
            ahead[(n, c)] = toks

        def poll():
            for g in list(running):
                if next(g, "end") == "end":
                    running.remove(g)

        def finished(n, c):
            i = order[n] + 1
            if i < len(LAYERS) and LAYERS[i] != 9:
                while len(running) >= 2:
                    poll()
                start_norm(LAYERS[i], c)

        class Inputs:

            def __init__(self, n, chunks):
                self.n = n
                for c in chunks:
                    if (n, c) not in ahead:
                        start_norm(n, c)

            def __getitem__(self, c):
                toks = ahead[(self.n, c)]
                while len(toks) < 2:
                    poll()
                return toks

            def __iter__(self):
                return (self[c] for c in range(4))

        def inputs_of(n, chunks=range(4)):
            return Inputs(n, chunks)

        def to_x(t, yT, kt, Wo, w, bias=None, scale=None, onto=None):
            bank = ps.take()
            pairs = [(yT(k), Wo[:, k, :]) for k in range(kt)]
            if bias is not None:
                pairs.append((ones[0:1, :], bias))
            m = mm(bank.ap[:, 0:D], pairs, w=[w, bank.w])
            if onto is not None:
                e = dve(V.tensor_tensor, onto[0], onto[0], bank.ap[:, 0:D], ALU.add, w=[m, onto[1]])
                ps.give(bank, e)
                return e
            if scale is None:
                xtok[t] = dve(V.tensor_tensor, X[:, t, :], X[:, t, :], bank.ap[:, 0:D], ALU.add, w=[m, xtok[t]])
            else:
                xtok[t] = dve(V.scalar_tensor_tensor, X[:, t, :], bank.ap[:, 0:D], scale, X[:, t, :], ALU.mult,
                              ALU.add, w=[m, xtok[t]])
            ps.give(bank, xtok[t])
            return m

        env = dict(nc=nc, T=T, V=V, C=C, G=G, pe=pe, act=act, dve=dve, pool=pool, dma=dma, X=X, xnT=xnT, ps=ps, A=A,
                   K=K, ident=ident, ones=ones, Arena=Arena, W=W, Wk=Wk, mm=mm, copy=copy, one_ap=one_ap,
                   eps_ap=eps_ap, z_tok=z_tok, normalise=normalise, norm_chunk=norm_chunk, to_x=to_x, xtok=xtok,
                   wtok=wtok, scr=scr, NSCR=NSCR, Wr=Wr, order=order, c_tok=c_tok, ctxT=ctxT, cnT=cnT,
                   barrier=barrier, XNr=XNr, norm_steps=norm_steps, normalise_steps=normalise_steps, running=running, poll=poll, start_norm=start_norm, ahead=ahead, finished=finished, inputs_of=inputs_of, st_ring=st_ring, xn_ring=xn_ring, PS=PS, bars=bars)
        env["ctx_tok"] = None
        if any(n in LAYERS for n in (1, 4, 7, 10)):
            env["ctx_tok"] = load_context(env)
        load_weights(LAYERS[0], [])
        for i, n in enumerate(LAYERS):
            b = barrier()
            after = LAYERS[i + 1] if i + 1 < len(LAYERS) else None
            env["late_weights"] = lambda w: load_weights(after, w) if after is not None else None
            if n != 0:
                env["late_weights"](b)
            if n == 2:
                env["wide"], = overlay(1, ("wide2", NSCR, FR))
            if n == 3:
                env["wide"], env["scr"] = overlay(1, ("wide3", 6144, FR), ("narrow3", NSCR - 6144, F32))
            if n == 8:
                env["wide"] = overlay(0, ("wide8", 30720, FR), ("narrow8", 768, F32))
            SUB[n](env, n)
            if n in (2, 3):
                env["scr"], = overlay(1, (f"scr{n}", NSCR, F32))
            if n == 8:
                Wr[0], = overlay(0, ("W08", WREG, F32))
                env["scr"], = overlay(1, ("scr8", NSCR, F32))
        dones = []
        for c in range(4):
            ov = out.rearrange("b (h p) d -> p (b h) d", p=P)
            dones.append(dma(ov[:, 4 * c:4 * c + 4, :], X[:, 4 * c:4 * c + 4, :], xtok[4 * c:4 * c + 4]))
        sp.wait(dones)
        for i, s in enumerate(dsem):
            n = (dcount[0] - i + 31) // 32
            if n > 0:
                sp.wait([(s, 16 * n)])
        while above:
            above.pop().close()
        block = ctx.enter_context(nc.Block())
        block.sync(lambda e: sp.play(e))
        block.tensor(lambda e: pe.play(e))
        block.scalar(lambda e: act.play(e))
        block.vector(lambda e: dve.play(e))
        block.gpsimd(lambda e: pool.play(e))


def load_context(E):
    pe, T, V, dve, ps, dma = E["pe"], E["T"], E["V"], E["dve"], E["ps"], E["dma"]
    ar = E["Arena"]([(E["scr"], 0, E["NSCR"])])
    raw = ar.get(8 * D).rearrange("p (t d) -> p t d", t=8)
    nrm = ar.get(8 * D).rearrange("p (t d) -> p t d", t=8)
    ld = dma(raw[0:S2, :, :], E["A"]["ctx"].rearrange("b s d -> s b d"))
    st = E["st_ring"].take()
    toks = []
    t = []
    for h in range(2):
        t = E["normalise"](nrm[0:S2, 4 * h:4 * h + 4, :], raw[0:S2, 4 * h:4 * h + 4, :], 4, S2, "ln", [ld, t], st)
    E["st_ring"].give(st, t)
    for src, dst, w in ((raw, E["ctxT"], ld), (nrm, E["cnT"], t)):
        for k in range(2):
            for h in range(2):
                bank = ps.take()
                for j in range(4):
                    m = pe(T.transpose, bank.ap[:, j * S2:(j + 1) * S2], src[0:S2, 4 * h + j, k * P:(k + 1) * P],
                           E["ident"][0:S2, 0:S2], w=[w, bank.w, E["c_tok"]], sig=j == 3)
                e = E["copy"](dst[:, k, 4 * h * S2:4 * (h + 1) * S2], bank.ap[:, 0:4 * S2], w=[m])
                ps.give(bank, e)
                toks.append(e)
    return toks


def ternary_weights(E, n):
    pe, act, dve, pool, T, V, C, ps = E["pe"], E["act"], E["dve"], E["pool"], E["T"], E["V"], E["C"], E["ps"]
    mm, wt = E["mm"], E["wtok"][n]
    ar = E["Arena"]([(E["Wr"][E["order"][n] % 2], 4096, WREG)])
    small = ar.get(16)
    red = ar.get(64)
    a, s, g = [ar.get(1024) for _ in range(3)]
    ready = []
    E["ternary"] = (small, ready)
    t = None
    for m, name in enumerate(("up", "down")):
        w = E["W"](n, name)
        q = dve(V.tensor_reduce, red, w.rearrange("p (a b) -> p a b", a=64), AX.X, ALU.add,
                apply_absolute_value=True, w=[wt, t])
        q = dve(V.tensor_reduce, small[:, m:m + 1], red, AX.X, ALU.add, w=[q])
        yield
        bank = ps.take()
        q = mm(bank.ap[:, 0:1], [(E["ones"], small[:, m:m + 1])], w=[q, bank.w])
        th = small[:, 4 + m:5 + m]
        tq = dve(V.tensor_scalar, th, bank.ap[:, 0:1], 0.5 / (1024 * 256), None, ALU.mult, w=[q])
        ps.give(bank, tq)
        yield
        for i in range(2):
            wi = w[:, 1024 * i:1024 * i + 1024]
            q1 = act(C.activation, a, wi, ACT.Abs, w=[wt, t, tq])
            q2 = act(C.activation, s, wi, ACT.Sign, w=[wt, t])
            yield
            q = dve(V.scalar_tensor_tensor, g, a, th, s, ALU.is_gt, ALU.mult, w=[tq, q1, q2, t])
            q = dve(V.tensor_tensor, g, g, wi, ALU.subtract, w=[q])
            t = dve(V.tensor_tensor, wi, wi, g, ALU.add, w=[q])
            yield
        ready.append(t)


def ternary(E, n):
    pe, act, dve, pool, T, V, C, ps = E["pe"], E["act"], E["dve"], E["pool"], E["T"], E["V"], E["C"], E["ps"]
    mm, X, xnT, wt = E["mm"], E["X"], E["xnT"], E["wtok"][n]
    ar = E["Arena"]([(E["scr"], 0, E["NSCR"])])
    if "ternary" not in E:
        E["running"].append(ternary_weights(E, n))
    xts = E["inputs_of"](n)
    while "ternary" not in E or len(E["ternary"][1]) < 2:
        E["poll"]()
    small, ready = E["ternary"]
    up = E["Wk"](n, "up", 2)
    down = E["Wk"](n, "down", 8)
    hs = ar.ring(4096, 2)
    sq = ar.ring(4096, 2)
    prev = None

    def second(c, hb, ht, qb, qt):
        h = hb.ap.rearrange("p (f n) -> p f n", f=8)
        q = qb.ap.rearrange("p (f n) -> p f n", f=8)
        for j in range(4):
            tl = 4 * c + j
            bank = ps.take()
            s1 = mm(bank.ap[:, 0:D], [(h[:, k, j * P:(j + 1) * P], down[:, k, :]) for k in range(8)],
                    w=[bank.w, ht, ready[1]])
            s2 = mm(bank.ap[:, 256:257], [(q[:, k, j * P:(j + 1) * P], E["ones"][:, 0:1]) for k in range(8)], w=[qt])
            r = small[:, 8 + 2 * (tl % 2):9 + 2 * (tl % 2)]
            r2 = small[:, 9 + 2 * (tl % 2):10 + 2 * (tl % 2)]
            u = act(C.activation, r, bank.ap[:, 256:257], ACT.Sqrt, scale=1.0 / 1024, w=[s2, E["xtok"][tl - 2]])
            u = dve(V.tensor_scalar, r, r, 1e-8, None, ALU.add, w=[u])
            u = dve(V.reciprocal, r2, r, w=[u])
            E["xtok"][tl] = dve(V.scalar_tensor_tensor, X[:, tl, :], bank.ap[:, 0:D], r2, X[:, tl, :], ALU.mult,
                                ALU.add, w=[u, s1, E["xtok"][tl]])
            ps.give(bank, E["xtok"][tl])
        sq.give(qb, s2)
        hs.give(hb, s1, qt)

    for c in range(4):
        xt = xts[c]
        hb, qb = hs.take(), sq.take()
        h = hb.ap.rearrange("p (f n) -> p f n", f=8)
        for f in range(8):
            bank = ps.take()
            m = mm(bank.ap, [(up[:, k, f * P:(f + 1) * P], xnT[:, k, c * 512:(c + 1) * 512]) for k in range(2)],
                   w=[bank.w, xt, ready[0]])
            ht = act(C.activation, h[:, f, :], bank.ap, ACT.Gelu, w=[m, hb.w])
            ps.give(bank, ht)
            qt = pool(E["G"].tensor_tensor, qb.ap[:, f * 512:(f + 1) * 512], h[:, f, :], h[:, f, :], ALU.mult,
                      w=[ht, qb.w])
        if prev:
            second(*prev)
        prev = (c, hb, ht, qb, qt)
    second(*prev)


def parts_of(E, src, hi, lo, w):
    dve, V = E["dve"], E["V"]
    th = dve(V.tensor_copy, hi, src, w=w)
    return [th, dve(V.tensor_tensor, lo, src, hi, ALU.subtract, w=[th])]


def signs(E, n):
    pe, act, dve, pool, T, V, C, G, ps = [E[k] for k in ("pe", "act", "dve", "pool", "T", "V", "C", "G", "ps")]
    mm, X, xnT, A, dma = E["mm"], E["X"], E["xnT"], E["A"], E["dma"]
    wide, narrow = E["wide"]
    ar = E["Arena"]([(wide, 0, 30720)])
    w0, w1, w2 = ar.get(2048), ar.get(8192), ar.get(2048)
    hr = ar.ring(8192, 2)
    xh, xl = ar.get(1024), ar.get(1024)
    stage = E["cnT"].rearrange("p k n -> p (k n)")
    sc = narrow[:, 0:8]
    bar = E["bars"][-1]
    raw0, raw1, raw2 = stage[:, 0:1024].bitcast(U8), stage[:, 0:1024].bitcast(U8), narrow[:, 256:768].bitcast(U8)
    t0 = dma(raw0, A["k0"], bar)
    t2 = dma(raw2, A["k2"], bar)
    ts = dma(sc[:, 0:3], A["s"], bar)
    k0 = raw0.rearrange("p (h n) -> p h n", h=2)
    q = dve(V.tensor_tensor, w0, k0[:, 0, :], k0[:, 1, :], ALU.subtract, w=[t0])
    r0 = dve(V.tensor_scalar, w0, w0, 2.0, None, ALU.mult, w=[q])
    r2 = dve(V.tensor_scalar, w2, raw2, 2.0, -1.0, ALU.mult, ALU.add, w=[t2])
    rs = dve(V.tensor_scalar, sc[:, 4:6], sc[:, 0:2], 2.0, None, ALU.mult, w=[ts])
    r1 = r0
    for i in range(2):
        t1 = dma(raw1, A["k1"][:, 4096 * i:4096 * i + 4096], [r1])
        r1 = dve(V.tensor_scalar, w1[:, 4096 * i:4096 * i + 4096], raw1, 2.0, -1.0, ALU.mult, ALU.add, w=[t1])
    fr = Ring([stage[:, 0:512], stage[:, 512:1024]])
    for b in fr.free:
        b.w = [r1]
    w0, w1, w2 = [a.rearrange("p (k f) -> p k f", k=k) for a, k in ((w0, 2), (w1, 8), (w2, 8))]
    xl = xl.rearrange("p (k n) -> p k n", k=2)
    xh = xh.rearrange("p (k n) -> p k n", k=2)
    xts = E["inputs_of"](n)
    free_x = []

    def split_x(c):
        return parts_of(E, xnT[:, :, c * 512:(c + 1) * 512], xh, xl, [xts[c], free_x])

    def layer(s, wm, kt, cur, ht):
        hb = hr.take()
        hi, lo = [a.rearrange("p (f n) -> p f n", f=8) for a in (hb.ap[:, 0:4096], hb.ap[:, 4096:8192])]
        es = []
        for f in range(8):
            E["poll"]()
            bank = ps.take()
            m = mm(bank.ap, [(wm[:, k, f * P:(f + 1) * P], part[:, k, :]) for k in range(kt) for part in cur],
                   w=[bank.w, ht, r0, r1])
            fb = fr.take()
            e = act(C.activation, fb.ap, bank.ap, ACT.Relu, scale=sc[:, 4 + s:5 + s], w=[m, rs, fb.w])
            ps.give(bank, e)
            th, tl = parts_of(E, fb.ap, hi[:, f, :], lo[:, f, :], [e, hb.w])
            fr.give(fb, tl)
            es += [th, tl]
        return hb, (hi, lo), es, m

    first = layer(0, w0, 2, (xh, xl), split_x(0))
    for c in range(4):
        fb_, cur, es, free_x = first
        xt = split_x(c + 1) if c < 3 else None
        sb_, cur, es, m = layer(1, w1, 8, cur, es)
        hr.give(fb_, m)
        if c < 3:
            first = layer(0, w0, 2, (xh, xl), xt)
        for j in range(4):
            t = 4 * c + j
            bank = ps.take()
            m = mm(bank.ap[:, 0:D], [(part[:, k, j * P:(j + 1) * P], w2[:, k, :]) for k in range(8) for part in cur],
                   w=[bank.w, es, r2])
            E["xtok"][t] = dve(V.scalar_tensor_tensor, X[:, t, :], bank.ap[:, 0:D], sc[:, 2:3], X[:, t, :], ALU.mult,
                               ALU.add, w=[m, E["xtok"][t]])
            ps.give(bank, E["xtok"][t])
        hr.give(sb_, m)
        E["finished"](n, c)


def experts(E, n):
    pe, act, dve, pool, T, V, C, G, ps = [E[k] for k in ("pe", "act", "dve", "pool", "T", "V", "C", "G", "ps")]
    mm, X, xnT, A, dma, W = E["mm"], E["X"], E["xnT"], E["A"], E["dma"], E["W"]
    reg = E["Wr"][E["order"][n] % 2]
    _, width = offsets(SPEC[n])
    ar, wide = E["Arena"]([(reg, width, WREG)]), E["Arena"]([(E["wide"], 0, E["NSCR"])])
    ring = ar.ring(2048, 2)
    gr = ar.ring(512, 2)
    wr, hr = wide.ring(2048, 3), wide.ring(4096, 2)
    xp = [wide.get(4096).rearrange("p (c k n) -> p c k n", c=4, k=2) for _ in range(2)]
    bar = E["bars"][-1]
    wt = E["wtok"][n]
    lg = ar.get(NT * 8).rearrange("p (t e) -> p t e", e=8)
    pr = ar.get(NT * 8).rearrange("p (t e) -> p t e", e=8)
    wg = ar.get(NT * 9).rearrange("p (t e) -> p t e", e=9)
    mx = ar.get(NT)
    sm = ar.get(NT)
    cmp1, cmp2 = ar.get(64), ar.get(64)
    wT = ar.get(2048)
    slots = []

    def load(e):
        b = ring.take()
        slots.append((b, dma(b.ap, A["we"][e], [bar, b.w])))

    def split(e, m):
        b = wr.take()
        sb_, st = slots[e]
        toks = parts_of(E, sb_.ap[:, 1024 * m:1024 * m + 1024], b.ap[:, 0:1024], b.ap[:, 1024:2048], [st, b.w])
        if m:
            ring.give(sb_, toks)
            if e + 2 < 9:
                load(e + 2)
        k = 2 if m == 0 else 4
        return b, [a.rearrange("p (k f) -> p k f", k=k) for a in (b.ap[:, 0:1024], b.ap[:, 1024:2048])], toks

    def three(l, r, k):
        return [(l[0][k], r[0][k]), (l[0][k], r[1][k]), (l[1][k], r[0][k])]

    for e in range(2):
        load(e)
    rw = W(n, "rw").rearrange("p (k e) -> p k e", k=2)
    xts = E["inputs_of"](n)
    bank = ps.take()
    for t in range(NT):
        m = mm(bank.ap[:, t * 8:t * 8 + 8], [(xnT[:, k, t * P:(t + 1) * P], rw[:, k, :]) for k in range(2)]
               + [(E["ones"][0:1, :], W(n, "rb")[0:1, :])], w=[bank.w, xts[t // 4], wt])
    lv = bank.ap[:, 0:128].rearrange("p (t e) -> p t e", e=8)
    t = dve(V.tensor_reduce, mx, lv, AX.X, ALU.max, w=[m])
    t = dve(V.tensor_tensor, lg, lv, mx.unsqueeze(2).to_broadcast([P, NT, 8]), ALU.subtract, w=[t])
    ps.give(bank, t)
    t = act(C.activation, pr, lg, ACT.Exp, w=[t])
    t = dve(V.tensor_reduce, sm, pr, AX.X, ALU.add, w=[t])
    t = dve(V.reciprocal, mx, sm, w=[t])
    t = dve(V.tensor_tensor, pr, pr, mx.unsqueeze(2).to_broadcast([P, NT, 8]), ALU.mult, w=[t])
    jgt = E["K"]("jgt").rearrange("p (e j) -> p e j", e=8)
    rk = ar.get(NT * 8).rearrange("p (t e) -> p t e", e=8)
    for g in range(2):
        c1 = cmp1.rearrange("p (t e) -> p t e", t=8)
        c2 = cmp2.rearrange("p (t e) -> p t e", t=8)
        pv = pr[:, 8 * g:8 * g + 8, :]
        for e in range(8):
            me = pv[:, :, e:e + 1].to_broadcast([P, 8, 8])
            a1, a2 = c1, c2
            q = dve(V.tensor_tensor, a1, pv, me, ALU.is_gt, w=[t])
            q = dve(V.tensor_tensor, a2, pv, me, ALU.is_equal, w=[q, t])
            q = dve(V.tensor_tensor, a2, a2, jgt[:, e, :].unsqueeze(1).to_broadcast([P, 8, 8]), ALU.mult, w=[q])
            q = dve(V.tensor_tensor, a1, a1, a2, ALU.add, w=[q])
            t = dve(V.tensor_reduce, rk[:, 8 * g:8 * g + 8, e], a1, AX.X, ALU.add, w=[q])
    t1 = dve(V.memset, wg[:, :, 8:9], 1.0)
    t = dve(V.scalar_tensor_tensor, wg[:, :, 0:8], rk, 1.5, pr, ALU.is_lt, ALU.mult, w=[t])
    for g in range(4):
        bank = ps.take()
        for j in range(4):
            m = pe(T.transpose, bank.ap[0:9, j * P:(j + 1) * P], wg[:, 4 * g + j, :], E["ident"], w=[t, t1, bank.w],
                   sig=j == 3)
        wtt = dve(V.tensor_copy, wT[0:9, g * 512:(g + 1) * 512], bank.ap[0:9, :], w=[m])
        ps.give(bank, wtt)
    b1 = W(n, "b1")
    xt = [parts_of(E, xnT[:, :, c * 512:(c + 1) * 512], xp[0][:, c], xp[1][:, c], [xts[c]]) for c in range(4)]

    def second(e, c, hb, hp, ht, w2):
        bw2, w2p, tw2 = w2
        for j in range(4):
            tl = 4 * c + j
            sl = slice(j * P, (j + 1) * P)
            b = ps.take()
            m = mm(b.ap[:, 0:D], [p for k in range(4) for p in three([{k: h[:, k, sl]} for h in hp],
                                                                    [{k: w[:, k, :]} for w in w2p], k)],
                   w=[ht, tw2, b.w], last=e < 8)
            if e < 8:
                E["xtok"][tl] = dve(V.scalar_tensor_tensor, X[:, tl, :], b.ap[:, 0:D], wg[:, tl, e:e + 1],
                                    X[:, tl, :], ALU.mult, ALU.add, w=[m, t, E["xtok"][tl]])
            else:
                m = mm(b.ap[:, 0:D], [(wT[0:9, tl * P:(tl + 1) * P], W(n, "b2")[0:9, :])], w=[wtt], first=False)
                E["xtok"][tl] = dve(V.tensor_tensor, X[:, tl, :], X[:, tl, :], b.ap[:, 0:D], ALU.add,
                                    w=[m, E["xtok"][tl]])
            ps.give(b, E["xtok"][tl])
        hr.give(hb, m)
        if c == 3:
            wr.give(bw2, m)
        if e == 8:
            E["finished"](n, c)
        return m

    prev = None
    nw1 = split(0, 0)
    for e in range(9):
        bw1, w1p, tw1 = nw1
        w2 = None
        for c in range(4):
            hb = hr.take()
            hp = [a.rearrange("p (f n) -> p f n", f=4) for a in (hb.ap[:, 0:2048], hb.ap[:, 2048:4096])]
            es = []
            for f in range(4):
                E["poll"]()
                bank = ps.take()
                m = mm(bank.ap, [p for k in range(2) for p in three([{k: w[:, k, f * P:(f + 1) * P]} for w in w1p],
                                                                    [{k: x[:, c, k, :]} for x in xp], k)],
                       w=[bank.w, tw1, xt[c]])
                gb = gr.take()
                g = act(C.activation, gb.ap, bank.ap, ACT.Gelu, bias=b1[:, 4 * e + f:4 * e + f + 1], w=[m, gb.w])
                ps.give(bank, g)
                ht = parts_of(E, gb.ap, hp[0][:, f, :], hp[1][:, f, :], [g, hb.w])
                gr.give(gb, ht)
                es += ht
            if c == 3:
                wr.give(bw1, m)
            if prev:
                second(*prev)
            if c == 0:
                w2 = split(e, 1)
            if c == 2 and e < 8:
                nw1 = split(e + 1, 0)
            prev = (e, c, hb, hp, es, w2)
    second(*prev)


def pipe(E, n, *stages):
    later = []

    def on():
        for g in list(later):
            if next(g, "end") == "end":
                later.remove(g)

    for s in range(n + max(l for l, _ in stages)):
        E["poll"]()
        for i, (lag, f) in enumerate(stages):
            if i == len(stages) - 1:
                on()
            if 0 <= s - lag < n:
                g = f(s - lag)
                if g is not None:
                    later.append(g)
    while later:
        on()


class Behind:

    def __init__(self, pro):
        self.pro, self.made, self.run = pro, {}, None

    def start(self, b):
        if b < NB:
            self.run = (b, self.pro(b))

    def step(self):
        if self.run:
            b, g = self.run
            r = next(g, "end")
            if r == "end":
                self.run = None
            elif r is not None:
                self.made[b] = r

    def end(self):
        while self.run:
            self.step()


def turn(E, bank, srcs, w):
    pe, T = E["pe"], E["T"]
    for i, (c, s, r, m) in enumerate(srcs):
        t = pe(T.transpose, bank.ap[0:m, c:c + r], s, E["ident"][0:r, 0:r], w=[w, bank.w], sig=i == len(srcs) - 1)
    return t


def finish_heads(E, n, b, Osb, ot_ring, Wo, bo, w, osb_give):
    inner = Osb.shape[2]
    kt = inner // P
    ob = ot_ring.take()
    ot = ob.ap.rearrange("p (k n) -> p k n", k=kt)
    toks = []
    for k in range(0, kt, 2):
        bank = E["ps"].take()
        m = turn(E, bank, [((kk * 2 + it) * P, Osb[:, it, (k + kk) * P:(k + kk + 1) * P], P, P)
                           for kk in range(2) for it in range(2)], w)
        e = E["copy"](ob.ap[:, k * S:(k + 2) * S], bank.ap, w=[m, ob.w])
        E["ps"].give(bank, e)
        toks.append(e)
    osb_give(m)
    yield
    for it in range(2):
        m = E["to_x"](2 * b + it, lambda k: ot[:, k, it * P:(it + 1) * P], kt, Wo, [toks], bias=bo)
    ot_ring.give(ob, m)
    if b % 2:
        E["finished"](n, b // 2)


def get(E):
    return [E[k] for k in ("pe", "act", "dve", "pool", "T", "V", "C", "G", "ps", "mm", "X", "xnT", "W", "Wk", "copy")]


def rope_tile(E, t, Wqk, bufs, w):
    pe, act, dve, pool, T, V, C, G, ps, mm, X, xnT, W, Wk, copy = get(E)
    it = t % 2
    bank = ps.take()
    m = mm(bank.ap, [(xnT[:, k, t * P:(t + 1) * P], Wqk[:, k, :]) for k in range(2)], w=[bank.w, w])
    rb, tb = bufs[0].take(), bufs[1].take()
    cos = E["K"]("cos")[:, 16 * it:16 * it + 16]
    sin = E["K"]("sin")[:, 16 * it:16 * it + 16]
    v = bank.ap.rearrange("p (h d) -> p h d", d=16)
    a = rb.ap.rearrange("p (h d) -> p h d", d=16)
    c = tb.ap.rearrange("p (h d) -> p h d", d=16)
    q1 = dve(V.tensor_tensor, a, v, cos.unsqueeze(1).to_broadcast([P, 32, 16]), ALU.mult, w=[m, rb.w])
    q2 = dve(V.tensor_tensor, c[:, :, 0:8], v[:, :, 8:16], sin[:, 0:8].unsqueeze(1).to_broadcast([P, 32, 8]),
             ALU.mult, w=[m, tb.w])
    q2 = dve(V.tensor_tensor, c[:, :, 8:16], v[:, :, 0:8], sin[:, 8:16].unsqueeze(1).to_broadcast([P, 32, 8]),
             ALU.mult, w=[m])
    ps.give(bank, q2)
    q = pool(G.tensor_tensor, rb.ap, rb.ap, tb.ap, ALU.add, w=[q1, q2])
    bufs[1].give(tb, q)

    def turned():
        bank = ps.take()
        m = turn(E, bank, [(j * P, rb.ap[:, j * P:(j + 1) * P], P, P) for j in range(4)], [q])
        bufs[0].give(rb, m)
        return bank, m
    return turned


def talking(E, n):
    pe, act, dve, pool, T, V, C, G, ps, mm, X, xnT, W, Wk, copy = get(E)
    wt = E["wtok"][n]
    ar, wide = E["Arena"]([(E["scr"], 0, E["NSCR"] - 6144)]), E["Arena"]([(E["wide"], 0, 6144)])
    Wqk, Wv, Wo = Wk(n, "Wqk", 2), Wk(n, "Wv", 2), Wk(n, "Wout", 2)
    rbufs = (ar.ring(512, 2), ar.ring(512, 2))
    kr, qg = wide.ring(1024, 2), wide.ring(1024, 4)
    qr, vr = ar.ring(512, 2), ar.ring(512, 2)
    pr, pt, vh = ar.ring(512, 4), ar.ring(512, 3), ar.ring(512, 6)
    ot = ar.ring(512, 2)
    sm = ar.ring(8, 6)
    wpre = W(n, "wpre").rearrange("p (k g) -> p k g", k=2)
    wpost = W(n, "wpost")
    xts = E["inputs_of"](n)
    st = {}

    def pro(b):
        qb, kb, vb = qr.take(), kr.take(), vr.take()
        q, v = [z.ap.rearrange("p (k n) -> p k n", k=2) for z in (qb, vb)]
        k = kb.ap.rearrange("p (o k n) -> p o k n", o=2, k=2)
        toks = []
        for it in range(2):
            t = 2 * b + it
            turned = rope_tile(E, t, Wqk, rbufs, [xts[b // 2], wt])
            yield
            yield
            yield
            bank, m = turned()
            bv = bank.ap.rearrange("p (j n) -> p j n", j=4)
            e1 = act(C.activation, q[:, :, it * P:(it + 1) * P], bv[:, 0:2, :], ACT.Copy, scale=0.25, w=[m, qb.w])
            sl = slice(it * P, (it + 1) * P)
            e2 = act(C.activation, k[:, 0, :, sl], bv[:, 2:4, :], ACT.Copy, w=[m, kb.w])
            e2 = dve(V.tensor_tensor, k[:, 1, :, sl], bv[:, 2:4, :], k[:, 0, :, sl], ALU.subtract, w=[e1, e2])
            ps.give(bank, e1, e2)
            bank = ps.take()
            m = mm(bank.ap[:, 0:D], [(xnT[:, k2, t * P:(t + 1) * P], Wv[:, k2, :]) for k2 in range(2)], w=[bank.w])
            e3 = copy(v[:, it, :], bank.ap[:, 0:D], w=[m, vb.w])
            ps.give(bank, e3)
            toks += [e1, e2, e3]
            yield
        yield dict(q=q, k=k, v=v, bufs=(qb, kb, vb), t=toks)

    next_ = Behind(pro)
    st = next_.made

    def sa(u):
        b, g = divmod(u, 16)
        if g == 0:
            if b == 0:
                next_.start(0)
            next_.end()
        if g == 1:
            next_.start(b + 1)
        next_.step()
        s = st[b]
        gb = qg.take()
        gv = gb.ap.rearrange("p (o k n) -> p o k n", o=2, k=2)
        for k in range(2):
            e = dve(V.tensor_scalar, gv[:, 0, k, :], s["q"][:, k, :], wpre[:, k, g:g + 1], None, ALU.mult,
                    w=[s["t"], gb.w])
        for k in range(2):
            e = dve(V.scalar_tensor_tensor, gv[:, 1, k, :], s["q"][:, k, :], wpre[:, k, g:g + 1], gv[:, 0, k, :],
                    ALU.mult, ALU.subtract, w=[e])
        vb = vh.take()
        ve = pool(G.tensor_tensor, vb.ap.rearrange("p (j g d) -> p j g d", j=2, g=16),
                  s["v"].rearrange("p j (g d) -> p j g d", g=16),
                  wpost[:, 16 * g:16 * g + 16].unsqueeze(1).unsqueeze(3).to_broadcast([P, 2, 16, 16]), ALU.mult,
                  w=[s["t"], vb.w])
        s[g] = (gb, gv, e, vb, ve)

    def s0(u):
        b, g = divmod(u, 16)
        s = st[b]
        gb, gv, e, vb, ve = s[g]
        bank = ps.take()
        for it in range(2):
            m = mm(bank.ap[:, it * S:(it + 1) * S],
                   [(gv[:, i, k, it * P:(it + 1) * P], s["k"][:, j, k, :]) for k in range(2)
                    for i, j in ((0, 0), (0, 1), (1, 0))], w=[e, bank.w])
        qg.give(gb, m)
        if g == 15:
            qr.give(s["bufs"][0], e)
            kr.give(s["bufs"][1], m)
            vr.give(s["bufs"][2], ve)
        sb_ = sm.take()
        pb = pr.take()
        p = pb.ap.rearrange("p (i n) -> p i n", i=2)
        sv = bank.ap.rearrange("p (i n) -> p i n", i=2)
        r = dve(V.tensor_reduce, sb_.ap[:, 0:2], sv, AX.X, ALU.max, negate=True, w=[m, sb_.w])
        for it in range(2):
            x = act(C.activation, p[:, it, :], sv[:, it, :], ACT.Exp, bias=sb_.ap[:, it:it + 1],
                    accum_out=sb_.ap[:, 2 + it:3 + it], w=[r, pb.w])
        ps.give(bank, x)
        s[g] = (sb_, pb, p, x, vb, ve)

    def sn(u):
        b, g = divmod(u, 16)
        s = st[b]
        sb_, pb, p, x, vb, ve = s[g]
        r = dve(V.reciprocal, sb_.ap[:, 4:6], sb_.ap[:, 2:4], w=[x])
        for it in range(2):
            x = dve(V.tensor_scalar, p[:, it, :], p[:, it, :], sb_.ap[:, 4 + it:5 + it], None, ALU.mult, w=[r])
        sm.give(sb_, x)
        s[g] = (pb, p, x, vb, ve)

    def s1(u):
        b, g = divmod(u, 16)
        pb, p, x, vb, ve = st[b][g]
        bank = ps.take()
        m = turn(E, bank, [((jt * 2 + it) * P, p[:, it, jt * P:(jt + 1) * P], P, P) for jt in range(2)
                           for it in range(2)], [x])
        pr.give(pb, m)
        tb = pt.take()
        e = copy(tb.ap, bank.ap, w=[m, tb.w])
        ps.give(bank, e)
        st[b][g] = (tb, e, vb, ve)

    def s2(u):
        b, g = divmod(u, 16)
        s = st[b]
        tb, e, vb, ve = s[g]
        if g == 0:
            s["o"] = [ps.take(), ps.take()]
        v = vb.ap.rearrange("p (j n) -> p j n", j=2)
        for f in range(2):
            m = mm(s["o"][f].ap[:, 0:S], [(v[:, j, f * P:(f + 1) * P], tb.ap[:, j * S:(j + 1) * S])
                                          for j in range(2)], w=[e, ve, s["o"][f].w], first=g == 0, last=g == 15)
        pt.give(tb, m)
        vh.give(vb, m)
        if g == 15:
            ob = ot.take()
            o = ob.ap.rearrange("p (k n) -> p k n", k=2)
            es = []
            for f in range(2):
                es.append(copy(o[:, f, :], s["o"][f].ap[:, 0:S], w=[m, ob.w]))
                ps.give(s["o"][f], es[-1])
            return end(b, ob, o, es)

    def end(b, ob, o, es):
        for it in range(2):
            m = E["to_x"](2 * b + it, lambda k: o[:, k, it * P:(it + 1) * P], 2, Wo, [es],
                          bias=W(n, "bo")[0:1, :])
        ot.give(ob, m)
        if b % 2:
            E["finished"](n, b // 2)
        yield

    pipe(E, 16 * NB, (0, sa), (1, s0), (2, sn), (3, s1), (4, s2))


def moe_heads(E, n):
    pe, act, dve, pool, T, V, C, G, ps, mm, X, xnT, W, Wk, copy = get(E)
    wt = E["wtok"][n]
    ar = E["Arena"]([(E["scr"], 0, E["NSCR"])])
    We = W(n, "We").rearrange("p (e n) -> p e n", e=4)
    Wo = Wk(n, "Wo", 2)
    pool_ = ar.get(16).rearrange("p (k b) -> p k b", k=2)
    hid = ar.get(8)
    hb_ = ar.get(1024).rearrange("p (b n) -> p b n", b=8)
    gw = ar.get(32).rearrange("p (b e) -> p b e", e=4)
    rk = ar.get(32).rearrange("p (b e) -> p b e", e=4)
    a1, a2 = [ar.get(32).rearrange("p (b e) -> p b e", e=4) for _ in range(2)]
    sm8 = ar.get(8)
    xts = E["inputs_of"](n)
    t = dve(V.tensor_reduce, pool_, xnT.rearrange("p k (b s) -> p k b s", b=8), AX.X, ALU.add, w=[*xts])
    t = dve(V.tensor_scalar, pool_, pool_, 1.0 / 256, None, ALU.mult, w=[t])
    bank = ps.take()
    wg1 = Wk(n, "Wg1", 2)
    m = mm(bank.ap[:, 0:8], [(wg1[:, k, :], pool_[:, k, :]) for k in range(2)], w=[t, wt, bank.w])
    t = act(C.activation, hid, bank.ap[:, 0:8], ACT.Relu, bias=W(n, "bg1"), w=[m])
    t = dve(V.tensor_copy, hb_, hid.unsqueeze(2).to_broadcast([P, 8, P]), w=[t])
    for b in range(8):
        m = mm(bank.ap[:, 16 + 4 * b:20 + 4 * b], [(hb_[:, b, :], W(n, "Wg2")),
                                                   (E["ones"][0:1, :], W(n, "bg2")[0:1, :])], w=[t])
    lv = bank.ap[:, 16:48].rearrange("p (b e) -> p b e", e=4)
    t = dve(V.tensor_reduce, sm8, lv, AX.X, ALU.max, w=[m])
    lg = ar.get(32).rearrange("p (b e) -> p b e", e=4)
    t = dve(V.tensor_tensor, gw, lv, sm8.unsqueeze(2).to_broadcast([P, 8, 4]), ALU.subtract, w=[t])
    t = dve(V.tensor_copy, lg, lv, w=[t])
    ps.give(bank, t)
    x = act(C.activation, gw, gw, ACT.Exp, w=[t])
    jgt = E["K"]("jgt").rearrange("p (e j) -> p e j", e=8)
    for e in range(4):
        me = lg[:, :, e:e + 1].to_broadcast([P, 8, 4])
        q = dve(V.tensor_tensor, a1, lg, me, ALU.is_gt, w=[t])
        q = dve(V.tensor_tensor, a2, lg, me, ALU.is_equal, w=[q])
        q = dve(V.tensor_tensor, a2, a2, jgt[:, e, 0:4].unsqueeze(1).to_broadcast([P, 8, 4]), ALU.mult, w=[q])
        q = dve(V.tensor_tensor, a1, a1, a2, ALU.add, w=[q])
        t = dve(V.tensor_reduce, rk[:, :, e], a1, AX.X, ALU.add, w=[q])
    t = dve(V.scalar_tensor_tensor, gw, rk, 1.5, gw, ALU.is_lt, ALU.mult, w=[t, x])
    t = dve(V.tensor_reduce, sm8, gw, AX.X, ALU.add, w=[t])
    t = dve(V.reciprocal, sm8, sm8, w=[t])
    gt = dve(V.tensor_tensor, gw, gw, sm8.unsqueeze(2).to_broadcast([P, 8, 4]), ALU.mult, w=[t])

    wcr = ar.ring(1536, 1)
    bcr = ar.ring(260, 1)
    qr, vr, kmr = ar.ring(512, 2), ar.ring(512, 2), ar.ring(4096, 2)
    att = Heads16(E, n, ar, Wo, W(n, "bo")[0:1, :])
    bqk = W(n, "bqk").rearrange("p (e c) -> p e c", e=4)
    bv = W(n, "bv")[0:1, :].rearrange("p (e c) -> p e c", e=4)

    def pro(b):
        wb, bb = wcr.take(), bcr.take()
        for e in range(4):
            g = gw[:, b, e:e + 1]
            g0 = gw[0:1, b, e:e + 1]
            if e == 0:
                c1 = [dve(V.tensor_scalar, wb.ap[:, c:c + 768], We[:, e, c:c + 768], g, None, ALU.mult,
                          w=[gt, wb.w, wt]) for c in (0, 768)]
                c2 = dve(V.tensor_scalar, bb.ap[:, 0:4], bqk[:, e, :], g, None, ALU.mult, w=[bb.w])
                c3 = dve(V.tensor_scalar, bb.ap[0:1, 4:260], bv[:, e, :], g0, None, ALU.mult)
            else:
                c2 = dve(V.scalar_tensor_tensor, bb.ap[:, 0:4], bqk[:, e, :], g, bb.ap[:, 0:4], ALU.mult, ALU.add,
                         w=[c2])
                c3 = dve(V.scalar_tensor_tensor, bb.ap[0:1, 4:260], bv[:, e, :], g0, bb.ap[0:1, 4:260], ALU.mult,
                         ALU.add, w=[c3])
                for i, c in enumerate((0, 768)):
                    c1[i] = dve(V.scalar_tensor_tensor, wb.ap[:, c:c + 768], We[:, e, c:c + 768], g,
                                wb.ap[:, c:c + 768], ALU.mult, ALU.add, w=[c1[i]])
                    yield
            yield
        wc = wb.ap.rearrange("p (m k n) -> p m k n", m=3, k=2)
        qb, vb, kb = qr.take(), vr.take(), kmr.take()
        q = qb.ap.rearrange("p (k n) -> p k n", k=2)
        v = vb.ap.rearrange("p (k n) -> p k n", k=2)
        km = kb.ap.rearrange("p (k h n) -> p k h n", k=2, h=8)
        xb = xnT[:, :, b * S:(b + 1) * S]
        toks = []
        for f in range(2):
            bank = ps.take()
            m1 = mm(bank.ap[:, 0:S], [(wc[:, 0, k, f * P:(f + 1) * P], xb[:, k, :]) for k in range(2)],
                    w=[c1, c2, c3, bank.w])
            m = mm(bank.ap[:, S:2 * S], [(wc[:, 1, k, f * P:(f + 1) * P], xb[:, k, :]) for k in range(2)])
            e1 = dve(V.tensor_scalar, q[:, f, :], bank.ap[:, 0:S], bb.ap[:, f:f + 1], 0.25, ALU.add, ALU.mult,
                     w=[m, qb.w])
            kt_ = att.kraw.take()
            e2 = act(C.activation, kt_.ap, bank.ap[:, S:2 * S], ACT.Identity, bias=bb.ap[:, 2 + f:3 + f],
                     w=[m, e1, kt_.w])
            ps.give(bank, e1, e2)
            e3 = att.mask(km[:, f, :, :], kt_.ap, S, [e2, kb.w])
            att.kraw.give(kt_, e3)
            toks += [e1, e3]
            yield
        bank = ps.take()
        for it in range(2):
            m = mm(bank.ap[:, it * S:(it + 1) * S], [(xb[:, k, it * P:(it + 1) * P], wc[:, 2, k, :])
                                                     for k in range(2)]
                   + [(E["ones"][0:1, :], bb.ap[0:1, 4:260])], w=[bank.w])
        e = copy(vb.ap, bank.ap, w=[m, vb.w])
        ps.give(bank, e)
        wcr.give(wb, m)
        bcr.give(bb, m)
        yield dict(q=q, v=v, km=km, t=toks + [e],
                    free=[(vr, vb)], free_qk=[(qr, qb), (kmr, kb)])

    att.run(pro)


class Heads16:

    def __init__(self, E, n, ar, Wo, bo, local=False):
        self.E, self.local, self.Wo, self.bo, self.n = E, local, Wo, bo, n
        self.kraw = ar.ring(256, 2)
        self.pr, self.pt = ar.ring(512, 5), ar.ring(512, 4)
        self.osb, self.ot = ar.ring(512, 1), ar.ring(512, 2)
        self.sm = ar.ring(8, 8)
        self.sums = ar.ring(64, 3)
        if local:
            self.g = ar.ring(512, 1)

    def mask(self, o, k, n, w):
        E = self.E
        return E["pool"](E["G"].tensor_tensor, o, k.unsqueeze(1).to_broadcast([P, 8, n]),
                         E["K"]("hm").unsqueeze(2).to_broadcast([P, 8, n]), ALU.mult, w=w)

    def run(self, pro, extra=None):
        pe, act, dve, pool, T, V, C, G, ps, mm, X, xnT, W, Wk, copy = get(self.E)
        E, local = self.E, self.local
        st = {}
        next_ = Behind(pro)

        def s0(u):
            b, r = divmod(u, 16)
            if r == 0:
                if b == 0:
                    next_.start(0)
                next_.end()
                st[b] = next_.made[b]
                st[b]["sum"] = self.sums.take()
            if r == (5 if local else 1):
                next_.start(b + 1)
            next_.step()
            s = st[b]
            sb_, pb = self.sm.take(), self.pr.take()
            bank = ps.take()
            sums = s["sum"].ap[:, 0:32].rearrange("p (i h) -> p i h", i=2)
            if local:
                kt, h8 = divmod(r, 8)
                lw = [(0, 0, P, 0, r), (1, P, S, 1, r)]
                for it, c, n, _, _ in lw:
                    m = mm(bank.ap[:, c:c + n], [(s["q"][:, kt, it * P:(it + 1) * P], s["km"][:, kt, h8, 0:n])],
                           w=[s["t"], bank.w])
                r_ = dve(V.scalar_tensor_tensor, pb.ap[:, 0:384], W(self.n, "dist"), float(2.0 ** (-(r + 1) * 0.5)),
                         bank.ap[:, 0:384], ALU.mult, ALU.add, w=[m, pb.w])
                ps.give(bank, r_)
                for it, c, n, _, _ in lw:
                    q = dve(V.tensor_reduce, sb_.ap[:, it:it + 1], pb.ap[:, c:c + n], AX.X, ALU.max, negate=True,
                            w=[r_, sb_.w])
                for it, c, n, _, _ in lw:
                    x = act(C.activation, pb.ap[:, c:c + n], pb.ap[:, c:c + n], ACT.Exp, bias=sb_.ap[:, it:it + 1],
                            accum_out=sums[:, it, r:r + 1], w=[q, s["sum"].w])
            else:
                kt, r2 = divmod(r, 8)
                pair, it = divmod(r2, 2)
                m = mm(bank.ap, [(s["q"][:, kt, it * P:(it + 1) * P],
                                  s["km"][:, kt, 2 * pair:2 * pair + 2, :])], w=[s["t"], bank.w])
                sv = bank.ap.rearrange("p (i n) -> p i n", i=2)
                q = dve(V.tensor_reduce, sb_.ap[:, 0:2], sv, AX.X, ALU.max, negate=True, w=[m, sb_.w])
                for j in range(2):
                    h = 8 * kt + 2 * pair + j
                    x = act(C.activation, pb.ap[:, j * S:(j + 1) * S], sv[:, j, :], ACT.Exp,
                            bias=sb_.ap[:, j:j + 1], accum_out=sums[:, it, h:h + 1], w=[q, pb.w, s["sum"].w])
                ps.give(bank, x)
            self.sm.give(sb_, x)
            s[r] = (pb, x)
            if r == 15:
                if extra:
                    m, s["more"] = extra(b, s)
                for ring, buf in s["free_qk"]:
                    ring.give(buf, m)

        def s1(u):
            b, r = divmod(u, 16)
            if local and r == 15:
                next(st[b]["more"])
            pb, x = st[b][r]
            bank = ps.take()
            n = 3 if local else 4
            m = turn(E, bank, [(j * P, pb.ap[:, j * P:(j + 1) * P], P, P) for j in range(n)], [x])
            self.pr.give(pb, m)
            tb = self.pt.take()
            e = copy(tb.ap[:, 0:n * P], bank.ap[:, 0:n * P], w=[m, tb.w])
            ps.give(bank, e)
            st[b][r] = (tb, e, x)

        def s2(u):
            b, r = divmod(u, 16)
            s = st[b]
            tb, e, x = s[r]
            if r == 0:
                s["o"] = ps.take()
            o = s["o"].ap.rearrange("p (i n) -> p i n", i=2)
            pt = tb.ap
            if local:
                items = [(0, r, [(0, 0)]), (1, r, [(1, 0), (2, 1)])]
            else:
                kt, r2 = divmod(r, 8)
                pair, it = divmod(r2, 2)
                items = [(it, 8 * kt + 2 * pair + j, [(2 * j, 0), (2 * j + 1, 1)]) for j in range(2)]
            for it, h, parts in items:
                m = mm(o[:, it, 16 * h:16 * h + 16],
                       [(pt[:, c * P:(c + 1) * P], s["v"][:, jt, 16 * h:16 * h + 16]) for c, jt in parts],
                       w=[e, s["o"].w])
            self.pt.give(tb, m)
            if r < 15:
                return
            if local:
                s["og"], s["og_t"] = next(s["more"])
            rs = s["sum"].ap[:, 32:64]
            q = dve(V.reciprocal, rs, s["sum"].ap[:, 0:32], w=[x])
            ob = self.osb.take()
            ov = ob.ap.rearrange("p (g d) -> p g d", d=16)
            q = dve(V.tensor_tensor, ov, s["o"].ap.rearrange("p (g d) -> p g d", d=16),
                    rs.unsqueeze(2).to_broadcast([P, 32, 16]), ALU.mult, w=[q, m, ob.w])
            ps.give(s["o"], q)
            self.sums.give(s["sum"], q)
            if local:
                q = dve(V.tensor_tensor, ob.ap, ob.ap, s["og"].ap, ALU.add, w=[q, s["og_t"]])
                ps.give(s["og"], q)
            for ring, buf in s["free"]:
                ring.give(buf, m)
            return finish_heads(E, self.n, b, ob.ap.rearrange("p (i n) -> p i n", i=2), self.ot, self.Wo, self.bo, [q],
                                lambda tok: self.osb.give(ob, tok))

        pipe(E, 16 * NB, (0, s0), (3, s1), (5, s2))


def local_heads(E, n):
    pe, act, dve, pool, T, V, C, G, ps, mm, X, xnT, W, Wk, copy = get(E)
    wt = E["wtok"][n]
    ar = E["Arena"]([(E["scr"], 0, E["NSCR"])])
    Wqk, Wv, Wo = Wk(n, "Wqk", 2), Wk(n, "Wv", 2), Wk(n, "Wo", 2)
    rbufs = (ar.ring(512, 2), ar.ring(512, 1))
    qr, vr, kmr = ar.ring(512, 2), ar.ring(512, 2), ar.ring(4096, 2)
    att = Heads16(E, n, ar, Wo, None, local=True)
    pg, pgT, vg, gs = ar.get(128), ar.get(256), ar.get(256), ar.get(96)
    xts = E["inputs_of"](n)
    held = {"g": None}

    def pro(b):
        qb, vb, kb = qr.take(), vr.take(), kmr.take()
        q = qb.ap.rearrange("p (k n) -> p k n", k=2)
        v = vb.ap.rearrange("p (k n) -> p k n", k=2)
        km = kb.ap.rearrange("p (k h n) -> p k h n", k=2, h=8)
        toks = []
        for it in range(2):
            t = 2 * b + it
            turned = rope_tile(E, t, Wqk, rbufs, [xts[b // 2], wt])
            yield
            yield
            yield
            bank, m = turned()
            bv = bank.ap.rearrange("p (j n) -> p j n", j=4)
            e1 = act(C.activation, q[:, :, it * P:(it + 1) * P], bv[:, 0:2, :], ACT.Copy, scale=0.25, w=[m, qb.w])
            kt_ = att.kraw.take()
            e2 = act(C.activation, kt_.ap, bank.ap[:, 256:512], ACT.Copy, w=[m, kt_.w])
            ps.give(bank, e1, e2)
            kk = kt_.ap.rearrange("p (k n) -> p k n", k=2)
            for f in range(2):
                e3 = att.mask(km[:, f, :, it * P:(it + 1) * P], kk[:, f, :], P, [e2, kb.w])
            att.kraw.give(kt_, e3)
            bank = ps.take()
            m = mm(bank.ap[:, 0:D], [(xnT[:, k2, t * P:(t + 1) * P], Wv[:, k2, :]) for k2 in range(2)], w=[bank.w])
            e4 = copy(v[:, it, :], bank.ap[:, 0:D], w=[m, vb.w])
            ps.give(bank, e4)
            toks += [e1, e3, e4]
            yield
        yield dict(q=q, v=v, km=km, t=toks, free=[(vr, vb)], free_qk=[(qr, qb), (kmr, kb)])

    def extra(b, s):
        hold = held["g"]
        bank = ps.take()
        for it in range(2):
            for kt in range(2):
                c = it * 64 + kt * 32
                m = mm(bank.ap[:, c:c + 32], [(s["q"][:, kt, it * P:(it + 1) * P], s["km"][:, kt, :, 0:256:64])],
                       w=[bank.w, s["t"]])
        m2 = mm(bank.ap[0:64, 128:128 + D], [(W(n, "gsel")[:, 64 * t:64 * t + 64], s["v"][:, t, :])
                                              for t in range(2)])
        sv = bank.ap[:, 0:128].rearrange("p (g j) -> p g j", j=4)
        pv = pg.rearrange("p (g j) -> p g j", j=4)
        bc = lambda a: a.unsqueeze(2).to_broadcast([P, 32, 4])
        q = dve(V.tensor_reduce, gs[:, 0:32], sv, AX.X, ALU.max, w=[m, m2, hold])
        q = dve(V.tensor_tensor, pv, sv, bc(gs[:, 0:32]), ALU.subtract, w=[q])
        q2 = dve(V.tensor_tensor, vg[0:64, :], bank.ap[0:64, 128:128 + D], W(n, "gmask", 64), ALU.mult,
                 w=[m2, hold])
        ps.give(bank, q, q2)
        x = act(C.activation, pg, pg, ACT.Exp, w=[q])
        return m2, more(b, s, x, q2)

    def more(b, s, x, q2):
        pv = pg.rearrange("p (g j) -> p g j", j=4)
        q = dve(V.tensor_reduce, gs[:, 32:64], pv, AX.X, ALU.add, w=[x])
        q = dve(V.reciprocal, gs[:, 64:96], gs[:, 32:64], w=[q])
        q = dve(V.tensor_tensor, pv, pv, gs[:, 64:96].unsqueeze(2).to_broadcast([P, 32, 4]), ALU.mult, w=[q])
        yield
        bank = ps.take()
        m = turn(E, bank, [(it * P, pg[:, it * 64:(it + 1) * 64], P, 64) for it in range(2)], [q])
        e = dve(V.tensor_copy, pgT[0:64, :], bank.ap[0:64, 0:256], w=[m])
        ps.give(bank, e)
        og = ps.take()
        for it in range(2):
            m = mm(og.ap[:, it * S:(it + 1) * S], [(pgT[0:64, it * P:(it + 1) * P], vg[0:64, :])],
                   w=[e, q2, og.w])
        held["g"] = m
        yield og, m

    att.run(pro, extra)


def few_keys(E, n):
    pe, act, dve, pool, T, V, C, G, ps, mm, X, xnT, W, Wk, copy = get(E)
    wt, A, dma = E["wtok"][n], E["A"], E["dma"]
    ar = E["Arena"]([(E["scr"], 0, E["NSCR"])])
    small = n == 4
    kt = 2 if small else 8
    inner = kt * P
    dh = inner // 16
    if small:
        Wq, Wkk, Wv, Wo = [Wk(n, x, 2) for x in ("Wq", "Wk", "Wv", "Wo")]
    else:
        Wq, Wkk, Wv, Wo = Wk(n, "wq", 2), Wk(n, "wk", 2), Wk(n, "wv", 2), Wk(n, "wo", 8)
    bo = W(n, "bo")[0:1, :]
    ctxT = E["ctxT"]
    kT = ar.get(kt * 616).rearrange("p (k n) -> p k n", k=kt)
    qr = ar.ring(kt * S, 2)
    if not small:
        for qb in qr.free:
            v_ = qb.ap.rearrange("p (k o n) -> p k o n", k=kt, o=2)
            z1 = pool(G.memset, v_[64:P, :, 0, :], 0.0)
            zero = [z1, pool(G.memset, v_[0:64, :, 1, :], 0.0)]
    vr = ar.ring(inner, 3 if small else 2)
    pr = ar.ring(16 * S2, 2)
    pt = ar.ring(512, 4)
    osb = ar.ring(2 * inner, 1)
    ot = ar.ring(2 * inner, 1)
    sm = ar.ring(48, 4)
    kts = []
    for f in range(kt):
        for h in range(2):
            bank = ps.take()
            m = mm(bank.ap[:, 0:308], [(Wkk[:, k, f * P:(f + 1) * P], ctxT[:, k, h * 308:(h + 1) * 308])
                                       for k in range(2)], w=[bank.w, wt, E["ctx_tok"]])
            o = kT[:, f, h * 308:(h + 1) * 308]
            if small:
                e = act(C.activation, o, bank.ap[:, 0:308], ACT.Identity, bias=W(n, "bk")[:, f:f + 1], w=[m])
            else:
                e = copy(o, bank.ap[:, 0:308], w=[m])
            ps.give(bank, e)
            kts.append(e)
    if small:
        mu = ar.get(154)
        pen = ar.get(616)
        kmr = ar.ring(2 * 8 * S2, 3)
        br = ar.ring(2 * S2, 3)
        mt = dma(mu.bitcast(U8), A["mbf"].rearrange("b s -> (b s)").partition_broadcast(P), E["bars"][-1])
        q = dve(V.tensor_scalar, pen, mu.bitcast(U8), -3e38, 2.0, ALU.mult, ALU.mult, w=[mt])
        pen_t = q
        am = W(n, "am").rearrange("p (i s) -> p i s", i=2)
    groups = [(0, 6), (6, 12), (12, 16)]
    xts = E["inputs_of"](n)
    if 11 in E["wtok"]:
        E["running"].append(ternary_weights(E, 11))
    st = {}

    def pro(b):
        vb = vr.take()
        toks = []
        if small:
            qb = qr.take()
            q = qb.ap.rearrange("p (k n) -> p k n", k=kt)
            bank = ps.take()
            f = 0
            for j in range(2):
                m = mm(bank.ap[:, j * S:(j + 1) * S],
                       [(Wq[:, k, (f + j) * P:(f + j + 1) * P], xnT[:, k, b * S:(b + 1) * S]) for k in range(2)],
                       w=[bank.w, xts[b // 2], wt])
            for j in range(2):
                e = dve(V.tensor_scalar, q[:, j, :], bank.ap[:, j * S:(j + 1) * S], W(n, "bq")[:, j:j + 1], 0.25,
                        ALU.add, ALU.mult, w=[m, qb.w])
            ps.give(bank, e)
            toks.append(e)
        for c in range(0, inner, 512):
            n_ = min(512, inner)
            bank = ps.take()
            pairs = [(ctxT[:, k, b * S2:(b + 1) * S2], Wv[:, k, c:c + n_]) for k in range(2)]
            if small:
                pairs.append((E["ones"][0:1, 0:S2], W(n, "bv")[0:1, :]))
            m = mm(bank.ap[0:S2, 0:n_], pairs, w=[bank.w, E["ctx_tok"]])
            e = copy(vb.ap[0:S2, c:c + n_], bank.ap[0:S2, 0:n_], w=[m, vb.w])
            ps.give(bank, e)
            toks.append(e)
        s = dict(v=vb.ap, t=toks, free=[(vr, vb)])
        if small:
            s.update(q=q, qb=qb)
            kb, bb = kmr.take(), br.take()
            km = kb.ap.rearrange("p (k h n) -> p k h n", k=2, h=8)
            for f in range(2):
                e = pool(G.tensor_tensor, km[:, f, :, :],
                         kT[:, f, b * S2:(b + 1) * S2].unsqueeze(1).to_broadcast([P, 8, S2]),
                         E["K"]("hm").unsqueeze(2).to_broadcast([P, 8, S2]), ALU.mult, w=[kts, kb.w])
            s["t"].append(e)
            e = pool(G.tensor_tensor, bb.ap.rearrange("p (i s) -> p i s", i=2), am,
                     pen[:, b * S2:(b + 1) * S2].unsqueeze(1).to_broadcast([P, 2, S2]), ALU.add,
                     w=[pen_t, wt, bb.w])
            s["bias"] = bb.ap.rearrange("p (i s) -> p i s", i=2)
            s["bt"] = e
            s["km"] = km
            s["free"] += [(kmr, kb), (br, bb)]
        st[b] = s

    def sq(u):
        b, it = divmod(u, 2)
        if it == 0:
            pro(b)
        qb = qr.take()
        q = qb.ap.rearrange("p (k o n) -> p k o n", k=kt, o=2)
        toks = []
        for f in (0, 4):
            bank = ps.take()
            for j in range(4):
                m = mm(bank.ap[:, j * P:(j + 1) * P],
                       [(Wq[:, k, (f + j) * P:(f + j + 1) * P], xnT[:, k, u * P:(u + 1) * P]) for k in range(2)],
                       w=[bank.w, xts[b // 2], wt])
            bv = bank.ap.rearrange("p (k n) -> p k n", k=4)
            for o in (0, 64):
                toks.append(act(C.activation, q[o:o + 64, f:f + 4, o // 64, :], bv[o:o + 64], ACT.Copy, scale=0.125,
                                w=[m, qb.w, zero]))
            ps.give(bank, toks[-1])
        st[b]["q", it] = (qb, q, toks)

    def s0(u):
        b, it = divmod(u, 2)
        if small and u == 0:
            pro(0)
        s = st[b]
        pb, sb_ = pr.take(), sm.take()
        p = pb.ap.rearrange("p (h n) -> p h n", h=16)
        xs = []
        for lo, hi in groups:
            bank = ps.take()
            if small:
                cuts = [(max(lo, 8 * f), min(hi, 8 * f + 8), f) for f in range(2)]
                for a, z, f in cuts:
                    if a < z:
                        m = mm(bank.ap[:, (a - lo) * S2:(z - lo) * S2],
                               [(s["q"][:, f, it * P:(it + 1) * P], s["km"][:, f, a - 8 * f:z - 8 * f, :])],
                               w=[bank.w, s["t"]])
            else:
                qb, q_, qt = s["q", it]
                for h in range(lo, hi):
                    m = mm(bank.ap[:, (h - lo) * S2:(h - lo + 1) * S2],
                           [(q_[:, h // 2, h % 2, :], kT[:, h // 2, b * S2:(b + 1) * S2])],
                           w=[bank.w, qt, s["t"], kts])
            qk = m
            nh = hi - lo
            sv = bank.ap[:, 0:nh * S2].rearrange("p (h n) -> p h n", n=S2)
            pv = p[:, lo:hi, :]
            mx = sb_.ap[:, lo:hi]
            src = sv
            if small:
                q = dve(V.tensor_tensor, pv, sv, s["bias"][:, it, :].unsqueeze(1).to_broadcast([P, nh, S2]), ALU.add,
                        w=[m, s["bt"], pb.w])
                bt = q
                src = pv
                m = q
            q = dve(V.tensor_reduce, mx, src, AX.X, ALU.max, w=[m, sb_.w])
            q = dve(V.tensor_tensor, pv, src, mx.unsqueeze(2).to_broadcast([P, nh, S2]), ALU.subtract,
                    w=[q, pb.w])
            ps.give(bank, q)
            x = act(C.activation, pv, pv, ACT.Exp, w=[q])
            xs.append(x)
        s[it] = (pb, p, xs, sb_)
        if small and it == 0 and b + 1 < NB:
            pro(b + 1)
        if not small:
            qr.give(qb, qk)
        elif it == 1:
            qr.give(s["qb"], qk)

    def s1(u):
        b, it = divmod(u, 2)
        s = st[b]
        pb, p, xs, sb_ = s[it]
        for (lo, hi), x in zip(groups, xs):
            q = dve(V.tensor_reduce, sb_.ap[:, 16 + lo:16 + hi], p[:, lo:hi, :], AX.X, ALU.add, w=[x])
        q = dve(V.reciprocal, sb_.ap[:, 32:48], sb_.ap[:, 16:32], w=[q])
        for g in range(4):
            bank = ps.take()
            m = turn(E, bank, [(j * P, p[:, 4 * g + j, :], P, S2) for j in range(4)], [xs[min(2, (4 * g + 3) // 6)]])
            tb = pt.take()
            e = copy(tb.ap[0:S2, :], bank.ap[0:S2, :], w=[m, tb.w])
            ps.give(bank, e)
            s[("t", g)] = (tb, e)
        pr.give(pb, m, q)
        s["r", it] = q

    def s2(u):
        b, it = divmod(u, 2)
        s = st[b]
        sb_, q = s[it][3], s["r", it]
        if it == 0:
            s["osb"] = osb.take()
        ob = s["osb"]
        ov = ob.ap.rearrange("p (i n) -> p i n", i=2)
        per = 512 // dh if not small else 16
        obank = None
        for h in range(16):
            if h % per == 0:
                obank = ps.take()
            tb, e = s[("t", h // 4)]
            c = (h % per) * dh
            m = mm(obank.ap[:, c:c + dh], [(tb.ap[0:S2, (h % 4) * P:(h % 4 + 1) * P], s["v"][0:S2, h * dh:(h + 1) * dh])],
                   w=[e, obank.w])
            if h % 4 == 3:
                pt.give(tb, m)
            if (h + 1) % per == 0:
                lo = h + 1 - per
                z = dve(V.tensor_tensor, ov[:, it, lo * dh:(h + 1) * dh].rearrange("p (h d) -> p h d", d=dh),
                        obank.ap[:, 0:per * dh].rearrange("p (h d) -> p h d", d=dh),
                        sb_.ap[:, 32 + lo:32 + h + 1].unsqueeze(2).to_broadcast([P, per, dh]), ALU.mult,
                        w=[m, q, ob.w])
                ps.give(obank, z)
        sm.give(sb_, z)
        if it == 1:
            for ring, buf in s["free"]:
                ring.give(buf, m, z)
            return finish_heads(E, n, b, ov, ot, Wo, bo, [z], lambda tok: osb.give(ob, tok))

    if small:
        pipe(E, 2 * NB, (1, s1), (0, s0), (1, s2))
    else:
        pipe(E, 2 * NB, (2, s1), (1, s0), (0, sq), (2, s2))


def latent_heads(E, n):
    pe, act, dve, pool, T, V, C, G, ps, mm, X, xnT, W, Wk, copy = get(E)
    wt = E["wtok"][n]
    ar = E["Arena"]([(E["scr"], 0, E["NSCR"])])
    many = n == 1
    H = 16 if many else 4
    inner = 64 * H
    kt = inner // P
    NK = 333
    cg = ar.get(1232).rearrange("p (k n) -> p k n", k=2)
    nq = 1 if many else 2
    qr, kr, vr = ar.ring(2 * kt * S, nq), ar.ring(kt * NK, nq), ar.ring(3 * inner, 2 if many else 3)
    pr, pt = ar.ring(672, 3), ar.ring(768, 2)
    xts = E["inputs_of"](n)
    osb = ar.ring(2 * inner, 1)
    ot = ar.ring(2 * inner, 1)
    sums = ar.ring(64, 2)
    sm = ar.ring(8, 6)
    g, bb = ("mg", "mb") if many else ("xg", "xb")
    for k in range(2):
        cgt = dve(V.tensor_scalar, cg[:, k, :], E["cnT"][:, k, :], W(n, g)[:, k:k + 1], W(n, bb)[:, k:k + 1],
                  ALU.mult, ALU.add, w=[E["ctx_tok"], wt])
    if many:
        Wq = Wk(n, "Wq", 2)
        Wkv = Wk(n, "Wkv", 2)
        Wo, bo = Wk(n, "Wout", 8), None
        vW = lambda k, c, m: Wkv[:, k, inner + c:inner + c + m]
    else:
        Wqk, Wvv = Wk(n, "Wqk", 2), Wk(n, "Wv", 2)
        Wo, bo = Wk(n, "Wo", 2), W(n, "bo")[0:1, :]
        vW = lambda k, c, m: Wvv[:, k, c:c + m]
        gq = ar.get(2)
        gqt = dve(V.tensor_scalar, gq[:, 0:1], W(n, "gq"), 0.125, None, ALU.mult, w=[wt])
        mu, pen = ar.get(154), ar.get(616)
        mt = E["dma"](mu.bitcast(U8), E["A"]["mbk"].rearrange("b s -> (b s)").partition_broadcast(P),
                      E["bars"][-1])
        pen_t = dve(V.tensor_scalar, pen, mu.bitcast(U8), -1.0, 1e30, ALU.add, ALU.mult, w=[mt])
        sqr, nrr, rsr = ar.ring(512, 2), ar.ring(512, 2), ar.ring(24, 2)
    for qb in qr.free:
        v_ = qb.ap.rearrange("p (k o n) -> p k o n", k=kt, o=2)
        z1 = pool(G.memset, v_[64:P, :, 0, :], 0.0)
        z2 = pool(G.memset, v_[0:64, :, 1, :], 0.0)
    zero = [z1, z2]

    def values(b, v):
        for j in range(3):
            rows = P if j < 2 else S2
            for c in range(0, inner, 512):
                m_ = min(512, inner)
                bank = ps.take()
                if j < 2:
                    l = lambda k: xnT[:, k, (2 * b + j) * P:(2 * b + j + 1) * P]
                else:
                    l = lambda k: cg[:, k, b * S2:(b + 1) * S2]
                m = mm(bank.ap[0:rows, 0:m_], [(l(k), vW(k, c, m_)) for k in range(2)],
                       w=[bank.w, xts[b // 2], cgt, wt])
                e = copy(v.ap[0:rows, j * inner + c:j * inner + c + m_], bank.ap[0:rows, 0:m_], w=[m, v.w])
                ps.give(bank, e)
                yield e

    qk_end = [[] for _ in range(kt)]

    def pro(b):
        vb = vr.take()
        vt, ft = [], {}
        made = dict(v=vb.ap.rearrange("p (j n) -> p j n", j=3), vt=vt, ft=ft, vb=vb)
        for e in values(b, vb):
            vt.append(e)
            yield
        if many:
            qb, kb = qk1
        else:
            qb, kb = qr.take(), kr.take()
        q = qb.ap.rearrange("p (k o n) -> p k o n", k=kt, o=2)
        k_ = kb.ap.rearrange("p (k n) -> p k n", k=kt)
        made.update(q=q, k=k_, qkb=(qb, kb))
        toks = []
        if many:
            yield made
            for f in range(kt):
                wf = slice(f * P, (f + 1) * P)
                bank = ps.take()
                m = mm(bank.ap[:, 0:S], [(Wq[:, k, wf], xnT[:, k, b * S:(b + 1) * S]) for k in range(2)],
                       w=[bank.w, zero])
                e = [act(C.activation, q[o:o + 64, f, o // 64, :], bank.ap[o:o + 64, 0:S], ACT.Copy, scale=0.125,
                         w=[m, qk_end[f]]) for o in (0, 64)]
                ps.give(bank, e)
                bank = ps.take()
                m = mm(bank.ap[:, 0:S], [(Wkv[:, k, wf], xnT[:, k, b * S:(b + 1) * S]) for k in range(2)],
                       w=[bank.w])
                m = mm(bank.ap[:, S:NK], [(Wkv[:, k, wf], cg[:, k, b * S2:(b + 1) * S2]) for k in range(2)],
                       w=[cgt])
                e2 = dve(V.tensor_copy, k_[:, f, :], bank.ap[:, 0:NK], w=[m, qk_end[f]])
                ps.give(bank, e2)
                ft[f] = [e, e2]
                yield
        else:
            def normed(j):
                rows = P if j < 2 else S2
                bank = ps.take()
                lo = 0 if j < 2 else 256
                l = (lambda k: xnT[:, k, (2 * b + j) * P:(2 * b + j + 1) * P]) if j < 2 else \
                    (lambda k: cg[:, k, b * S2:(b + 1) * S2])
                m = mm(bank.ap[0:rows, lo:512], [(l(k), Wqk[:, k, lo:512]) for k in range(2)], w=[bank.w])
                s_, n_, r_ = sqr.take(), nrr.take(), rsr.take()
                nh = (512 - lo) // 64
                e = act(C.activation, s_.ap[0:rows, lo:512], bank.ap[0:rows, lo:512], ACT.Square, w=[m, s_.w])
                h8 = lambda a: a[0:rows, lo:512].rearrange("p (h d) -> p h d", d=64)
                r = r_.ap[0:rows, 0:nh]
                e1 = dve(V.tensor_reduce, r, h8(s_.ap), AX.X, ALU.add, w=[e, r_.w])
                sqr.give(s_, e1)
                e2 = act(C.activation, r, r, ACT.Sqrt, scale=1.0 / 64, w=[e1])
                e2 = dve(V.tensor_scalar, r, r, 1e-8, None, ALU.max, w=[e2])
                e2 = dve(V.reciprocal, r, r, w=[e2])
                e2 = dve(V.tensor_tensor, h8(n_.ap), h8(bank.ap), r.unsqueeze(2).to_broadcast([rows, nh, 64]),
                         ALU.mult, w=[e2, n_.w])
                rsr.give(r_, e2)
                ps.give(bank, e2)

                def turned():
                    bank = ps.take()
                    m = turn(E, bank, [(c * P, n_.ap[0:rows, c * P:(c + 1) * P], rows, P)
                                       for c in range(lo // P, 4)], [e2])
                    nrr.give(n_, m)
                    bv = bank.ap.rearrange("p (c n) -> p c n", c=4)
                    if j < 2:
                        for o in (0, 64):
                            e3 = act(C.activation, q[o:o + 64, :, o // 64, j * P:(j + 1) * P], bv[o:o + 64, 0:2, :],
                                     ACT.Copy, scale=gq[o:o + 64, 0:1], w=[m, qb.w, gqt, zero])
                        toks.append(e3)
                    kd = k_[:, :, j * P:(j + 1) * P] if j < 2 else k_[:, :, S:NK]
                    e4 = act(C.activation, kd, bv[:, 2:4, 0:rows], ACT.Copy, scale=W(n, "gk")[:, 0:1], w=[m, kb.w])
                    toks.append(e4)
                    ps.give(bank, e4)
                return turned

            t0 = normed(0)
            yield
            t1 = normed(1)
            yield
            t0()
            t2 = normed(2)
            yield
            t1()
            yield
            t2()
            for f in range(kt):
                ft[f] = toks
            yield made

    next_ = Behind(pro)
    st = next_.made
    qk1 = (qr.take(), kr.take()) if many else None

    def s0(u):
        b, h = divmod(u, H)
        if u == 0:
            next_.start(0)
            next_.end()
        if not many and h == 0:
            next_.end()
        if h == (4 if many else 0):
            next_.start(b + 1)
        for _ in range(1 if many else 3):
            next_.step()
        s = st[b]
        if h == 0:
            s["sum"] = sums.take()
        pb, sb_ = pr.take(), sm.take()
        su = s["sum"].ap.rearrange("p (r i h) -> p r i h", r=2, i=2)
        xs = []
        for it in range(2):
            bank = ps.take()
            ql = s["q"][:, h // 2, h % 2, it * P:(it + 1) * P]
            if many:
                m = mm(bank.ap[:, 0:NK], [(ql, s["k"][:, h // 2, :])], w=[bank.w, s["ft"][h // 2]])
            else:
                m = mm(bank.ap[:, 0:S], [(ql, s["k"][:, h // 2, 0:S])], w=[bank.w, s["ft"][h // 2]])
                m = mm(bank.ap[:, S:NK], [(ql, s["k"][:, h // 2, S:NK]),
                                          (E["ones"][0:1, :], pen[0:1, b * S2:(b + 1) * S2])], w=[pen_t])
            q = dve(V.tensor_reduce, sb_.ap[:, it:it + 1], bank.ap[:, 0:NK], AX.X, ALU.max, negate=True,
                    w=[m, sb_.w])
            x = act(C.activation, pb.ap[:, it * 336:it * 336 + NK], bank.ap[:, 0:NK], ACT.Exp,
                    bias=sb_.ap[:, it:it + 1], accum_out=su[:, 0, it, h:h + 1], w=[q, pb.w, s["sum"].w])
            ps.give(bank, x)
        sm.give(sb_, x)
        s[h] = (pb, x)
        qk_end[h // 2] = m
        if h == H - 1 and not many:
            qr.give(s["qkb"][0], m)
            kr.give(s["qkb"][1], m)

    def s1(u):
        b, h = divmod(u, H)
        pb, x = st[b][h]
        p = pb.ap.rearrange("p (i n) -> p i n", i=2)
        bank, bank2 = ps.take(), ps.take()
        m = turn(E, bank, [((jt * 2 + it) * P, p[:, it, jt * P:(jt + 1) * P], P, P) for jt in range(2)
                           for it in range(2)], [x])
        m2 = turn(E, bank2, [(it * P, p[:, it, S:NK], P, S2) for it in range(2)], [x])
        pr.give(pb, m2)
        tb = pt.take()
        e = dve(V.tensor_copy, tb.ap[:, 0:512], bank.ap, w=[m, tb.w])
        e2 = act(C.activation, tb.ap[0:S2, 512:768], bank2.ap[0:S2, 0:256], ACT.Copy, w=[m2, tb.w])
        ps.give(bank, e)
        ps.give(bank2, e2)
        st[b][h] = (tb, [e, e2], x)

    def s2(u):
        b, h = divmod(u, H)
        s = st[b]
        tb, e, x = s[h]
        hp = min(8, H)
        if h == 0:
            s["osb"] = osb.take()
        if h % hp == 0:
            s["o"] = [ps.take(), ps.take()]
        for it in range(2):
            c = (h % hp) * 64
            m = mm(s["o"][it].ap[:, c:c + 64],
                   [(tb.ap[:, (jt * 2 + it) * P:(jt * 2 + it + 1) * P], s["v"][:, jt, h * 64:(h + 1) * 64])
                    for jt in range(2)]
                   + [(tb.ap[0:S2, 512 + it * P:512 + (it + 1) * P], s["v"][0:S2, 2, h * 64:(h + 1) * 64])],
                   w=[e, s["vt"], s["o"][it].w])
        pt.give(tb, m)
        su = s["sum"].ap.rearrange("p (r i h) -> p r i h", r=2, i=2)
        ov = s["osb"].ap.rearrange("p (i n) -> p i n", i=2)
        if (h + 1) % hp == 0:
            lo = h + 1 - hp
            for it in range(2):
                q = dve(V.reciprocal, su[:, 1, it, lo:h + 1], su[:, 0, it, lo:h + 1], w=[x])
                q = dve(V.tensor_tensor, ov[:, it, lo * 64:(h + 1) * 64].rearrange("p (h d) -> p h d", d=64),
                        s["o"][it].ap[:, 0:hp * 64].rearrange("p (h d) -> p h d", d=64),
                        su[:, 1, it, lo:h + 1].unsqueeze(2).to_broadcast([P, hp, 64]), ALU.mult,
                        w=[q, m, s["osb"].w])
                ps.give(s["o"][it], q)
        if h == H - 1:
            sums.give(s["sum"], q)
            vr.give(s["vb"], m)
            return finish_heads(E, n, b, ov, ot, Wo, bo, [q], lambda tok: osb.give(s["osb"], tok))

    pipe(E, H * NB, (0, s0), (2, s1), (3, s2))


def softplus(E, o, x, t1, t2, n_w):
    pe, act, dve, pool, T, V, C, G, ps, mm, X, xnT, W, Wk, copy = get(E)
    q = act(C.activation, t1, x, ACT.Abs, w=n_w)
    q = act(C.activation, t1, t1, ACT.Exp, scale=-1.0, w=[q])
    ql = act(C.activation, t2, t1, ACT.Ln, bias=E["one_ap"], w=[q, E["z_tok"]])
    qo = dve(V.scalar_tensor_tensor, t2, x, 0.0, t2, ALU.max, ALU.add, w=[ql])
    qm = dve(V.tensor_scalar, o, t1, 1.0, -1.0, ALU.add, ALU.add, w=[q, qo])
    qm = pool(G.tensor_tensor, t1, t1, o, ALU.subtract, w=[qm])
    return dve(V.tensor_tensor, o, t2, t1, ALU.add, w=[qo, qm])


def gated(E, n):
    pe, act, dve, pool, T, V, C, G, ps, mm, X, xnT, W, Wk, copy = get(E)
    wt = E["wtok"][n]
    ar = E["Arena"]([(E["scr"], 0, E["NSCR"])])
    sets = Ring([ar.get(7 * 1024) for _ in range(3)])
    la, tz = ar.get(2), ar.get(8)
    q = dve(V.tensor_scalar, tz[:, 0:2], W(n, "lam"), -1.0, None, ALU.mult, w=[wt])
    q = softplus(E, tz[:, 6:8], tz[:, 0:2], tz[:, 2:4], tz[:, 4:6], [q])
    lat = dve(V.tensor_scalar, la, tz[:, 6:8], -0.125, None, ALU.mult, w=[q])
    Wm = {k: Wk(n, k, 2) for k in ("lin", "conv", "a", "x", "lin2", "w1", "w2", "w3")}
    col_ = lambda name, f: W(n, name)[:, f:f + 1]
    v2 = lambda a: a.rearrange("p (k n) -> p k n", k=2)

    def project(name, src, w, evac):
        toks = []
        for f in range(2):
            bank = ps.take()
            m = mm(bank.ap, [(Wm[name][:, k, f * P:(f + 1) * P], src[:, k, :]) for k in range(2)], w=[bank.w, w])
            e = evac(f, bank, m)
            ps.give(bank, e)
            toks.append(e)
        return toks

    def chunk(c):
        sb_ = sets.take()
        buf = [sb_.ap[:, 1024 * i:1024 * i + 1024] for i in range(6)]
        R = sb_.ap[:, 6144:7168].rearrange("p (t d) -> p t d", t=4)
        lin, gel, xc, rt, gi, _ = [v2(b) for b in buf]
        y = xc
        done = sb_.w
        while not E["st_ring"].free:
            yield
        stb = E["st_ring"].take()
        for e in E["normalise_steps"](R, X[:, 4 * c:4 * c + 4, :], 4, P, "ln", [done], stb,
                                      E["xtok"][4 * c:4 * c + 4]):
            yield
        E["st_ring"].give(stb, e)
        r_t = [e] * 4

        def normed(g):
            toks = []
            for _ in E["norm_steps"](c, toks, ["rms16"], g=W(n, g), w=[wt], source=(R, r_t)):
                yield
            return toks

        xt = yield from normed("g1")
        xs = xnT[:, :, c * 512:(c + 1) * 512]
        t_lin = project("lin", xs, xt, lambda f, b, m: dve(
            V.tensor_scalar, lin[:, f, :], b.ap, col_("blin", f), None, ALU.add, w=[m, done]))
        yield
        t_xc = project("conv", lin, t_lin, lambda f, b, m: dve(
            V.tensor_scalar, xc[:, f, :], b.ap, col_("bconv", f), None, ALU.add, w=[m, done]))
        yield
        t_r = project("a", xc, t_xc, lambda f, b, m: act(
            C.activation, rt[:, f, :], b.ap, ACT.Sigmoid, bias=col_("ba", f), w=[m, done]))
        t_i = project("x", xc, t_xc, lambda f, b, m: act(
            C.activation, gi[:, f, :], b.ap, ACT.Sigmoid, bias=col_("bx", f), w=[m, done]))
        yield
        for f in range(2):
            t_a = act(C.activation, rt[:, f, :], rt[:, f, :], ACT.Exp, scale=la[:, f:f + 1], w=[t_r, lat])
        q = pool(G.tensor_tensor, buf[4], buf[4], buf[2], ALU.mult, w=[t_i, t_xc])
        o = dve(V.tensor_tensor, buf[5], buf[3], buf[3], ALU.mult, w=[t_a, done])
        z = dve(V.memset, buf[3].rearrange("p (b s) -> p b s", s=S)[:, :, 0:1], 0.0, w=[o])
        o = dve(V.tensor_scalar, buf[5], buf[5], -1.0, 1.0, ALU.mult, ALU.add, w=[o])
        yield
        t_gel = act(C.activation, buf[1], buf[0], ACT.Gelu, w=[t_lin, done])
        o = act(C.activation, buf[5], buf[5], ACT.Sqrt, w=[o])
        yield
        o = dve(V.tensor_tensor, buf[4], buf[4], buf[5], ALU.mult, w=[o, q])
        o = dve(V.tensor_tensor_scan, buf[5], buf[3], buf[4], 0.0, ALU.mult, ALU.add, w=[o, z, done])
        o = dve(V.tensor_tensor, buf[2], buf[5], buf[1], ALU.mult, w=[o, t_gel])
        yield
        for j in range(4):
            i = 4 * c + j
            r_t[j] = E["to_x"](j, lambda k: y[:, k, j * P:(j + 1) * P], 2, Wm["lin2"], [o],
                               bias=W(n, "blin2")[0:1, :], onto=(R[:, j, :], [r_t[j], xt]))
            E["xtok"][i] = pool(G.tensor_tensor, X[:, i, :], X[:, i, :], R[:, j, :], ALU.add,
                                w=[r_t[j], E["xtok"][i]])
        t_x = E["xtok"][4 * c + 3]
        yield
        xt = yield from normed("g2")
        t_s = project("w1", xs, xt, lambda f, b, m: act(
            C.activation, gel[:, f, :], b.ap, ACT.Sigmoid, bias=col_("b1", f), w=[m, o]))
        t_g = act(C.activation, buf[1], buf[1], ACT.Gelu, w=[t_s])
        yield
        t_c = project("w2", xs, xt, lambda f, b, m: dve(
            V.scalar_tensor_tensor, lin[:, f, :], b.ap, col_("b2", f), gel[:, f, :], ALU.add, ALU.mult,
            w=[m, t_g, t_xc]))
        yield
        for j in range(4):
            m = E["to_x"](4 * c + j, lambda k: lin[:, k, j * P:(j + 1) * P], 2, Wm["w3"], t_c,
                          bias=W(n, "b3")[0:1, :])
        sets.give(sb_, m, t_c, o, xt, t_x)
        E["finished"](n, c)
        yield

    LAG = 2
    flows = []
    for c in range(4):
        while len(flows) > 2 or (flows and steps < LAG):
            E["poll"]()
            steps += 1
            for g in list(flows):
                if next(g, "end") == "end":
                    flows.remove(g)
        flows.append(chunk(c))
        steps = 0
    while flows:
        E["poll"]()
        for g in list(flows):
            if next(g, "end") == "end":
                flows.remove(g)


def mamba(E, n):
    pe, act, dve, pool, T, V, C, G, ps, mm, X, xnT, W, Wk, copy = get(E)
    wt = E["wtok"][n]
    mine = E["order"][n] % 2
    _, width = offsets(SPEC[n])
    ar = E["Arena"]([(E["scr"], 0, E["NSCR"]), (E["Wr"][mine], width, WREG)])
    other = E["Arena"]([(E["Wr"][1 - mine], 0, WREG)])
    u, cd = other.get(2048), other.get(2048).rearrange("p (f k m) -> p f k m", f=4, k=4)
    deltas, dus = [[other.get(2048), ar.get(2048)] for _ in range(2)]
    ra, rb = ar.ring(2048, 3), ar.ring(2048, 3)
    bs, cs = ar.ring(512, 2), ar.ring(512, 3)
    tt = ar.get(4096)
    parts = [ar.get(256).bitcast(BF16) for _ in range(2)]
    dd = ar.get(512).rearrange("p (f m) -> p f m", f=4)
    sel = ar.get(16).bitcast(BF16)
    sel_c = sel.unsqueeze(2).to_broadcast([P, 32, P])
    dsum = ar.get(4)
    t1, t2 = tt[:, 0:2048], tt[:, 2048:4096]
    up = tt[:, 0:2072].rearrange("p (f b s) -> p f b s", f=4, b=2)
    dtb, xbc, r1 = [tt[:, 2560 + 512 * i:3072 + 512 * i] for i in range(3)]
    v4 = lambda a: a.rearrange("p (f n) -> p f n", f=4)
    uv = v4(u)
    xts = E["inputs_of"](n, [0])
    t_x = xts[0]
    ident = E["ident"]
    conv = Wk(n, "conv", 4)
    for f in range(4):
        for k in range(4):
            t_cd = dve(V.tensor_scalar, cd[:, f, k, :], ident, conv[:, f, k:k + 1], None, ALU.mult,
                       w=[wt])
    t_d = dve(V.tensor_tensor, dsum, W(n, "D0"), W(n, "D1"), ALU.add)
    for f in range(4):
        t_d = dve(V.tensor_scalar, dd[:, f, :], ident, dsum[:, f:f + 1], None, ALU.mult, w=[t_d])
    t_sel = dve(V.tensor_copy, sel, E["K"]("sel"), w=[E["c_tok"]])
    As = []
    for d in range(2):
        a = W(n, f"A{d}")
        q = act(C.activation, a, a, ACT.Exp, w=[wt])
        t_A = dve(V.tensor_scalar, a, a, -1.0, None, ALU.mult, w=[q])
        As.append(a.rearrange("p (f n) -> p f n", f=4))
    Win, Wout = Wk(n, "Win", 2), Wk(n, "Wout", 4)
    last = {"exp": [[], []], "g": [[], []], "sel": [[], []], "u": [], "tt": []}

    def ready(k):
        c, d = divmod(k, 2)
        xs = lambda k: xnT[:, k, c * 512:(c + 1) * 512]
        if d == 0:
            t_up = pool(G.memset, up[:, :, :, 0:3], 0.0, w=[last["tt"]])
            ups = []
            for f in range(4):
                bank = ps.take()
                m = mm(bank.ap, [(Win[:, k, f * P:(f + 1) * P], xs(k)) for k in range(2)], w=[bank.w, xts[c], wt])
                e = act(C.activation, up[:, f, :, 3:259], bank.ap.rearrange("p (b s) -> p b s", b=2), ACT.Copy,
                        w=[m, last["tt"]])
                ps.give(bank, e)
                ups.append(e)
                if f % 2:
                    yield
            for f in range(4):
                bank = ps.take()
                m = mm(bank.ap, [(cd[:, f, k, :], up[:, f, :, k:k + S]) for k in range(4)],
                       w=[bank.w, ups[f], t_cd, t_up])
                e = act(C.activation, uv[:, f, :], bank.ap, ACT.Identity, bias=W(n, "bconv")[:, f:f + 1],
                        w=[m, last["u"]])
                ps.give(bank, e)
                if f % 2:
                    yield
            last["tt"] = [m]
            last["u_made"] = act(C.activation, u, u, ACT.Silu, w=[e])
            yield
        t_u = last["u_made"]
        wd, wb = Wk(n, f"Wxd{d}", 4), Wk(n, f"Wxb{d}", 4)
        bank = ps.take()
        m = mm(bank.ap[0:64, :], [(wd[:, k, :], uv[:, k, :]) for k in range(4)], w=[bank.w, t_u])
        e_dt = act(C.activation, dtb[0:64, :], bank.ap[0:64, :], ACT.Copy, w=[m, last["tt"]])
        ps.give(bank, e_dt)
        yield
        bank = ps.take()
        m = mm(bank.ap[0:96, :], [(wb[:, k, :], uv[:, k, :]) for k in range(4)], w=[bank.w])
        m_u = m
        pt = parts[d]
        q = act(C.activation, xbc[0:96, :], bank.ap[0:96, :], ACT.Copy, w=[m, last["tt"]])
        ps.give(bank, q)
        q = dve(V.tensor_copy, pt[0:96, :], xbc[0:96, :], w=[q, last["sel"][d]])
        for lo, hi in ((32, 64), (64, 96)):
            q = dve(V.tensor_tensor, r1[lo:hi, :], xbc[lo:hi, :], pt[lo:hi, :], ALU.subtract, w=[q, last["tt"]])
            q = dve(V.tensor_copy, pt[lo:hi, :], r1[lo:hi, :], w=[q])
        yield
        q = dve(V.tensor_tensor, r1[64:96, :], r1[64:96, :], pt[64:96, :], ALU.subtract, w=[q])
        t_p = dve(V.tensor_copy, pt[64:96, :], r1[64:96, :], w=[q])
        delta, du = deltas[d], dus[d]
        for f in range(4):
            bank = ps.take()
            m = mm(bank.ap, [(W(n, f"Wdt{d}", 64)[:, f * P:(f + 1) * P], dtb[0:64, :])], w=[bank.w, e_dt])
            e = act(C.activation, v4(delta)[:, f, :], bank.ap, ACT.Identity, bias=W(n, f"bdt{d}")[:, f:f + 1],
                    w=[m, last["g"][d]])
            ps.give(bank, e)
            if f % 2:
                yield
        q = act(C.activation, t1, delta, ACT.Abs, w=[e, last["tt"]])
        yield
        q = act(C.activation, t1, t1, ACT.Exp, scale=-1.0, w=[q])
        yield
        ql = act(C.activation, t2, t1, ACT.Ln, bias=E["one_ap"], w=[q, E["z_tok"], m, t_p])
        yield
        qo = dve(V.scalar_tensor_tensor, t2, delta, 0.0, t2, ALU.max, ALU.add, w=[ql])
        qm = dve(V.tensor_scalar, delta, t1, 1.0, -1.0, ALU.add, ALU.add, w=[q, qo])
        qm = pool(G.tensor_tensor, t1, t1, delta, ALU.subtract, w=[qm, ql])
        yield
        yield
        t_dl = dve(V.tensor_tensor, delta, t2, t1, ALU.add, w=[qo, qm])
        last["tt"] = [t_dl]
        yield
        t_du = pool(G.tensor_tensor, du, delta, u, ALU.mult, w=[t_dl, t_u, last["g"][d]])
        last["u"] = [t_du, m_u]
        yield dict(t_p=t_p, t_dl=t_dl, t_du=t_du)

    def gate(c):
        for f in range(4):
            bank = ps.take()
            m = mm(bank.ap, [(Win[:, k, 512 + f * P:512 + (f + 1) * P], xnT[:, k, c * 512:(c + 1) * 512])
                             for k in range(2)], w=[bank.w])
            e = act(C.activation, v4(t1)[:, f, :], bank.ap, ACT.Copy, w=[m, last["tt"]])
            ps.give(bank, e)
            if f % 2:
                yield
        yield act(C.activation, t1, t1, ACT.Silu, w=[e])

    made, hold, ys, gated_ = {}, {}, {}, {}

    def behind(k):
        if k + 1 < 2 * NB // 2:
            for r in ready(k + 1):
                if r:
                    made[k + 1] = r
                yield
        else:
            E["late_weights"]([pe.now(), act.now(), dve.now(), pool.now()])
        if k % 2:
            for r in gate(k // 2):
                if r:
                    gated_[k // 2] = r
                yield

    def head(k, s_):
        d = k % 2
        mk = made[k]
        delta, du = deltas[d], dus[d]
        bb, bc = ps.take(), ps.take()
        m = mm(bb.ap, [(sel_c[0:96, s_, :], parts[d][0:96, :])], w=[bb.w, mk["t_p"], t_sel])
        m2 = mm(bc.ap, [(sel_c[0:96, 16 + s_, :], parts[d][0:96, :])], w=[bc.w])
        da, db, b_, c_ = ra.take(), rb.take(), bs.take(), cs.take()
        e = act(C.activation, b_.ap, bb.ap, ACT.Copy, w=[m, b_.w])
        ps.give(bb, e)
        e2 = act(C.activation, c_.ap, bc.ap, ACT.Copy, w=[m2, c_.w])
        ps.give(bc, e2)
        for f in range(4):
            x = act(C.activation, v4(da.ap)[:, f, :], v4(delta)[:, f, :], ACT.Exp,
                    scale=As[d][:, f, s_:s_ + 1], w=[mk["t_dl"], da.w, t_A])
        g = pool(G.tensor_tensor, v4(db.ap), v4(du), b_.ap.unsqueeze(1).to_broadcast([P, 4, 512]),
                 ALU.mult, w=[e, mk["t_du"], db.w])
        bs.give(b_, g)
        reset = 0 if d == 0 else S - 1
        z = pool(G.memset, da.ap.rearrange("p (b s) -> p b s", s=S)[:, :, reset:reset + 1], 0.0, w=[x])
        hold[16 * k + s_] = (da, db, c_, e2, z, g)
        if s_ == 15:
            last["g"][d], last["sel"][d] = [x, g], [m2]

    def tail(k, s_):
        d = k % 2
        c = k // 2
        if k % 2 == 0 and s_ == 0:
            ys[c] = [ps.take() for _ in range(4)]
            for f in range(4):
                m = mm(ys[c][f].ap, [(dd[:, f, :], uv[:, f, :])], w=[ys[c][f].w, last["u_made"], t_d], last=False)
        da, db, bc, m2, z, g = hold.pop(16 * k + s_)
        r = slice(None, None, 1 if d == 0 else -1)
        q = dve(V.tensor_tensor_scan, db.ap[:, r], da.ap[:, r], db.ap[:, r], 0.0, ALU.mult, ALU.add,
                w=[z, g])
        q = dve(V.tensor_tensor, v4(da.ap), v4(db.ap), bc.ap.unsqueeze(1).to_broadcast([P, 4, 512]),
                ALU.mult, w=[q, m2])
        cs.give(bc, q)
        for f in range(4):
            m = mm(ys[c][f].ap, [(ident, v4(da.ap)[:, f, :])], w=[q], first=False,
                   last=(d == 1 and s_ == 15))
        ra.give(da, m)
        rb.give(db, q)
        if k % 2 and s_ == 15:
            y = v4(t2)
            for f in range(4):
                q = dve(V.scalar_tensor_tensor, y[:, f, :], ys[c][f].ap, 0.5, v4(t1)[:, f, :], ALU.mult,
                        ALU.mult, w=[m, gated_[c], last["tt"]])
                ps.give(ys[c][f], q)
            for j in range(4):
                mo = E["to_x"](4 * c + j, lambda k: y[:, k, j * P:(j + 1) * P], 4, Wout, [q])
            last["tt"] = [q, mo]
            E["finished"](n, c)

    for r in ready(0):
        if r:
            made[0] = r
    run = iter(())
    N = 16 * 8
    for i in range(N + 2):
        E["poll"]()
        if i % 16 == 0 and i < N:
            for _ in run:
                pass
        if i < N:
            head(*divmod(i, 16))
        if i > 1:
            tail(*divmod(i - 2, 16))
        if i % 32 == 4 and i + 32 < N:
            E["start_norm"](n, i // 32 + 1)
        if i % 16 == 1 and i < N:
            run = behind(i // 16)
        next(run, None)
    for _ in run:
        pass


SUB = {0: mamba, 1: latent_heads, 2: experts, 3: talking, 4: few_keys, 5: moe_heads, 6: local_heads,
       7: latent_heads, 8: signs, 9: gated, 10: few_keys, 11: ternary}


def kl(w):
    k = w.shape[0] // P
    return w.reshape(k, P, -1).transpose(1, 0, 2).reshape(P, -1)


def col(v):
    return v.reshape(-1, P).T


def row(v, at=0):
    v = v.reshape(-1)
    a = np.zeros((P, v.size), v.dtype)
    a[at] = v
    return a


def top(w):
    a = np.zeros((P, w.shape[1]), w.dtype)
    a[:w.shape[0]] = w
    return a


def constants(g, b):
    c = {}
    p = np.arange(P)
    c["ident"] = np.eye(P)
    c["sel"] = (p[:, None] % 32 == np.arange(32)[None, :])
    c["hm"] = (p[:, None] // 16 == np.arange(8)[None, :])
    inv = (np.float32(1.0) / np.float32(10000.0) ** (np.arange(8, dtype=np.float32) / np.float32(8))).astype(np.float32)
    ang = np.arange(256, dtype=np.float32)[:, None] * inv[None, :]
    cos, sin = np.cos(ang.astype(np.float64)), np.sin(ang.astype(np.float64))
    two = lambda a: a.reshape(2, P, 16).transpose(1, 0, 2).reshape(P, 32)
    c["cos"] = two(np.concatenate([cos, cos], 1))
    c["sin"] = two(np.concatenate([-sin, sin], 1))
    c["jgt"] = np.broadcast_to((np.arange(8)[None, :] < np.arange(8)[:, None]).reshape(1, 64), (P, 64))
    c["one"] = np.ones((P, P))
    c["lg1"], c["lb1"] = [np.zeros((P, 2)) if a is None else a for a in (g, b)]
    return np.concatenate([np.asarray(c[n], np.float32).reshape(P, w) for n, w in CONST], 1)


def window_constants():
    p = np.arange(P)
    i0, j0 = p[:, None], np.arange(128)[None, :]
    i1, j1 = p[:, None] + 128, np.arange(256)[None, :]
    part = lambda i, j: np.where((i >= j) & (i - j <= 64), (j - i).astype(np.float64), -1e33)
    dist = np.concatenate([part(i0, j0), part(i1, j1)], 1)
    r = np.arange(64)
    gsel = np.concatenate([(p[:, None] + 128 * t == 64 * (r[None, :] % 4)) for t in range(2)], 1)
    gmask = (p[:, None] // 4 == np.arange(256)[None, :] // 16)
    return [np.asarray(a, np.float32) for a in (dist, gsel, gmask)]


def blocks(n, a):
    if n == 0:
        bc = lambda w: np.concatenate([w[64:96]] * 3, 0).T
        return [kl(a["W_in"].T), top(a["fWdt"].T), top(a["bWdt"].T), kl(a["W_out"].T), kl(a["fWx"][:64].T),
                kl(a["bWx"][:64].T), kl(bc(a["fWx"])), kl(bc(a["bWx"])), kl(a["W_conv"].reshape(512, 4)),
                col(a["b_conv"]), col(a["fD"]), col(a["bD"]), col(a["fbdt"]), col(a["bbdt"]), kl(a["fA_log"]),
                kl(a["bA_log"])]
    if n == 1:
        return [kl(a["Wq"]), kl(a["Wkv"]), kl(a["Wout"]), col(a["ln_m_g"]), col(a["ln_m_b"]), col(a["ln_l_g"]),
                col(a["ln_l_b"])]
    if n == 2:
        b2 = top(a["rb2"])
        b2[8] = a["sb2"]
        return [kl(a["router_w"]), row(a["router_b"]), np.concatenate([col(a["rb1"].reshape(-1)), col(a["sb1"])], 1),
                b2]
    if n == 3:
        w = a["w_qkv"]
        return [kl(w[:, :512]), kl(w[:, 512:]), kl(a["w_out"].T), kl(np.repeat(a["w_pre"].T, 16, 0)),
                np.broadcast_to(a["w_post"].T.reshape(1, 256), (P, 256)), row(a["b_out"])]
    if n == 4:
        return [kl(a["Wq"].T), kl(a["Wk"].T), kl(a["Wv"].T), kl(a["Wo"].T), col(a["bq"]), col(a["bk"]), row(a["bv"]),
                row(a["bo"]), kl(a["fside"])]
    if n == 5:
        we = np.concatenate([np.concatenate([kl(a[m][e]) for m in ("Wq", "Wk", "Wv")], 1) for e in range(4)], 1)
        bqk = np.concatenate([np.concatenate([col(a["bq"][e]), col(a["bk"][e])], 1) for e in range(4)], 1)
        return [we, kl(a["Wo"]), kl(a["Wg1"]), kl(a["Wg2"]), col(a["bg1"]), row(a["bg2"]), bqk, row(a["bv"]),
                row(a["bo"])]
    if n == 6:
        c = window_constants()
        return [kl(np.concatenate([a["Wq"], a["Wk"]], 1)), kl(a["Wv"]), kl(a["Wo"])] + c
    if n == 7:
        return [kl(np.concatenate([a["W_q"], a["W_kv"][:, :256]], 1)), kl(a["W_kv"][:, 256:]), kl(a["W_out"]),
                col(a["ln_x_g"]), col(a["ln_x_b"]), col(a["ln_l_g"]), col(a["ln_l_b"]),
                col(np.concatenate([a["q_gamma"]] * 2)), col(np.concatenate([a["k_gamma"]] * 2)), row(a["b_out"])]
    if n == 9:
        ws = ["W_lin", "W_conv", "Wa", "Wx", "W_lin2", "W1", "W2", "W3"]
        bs = ["b_lin", "b_conv", "ba", "bx", "b1", "b2"]
        return [kl(a[w].T) for w in ws] + [col(a[b]) for b in bs] + [row(a["b_lin2"]), row(a["b3"]), col(a["g1"]),
                                                                     col(a["g2"]), col(a["Lam"])]
    if n == 10:
        return [kl(a[w].reshape(256, 1024)) for w in ("wq", "wk", "wv")] + [kl(a["wo"].reshape(1024, 256)),
                                                                          row(a["bo"])]
    if n == 11:
        return [kl(a["w_up"].T), kl(a["w_down"].T)]
    return None


NAMES = {0: "L0_attn_", 1: "L0_xattn_", 2: "L0_ffn_", 3: "L1_attn_", 4: "L1_xattn_", 5: "L1_ffn_", 6: "L2_attn_",
         7: "L2_xattn_", 8: "L2_ffn_", 9: "L3_attn_", 10: "L3_xattn_", 11: "L3_ffn_"}


def kernel(**inputs):
    import numpy as _np
    import concourse.bacc as _bacc
    from concourse import mybir as _mybir
    from concourse.bass_utils import run_bass_kernel_spmd as _run

    inp = {k: _np.asarray(v) for k, v in inputs.items()}
    g = [col(inp["L0_xattn_" + k]) if "L0_xattn_" + k in inp else None for k in ("ln_l_g", "ln_l_b")]
    arrays = {"const": constants(*g), "x": inp["x"], "ctx": inp["ctx_1024"]}
    for n in LAYERS:
        a = {k[len(NAMES[n]):]: v for k, v in inp.items() if k.startswith(NAMES[n])}
        a["fside"] = inp["fside_SxS2_0"]
        b = blocks(n, a)
        if b is not None:
            for (name, w), arr in zip(SPEC[n], b):
                assert arr.shape == (P, w), (n, name, arr.shape)
            arrays[f"w{n}"] = _np.concatenate(b, 1)
        if n == 2:
            arrays["we"] = _np.stack([_np.concatenate([kl(a["rw1"][e]), kl(a["rw2"][e])], 1) for e in range(8)]
                                     + [_np.concatenate([kl(a["sw1"]), kl(a["sw2"])], 1)])
        if n == 4:
            arrays["mbf"] = inp["mask_BxS2_bf0"]
        if n == 7:
            arrays["mbk"] = inp["mask_BxS2_bk0"]
        if n == 8:
            arrays["k0"] = kl(a["k0"])
            arrays["k1"] = kl(a["k1"])
            arrays["k2"] = kl(a["k2"])
            arrays["s"] = _np.broadcast_to(_np.stack([a["s0"], a["s1"], a["s2"]]).reshape(1, 3), (P, 3))
    nc = _bacc.Bacc("TRN2", target_bir_lowering=False, num_devices=1)
    maps, A = {}, {}
    for name, arr in arrays.items():
        arr = _np.ascontiguousarray(arr)
        maps[f"in_{name}"] = arr
        A[name] = nc.dram_tensor(f"in_{name}", arr.shape, _mybir.dt.from_np(arr.dtype), kind="ExternalInput").ap()
    out = nc.dram_tensor("out_0", (NB, S, D), F32, kind="ExternalOutput").ap()
    build(nc, A, out)
    r = _run(nc, [maps], core_ids=[0])
    return r.results[0]["out_0"]
```
